# Optimizing a Trainium2 kernel written in Bass

```python
import numpy as np
import jax
import jax.numpy as jnp

def _softmax(x, axis=-1):
    return jax.nn.softmax(x, axis=axis)

def _gelu(x):
    return jax.nn.gelu(x, approximate=True)

def _silu(x):
    return jax.nn.silu(x)

def _sigmoid(x):
    return jax.nn.sigmoid(x)

def _layernorm(x, axis=-1, eps=1e-05):
    m = jnp.mean(x, axis=axis, keepdims=True)
    v = jnp.var(x, axis=axis, keepdims=True)
    return (x - m) / jnp.sqrt(v + eps)

def _scatter_add(tgt, idx, src, axis=0):
    return tgt.at[idx].add(src)

def _segment_sum(src, seg, n):
    return jax.ops.segment_sum(src, seg, n)
kernel_name = 'mk_decoder_postln_d4_seqx_r8_b21d94'

def setup_inputs(seed: int=0):
    np.random.seed(seed)
    _w = jnp.asarray

    def _rec_inputs():
        import jax
        import jax.numpy as jnp
        _rk = jax.random.key(seed)
        x = -0.0003929 + 0.9999 * jax.random.normal(jax.random.fold_in(_rk, 1), (8, 128, 512), jnp.float32)
        _lenS = 128 - jax.random.randint(jax.random.fold_in(_rk, 7), (8,), 0, max(1, 128 // 4) + 1, jnp.int32)
        _lenS2 = 128 - jax.random.randint(jax.random.fold_in(_rk, 8), (8,), 0, max(1, 128 // 4) + 1, jnp.int32)
        _ctx_4096P = jax.random.normal(jax.random.fold_in(_rk, 11), (8, 16, 512), jnp.float32)
        _ctx_4096c = jax.random.dirichlet(jax.random.fold_in(_rk, 511), 0.3 * jnp.ones((16,), jnp.float32), (8, 128))
        _ctx_4096t = jnp.einsum('bsk,bkd->bsd', _ctx_4096c, _ctx_4096P)
        _ctx_4096t = _ctx_4096t * jax.lax.rsqrt(jnp.mean(jnp.square(_ctx_4096t)) + 1e-12) * 0.953939
        ctx_4096 = 2.81802e-05 + 1.00001 * (_ctx_4096t + 0.3 * jax.random.normal(jax.random.fold_in(_rk, 611), (8, 128, 512), jnp.float32))
        _validS = jnp.arange(128)[None, :] < _lenS[:, None]
        _validS2 = jnp.arange(128)[None, :] < _lenS2[:, None]
        _causal = jnp.tril(jnp.ones((128, 128), dtype=bool))
        mask_BxSxS2_ff0 = jnp.where(jnp.ones((8, 128, 128), dtype=bool), 0.0, -1000000000.0).astype(jnp.float32)
        return (x, ctx_4096, mask_BxSxS2_ff0)
    x, ctx_4096, mask_BxSxS2_ff0 = _rec_inputs()

    def _L0_attn_setup():
        import jax, jax.numpy as jnp
        import numpy as np
        HIDDEN = 512
        NUM_HEADS = 32
        HEAD_DIM = HIDDEN // NUM_HEADS

        def _fp8_roundtrip(x):
            return x.astype(jnp.float8_e4m3fn).astype(jnp.float32)
        key = jax.random.key(seed)
        ks = jax.random.split(key, 10)
        B, S = (2, 512)
        hidden_states = jax.random.normal(ks[0], (B, S, HIDDEN), dtype=jnp.float32)
        scale = 0.02

        def lin(kw, kb):
            w = jax.random.normal(kw, (HIDDEN, HIDDEN), dtype=jnp.float32) * scale
            b = jax.random.normal(kb, (HIDDEN,), dtype=jnp.float32) * scale
            return (w, b)
        wq, bq = lin(ks[1], ks[2])
        wk, bk = lin(ks[3], ks[4])
        wv, bv = lin(ks[5], ks[6])
        wl, bl = lin(ks[7], ks[8])
        wq, bq = (_fp8_roundtrip(wq), _fp8_roundtrip(bq))
        wk, bk = (_fp8_roundtrip(wk), _fp8_roundtrip(bk))
        wv, bv = (_fp8_roundtrip(wv), _fp8_roundtrip(bv))
        return {'hidden_states': hidden_states, 'wq': wq, 'bq': bq, 'wk': wk, 'bk': bk, 'wv': wv, 'bv': bv, 'wl': wl, 'bl': bl}
    _L0_attn_all = _L0_attn_setup()
    _L0_attn_in = {k: v for k, v in _L0_attn_all.items() if k in ('wq', 'bq', 'wk', 'bk', 'wv', 'bv', 'wl', 'bl')}
    del _L0_attn_all

    def _L0_xattn_setup():
        import jax, jax.numpy as jnp
        import numpy as np
        EMB_DIM = 512
        NHEADS = 32
        KVHEADS = 8
        HEAD_DIM = 128
        ROPE_BASE = 10000.0

        def _rope(x):
            B, H, S, D = x.shape
            inv_freq = 1.0 / ROPE_BASE ** (jnp.arange(0, D, 2, dtype=jnp.float32) / D)
            ang = jnp.arange(S, dtype=jnp.float32)[:, None] * inv_freq[None, :]
            cos = jnp.concatenate([jnp.cos(ang), jnp.cos(ang)], axis=-1)
            sin = jnp.concatenate([jnp.sin(ang), jnp.sin(ang)], axis=-1)
            x1, x2 = (x[..., :D // 2], x[..., D // 2:])
            rot = jnp.concatenate([-x2, x1], axis=-1)
            return x * cos + rot * sin
        key = jax.random.key(seed)
        ks = jax.random.split(key, 7)
        B, S = (2, 256)
        std_qk = EMB_DIM ** (-0.5)
        std_vd = (1.0 / (EMB_DIM * NHEADS * HEAD_DIM) ** 0.5) ** 0.5
        return {'q': jax.random.normal(ks[0], (B, S, EMB_DIM), jnp.float32), 'k': jax.random.normal(ks[1], (B, S, EMB_DIM), jnp.float32), 'v': jax.random.normal(ks[2], (B, S, EMB_DIM), jnp.float32), 'Wq': jax.random.normal(ks[3], (NHEADS * HEAD_DIM, EMB_DIM), jnp.float32) * std_qk, 'Wk': jax.random.normal(ks[4], (KVHEADS * HEAD_DIM, EMB_DIM), jnp.float32) * std_qk, 'Wv': jax.random.normal(ks[5], (KVHEADS * HEAD_DIM, EMB_DIM), jnp.float32) * std_vd, 'Wd': jax.random.normal(ks[6], (EMB_DIM, NHEADS * HEAD_DIM), jnp.float32) * std_vd}
    _L0_xattn_all = _L0_xattn_setup()
    _L0_xattn_in = {k: v for k, v in _L0_xattn_all.items() if k in ('Wq', 'Wk', 'Wv', 'Wd')}
    del _L0_xattn_all

    def _L0_ffn_setup():
        import jax, jax.numpy as jnp
        import numpy as np
        HID, BOT, RDIM, NSLOT, K, VB = (512, 64, 48, 128, 8, 32)
        TAU_LOW, TAU_HIGH, EARLY_EXIT = (0.5, 2.0, 0.05)

        def _uncertainty(h, Wu1, bu1, Wu2, bu2):
            var = jnp.var(h, axis=-1)
            log_var = jnp.log1p(var)
            norm_var = log_var / (jnp.mean(log_var) + 1e-06)
            learned = (jax.nn.gelu(h @ Wu1.T + bu1) @ Wu2.T + bu2)[..., 0]
            return jnp.clip(norm_var * 0.5 + jax.nn.sigmoid(learned) * 2.5, 0.0, 5.0)
        key = jax.random.key(seed)
        ks = jax.random.split(key, 12)
        B, S = (2, 256)
        return {'hidden_states': jax.random.normal(ks[0], (B, S, HID), dtype=jnp.float32), 'Wq': jax.random.normal(ks[1], (BOT, HID), dtype=jnp.float32) / np.sqrt(HID), 'Wr': jax.random.normal(ks[2], (RDIM, BOT), dtype=jnp.float32) / np.sqrt(BOT), 'aux_keys': jax.random.normal(ks[3], (NSLOT, BOT), dtype=jnp.float32) * 0.01, 'aux_values': jax.random.normal(ks[4], (NSLOT, HID), dtype=jnp.float32) * 0.02, 'Wvd': jax.random.normal(ks[5], (VB, HID), dtype=jnp.float32) * 0.1 / np.sqrt(HID), 'Wvu': jax.random.normal(ks[6], (HID, VB), dtype=jnp.float32) * 0.1 / np.sqrt(VB), 'Wu1': jax.random.normal(ks[7], (HID // 4, HID), dtype=jnp.float32) / np.sqrt(HID), 'bu1': jnp.zeros((HID // 4,), dtype=jnp.float32), 'Wu2': jax.random.normal(ks[8], (1, HID // 4), dtype=jnp.float32) * 0.01, 'bu2': jnp.zeros((1,), dtype=jnp.float32), 'gate_w1': jnp.float32(0.5), 'gate_bias': jnp.float32(-1.0), 'log_rel': jnp.zeros((NSLOT,), dtype=jnp.float32)}
    _L0_ffn_all = _L0_ffn_setup()
    _L0_ffn_in = {k: v for k, v in _L0_ffn_all.items() if k in ('Wq', 'Wr', 'aux_keys', 'aux_values', 'Wvd', 'Wvu', 'Wu1', 'bu1', 'Wu2', 'bu2', 'gate_w1', 'gate_bias', 'log_rel')}
    del _L0_ffn_all

    def _L1_attn_setup():
        import jax, jax.numpy as jnp
        import numpy as np
        DIM = 512
        NUM_HEAD = 32
        NUM_KV_HEAD = 8
        ROPE_THETA = 10000.0
        B, T = (2, 256)

        def apply_rope(x, start_pos=0, theta=ROPE_THETA):
            d = x.shape[-1]
            half = d // 2
            inv_freq = 1.0 / theta ** (jnp.arange(0, half, dtype=jnp.float32) / half)
            pos = jnp.arange(x.shape[1], dtype=jnp.float32) + start_pos
            ang = pos[:, None] * inv_freq[None, :]
            cos = jnp.cos(ang)[None, :, None, :]
            sin = jnp.sin(ang)[None, :, None, :]
            x1, x2 = (x[..., :half], x[..., half:])
            return jnp.concatenate([x1 * cos - x2 * sin, x1 * sin + x2 * cos], axis=-1)
        key = jax.random.key(seed)
        ks = jax.random.split(key, 5)
        scale = 0.02
        X = jax.random.normal(ks[0], (B, T, DIM), dtype=jnp.float32)
        Wq = jax.random.normal(ks[1], (DIM, DIM), dtype=jnp.float32) * scale
        Wk = jax.random.normal(ks[2], (DIM, DIM // NUM_HEAD * NUM_KV_HEAD), dtype=jnp.float32) * scale
        Wv = jax.random.normal(ks[3], (DIM, DIM // NUM_HEAD * NUM_KV_HEAD), dtype=jnp.float32) * scale
        Wo = jax.random.normal(ks[4], (DIM, DIM), dtype=jnp.float32) * scale
        return {'X': X, 'Wq': Wq, 'Wk': Wk, 'Wv': Wv, 'Wo': Wo}
    _L1_attn_all = _L1_attn_setup()
    _L1_attn_in = {k: v for k, v in _L1_attn_all.items() if k in ('Wq', 'Wk', 'Wv', 'Wo')}
    del _L1_attn_all

    def _L1_xattn_setup():
        import jax, jax.numpy as jnp
        import numpy as np
        BS, SEQ, D_MODEL = (4, 128, 512)
        N_Q_HEADS, N_KV_HEADS, D_K, D_V = (32, 8, 128, 128)
        ROPE_BASE = 10000.0

        def _rotate_half(x):
            x1, x2 = jnp.split(x, 2, axis=-1)
            return jnp.concatenate([-x2, x1], axis=-1)

        def _apply_rope(x, pos0):
            d = x.shape[-1]
            seq = x.shape[2]
            inv_freq = 1.0 / ROPE_BASE ** (jnp.arange(0, d, 2, dtype=jnp.float32) / d)
            pos = (pos0 + jnp.arange(seq)).astype(jnp.float32)
            ang = pos[:, None] * inv_freq[None, :]
            cos = jnp.concatenate([jnp.cos(ang), jnp.cos(ang)], axis=-1)
            sin = jnp.concatenate([jnp.sin(ang), jnp.sin(ang)], axis=-1)
            return x * cos[None, None] + _rotate_half(x) * sin[None, None]
        key = jax.random.key(seed)
        ks = jax.random.split(key, 8)
        w_scale = 0.02
        return {'query': jax.random.normal(ks[0], (BS, SEQ, D_MODEL), dtype=jnp.float32), 'key': jax.random.normal(ks[1], (BS, SEQ, D_MODEL), dtype=jnp.float32), 'value': jax.random.normal(ks[2], (BS, SEQ, D_MODEL), dtype=jnp.float32), 'mask': jnp.zeros((BS, SEQ, SEQ), dtype=jnp.float32), 'wq': jax.random.normal(ks[3], (D_MODEL, N_Q_HEADS * D_K), dtype=jnp.float32) * w_scale, 'wk': jax.random.normal(ks[4], (D_MODEL, N_KV_HEADS * D_K), dtype=jnp.float32) * w_scale, 'wv': jax.random.normal(ks[5], (D_MODEL, N_KV_HEADS * D_V), dtype=jnp.float32) * w_scale, 'wo': jax.random.normal(ks[6], (N_Q_HEADS * D_V, D_MODEL), dtype=jnp.float32) * w_scale, 'curr_seq_pos': 0}
    _L1_xattn_all = _L1_xattn_setup()
    _L1_xattn_in = {k: v for k, v in _L1_xattn_all.items() if k in ('wq', 'wk', 'wv', 'wo')}
    del _L1_xattn_all

    def _L1_ffn_setup():
        import jax, jax.numpy as jnp
        import numpy as np
        MAX_THRESHOLD = 1.0 / 8.0
        SCALING = 32.0 / 16.0
        key = jax.random.key(seed)
        ks = jax.random.split(key, 8)
        B_, S, D, O, E, R = (4, 256, 512, 512, 8, 16)
        sd = 1.0 / np.sqrt(D)
        return {'x': jax.random.normal(ks[0], (B_, S, D), jnp.float32), 'W_base': jax.random.normal(ks[1], (O, D), jnp.float32) * sd, 'b_base': jax.random.normal(ks[2], (O,), jnp.float32) * 0.01, 'W_gate': jax.random.normal(ks[3], (E, D), jnp.float32) * sd, 'W_thr': jax.random.normal(ks[4], (1, D), jnp.float32) * sd, 'b_thr': jax.random.normal(ks[5], (1,), jnp.float32) * 0.01, 'A': jax.random.normal(ks[6], (E, R, D), jnp.float32) * sd, 'B': jax.random.normal(ks[7], (O,), jnp.float32)[None, :, None] * jnp.zeros((E, O, R), jnp.float32) + jax.random.normal(jax.random.fold_in(key, 7), (E, O, R), jnp.float32) * (1.0 / np.sqrt(R))}
    _L1_ffn_all = _L1_ffn_setup()
    _L1_ffn_in = {k: v for k, v in _L1_ffn_all.items() if k in ('W_base', 'b_base', 'W_gate', 'W_thr', 'b_thr', 'A', 'B')}
    del _L1_ffn_all

    def _L2_attn_setup():
        import jax, jax.numpy as jnp
        import numpy as np
        import math
        B, L, D, H = (32, 64, 512, 32)
        HD = D // H
        key = jax.random.key(seed)
        ks = jax.random.split(key, 9)
        s = 1.0 / math.sqrt(D)
        return {'x': jax.random.normal(ks[0], (B, L, D), jnp.float32), 'Wq': jax.random.normal(ks[1], (D, D), jnp.float32) * s, 'bq': jax.random.normal(ks[2], (D,), jnp.float32) * s, 'Wk': jax.random.normal(ks[3], (D, D), jnp.float32) * s, 'bk': jax.random.normal(ks[4], (D,), jnp.float32) * s, 'Wv': jax.random.normal(ks[5], (D, D), jnp.float32) * s, 'bv': jax.random.normal(ks[6], (D,), jnp.float32) * s, 'Wo': jax.random.normal(ks[7], (D, D), jnp.float32) * s, 'bo': jax.random.normal(ks[8], (D,), jnp.float32) * s}
    _L2_attn_all = _L2_attn_setup()
    _L2_attn_in = {k: v for k, v in _L2_attn_all.items() if k in ('Wq', 'bq', 'Wk', 'bk', 'Wv', 'bv', 'Wo', 'bo')}
    del _L2_attn_all

    def _L2_xattn_setup():
        import jax, jax.numpy as jnp
        import numpy as np
        B, C, N = (8, 64, 512)
        key = jax.random.key(seed)
        k1, k2, k3 = jax.random.split(key, 3)
        k = jax.random.normal(k1, (B, C, N), dtype=jnp.float32)
        q = jax.random.normal(k2, (B, C, N), dtype=jnp.float32)
        v = jax.random.normal(k3, (B, C, N), dtype=jnpp.float32) if False else jax.random.normal(k3, (B, C, N), dtype=jnp.float32)
        return {'k': k, 'q': q, 'v': v}
    _L2_xattn_all = _L2_xattn_setup()
    _L2_xattn_in = {k: v for k, v in _L2_xattn_all.items() if k in ()}
    del _L2_xattn_all

    def _L2_ffn_setup():
        import jax, jax.numpy as jnp
        import numpy as np
        NUM_EXPERTS = 8
        TOP_K = 2
        RANK = 16
        LORA_ALPHA = 32
        SCALING = LORA_ALPHA / RANK
        key = jax.random.key(seed)
        ks = jax.random.split(key, 6)
        B, S, D_IN, D_OUT = (4, 256, 512, 512)
        x = jax.random.normal(ks[0], (B, S, D_IN), dtype=jnp.float32)
        W_base = jax.random.normal(ks[1], (D_OUT, D_IN), dtype=jnp.float32) * 0.02
        b_base = jax.random.normal(ks[2], (D_OUT,), dtype=jnp.float32) * 0.02
        W_router = jax.random.normal(ks[3], (NUM_EXPERTS, D_IN), dtype=jnp.float32) * 0.02
        A = jax.random.normal(ks[4], (NUM_EXPERTS, RANK, D_IN), dtype=jnp.float32) * 0.02
        Bm = jax.random.normal(ks[5], (D_OUT, RANK), dtype=jnp.float32) * 0.02
        Bm = jnp.broadcast_to(Bm, (NUM_EXPERTS, D_OUT, RANK)) * jnp.arange(1, NUM_EXPERTS + 1, dtype=jnp.float32)[:, None, None] * 0.2
        return {'x': x, 'W_base': W_base, 'b_base': b_base, 'W_router': W_router, 'A': A, 'B': Bm}
    _L2_ffn_all = _L2_ffn_setup()
    _L2_ffn_in = {k: v for k, v in _L2_ffn_all.items() if k in ('W_base', 'b_base', 'W_router', 'A', 'B')}
    del _L2_ffn_all

    def _L3_attn_setup():
        import jax, jax.numpy as jnp
        import numpy as np
        H = 512
        D = H // 4
        key = jax.random.key(seed)
        k1, k2, k3, k4, k5 = jax.random.split(key, 5)
        x = jax.random.normal(k1, (4, 512, H), dtype=jnp.float32)
        s_in = 1.0 / np.sqrt(H)
        Wqkv = jax.random.normal(k2, (H, 3 * D), dtype=jnp.float32) * s_in
        bqkv = jax.random.normal(k3, (3 * D,), dtype=jnp.float32) * 0.01
        Wo = jax.random.normal(k4, (D, H), dtype=jnp.float32) * (1.0 / np.sqrt(D))
        bo = jax.random.normal(k5, (H,), dtype=jnp.float32) * 0.01
        return {'x': x, 'Wqkv': Wqkv, 'bqkv': bqkv, 'Wo': Wo, 'bo': bo}
    _L3_attn_all = _L3_attn_setup()
    _L3_attn_in = {k: v for k, v in _L3_attn_all.items() if k in ('Wqkv', 'bqkv', 'Wo', 'bo')}
    del _L3_attn_all

    def _L3_xattn_setup():
        import jax, jax.numpy as jnp
        import numpy as np
        B, Q, D = (8, 64, 512)
        CTX = 512
        H, KV, HD = (16, 4, 96)
        G = H // KV
        key = jax.random.key(seed)
        ks = jax.random.split(key, 6)
        s = 0.02
        return {'latents': jax.random.normal(ks[0], (B, Q, D), jnp.float32), 'context': jax.random.normal(ks[1], (B, CTX, D), jnp.float32), 'Wq': jax.random.normal(ks[2], (H * HD, D), jnp.float32) * s, 'Wk': jax.random.normal(ks[3], (KV * HD, D), jnp.float32) * s, 'Wv': jax.random.normal(ks[4], (KV * HD, D), jnp.float32) * s, 'Wo': jax.random.normal(ks[5], (D, H * HD), jnp.float32) * s}
    _L3_xattn_all = _L3_xattn_setup()
    _L3_xattn_in = {k: v for k, v in _L3_xattn_all.items() if k in ('Wq', 'Wk', 'Wv', 'Wo')}
    del _L3_xattn_all

    def _L3_ffn_setup():
        import jax, jax.numpy as jnp
        import numpy as np
        R = 16
        NUM_EXPERTS = 8
        TOP_K = 2
        LORA_ALPHA = 32
        SCALING = LORA_ALPHA / R
        key = jax.random.key(seed)
        ks = jax.random.split(key, 6)
        d_in, d_out = (512, 512)
        x = jax.random.normal(ks[0], (4, 256, d_in), dtype=jnp.float32)
        W_base = jax.random.normal(ks[1], (d_out, d_in), dtype=jnp.float32) * 0.02
        b_base = jax.random.normal(ks[2], (d_out,), dtype=jnp.float32) * 0.02
        W_router = jax.random.normal(ks[3], (NUM_EXPERTS, d_in), dtype=jnp.float32) * 0.01
        A = jax.random.normal(ks[4], (NUM_EXPERTS, R, d_in), dtype=jnp.float32) * 0.02
        B = jax.random.normal(ks[5], (NUM_EXPERTS, d_out, R), dtype=jnp.float32) * 0.02
        return {'x': x, 'W_base': W_base, 'b_base': b_base, 'W_router': W_router, 'A': A, 'B': B}
    _L3_ffn_all = _L3_ffn_setup()
    _L3_ffn_in = {k: v for k, v in _L3_ffn_all.items() if k in ('W_base', 'b_base', 'W_router', 'A', 'B')}
    del _L3_ffn_all
    return {'x': x, 'ctx_4096': ctx_4096, 'mask_BxSxS2_ff0': mask_BxSxS2_ff0, 'L0_attn_wq': _L0_attn_in['wq'], 'L0_attn_bq': _L0_attn_in['bq'], 'L0_attn_wk': _L0_attn_in['wk'], 'L0_attn_bk': _L0_attn_in['bk'], 'L0_attn_wv': _L0_attn_in['wv'], 'L0_attn_bv': _L0_attn_in['bv'], 'L0_attn_wl': _L0_attn_in['wl'], 'L0_attn_bl': _L0_attn_in['bl'], 'L0_xattn_Wq': _L0_xattn_in['Wq'], 'L0_xattn_Wk': _L0_xattn_in['Wk'], 'L0_xattn_Wv': _L0_xattn_in['Wv'], 'L0_xattn_Wd': _L0_xattn_in['Wd'], 'L0_ffn_Wq': _L0_ffn_in['Wq'], 'L0_ffn_Wr': _L0_ffn_in['Wr'], 'L0_ffn_aux_keys': _L0_ffn_in['aux_keys'], 'L0_ffn_aux_values': _L0_ffn_in['aux_values'], 'L0_ffn_Wvd': _L0_ffn_in['Wvd'], 'L0_ffn_Wvu': _L0_ffn_in['Wvu'], 'L0_ffn_Wu1': _L0_ffn_in['Wu1'], 'L0_ffn_bu1': _L0_ffn_in['bu1'], 'L0_ffn_Wu2': _L0_ffn_in['Wu2'], 'L0_ffn_bu2': _L0_ffn_in['bu2'], 'L0_ffn_gate_w1': _L0_ffn_in['gate_w1'], 'L0_ffn_gate_bias': _L0_ffn_in['gate_bias'], 'L0_ffn_log_rel': _L0_ffn_in['log_rel'], 'L1_attn_Wq': _L1_attn_in['Wq'], 'L1_attn_Wk': _L1_attn_in['Wk'], 'L1_attn_Wv': _L1_attn_in['Wv'], 'L1_attn_Wo': _L1_attn_in['Wo'], 'L1_xattn_wq': _L1_xattn_in['wq'], 'L1_xattn_wk': _L1_xattn_in['wk'], 'L1_xattn_wv': _L1_xattn_in['wv'], 'L1_xattn_wo': _L1_xattn_in['wo'], 'L1_ffn_W_base': _L1_ffn_in['W_base'], 'L1_ffn_b_base': _L1_ffn_in['b_base'], 'L1_ffn_W_gate': _L1_ffn_in['W_gate'], 'L1_ffn_W_thr': _L1_ffn_in['W_thr'], 'L1_ffn_b_thr': _L1_ffn_in['b_thr'], 'L1_ffn_A': _L1_ffn_in['A'], 'L1_ffn_B': _L1_ffn_in['B'], 'L2_attn_Wq': _L2_attn_in['Wq'], 'L2_attn_bq': _L2_attn_in['bq'], 'L2_attn_Wk': _L2_attn_in['Wk'], 'L2_attn_bk': _L2_attn_in['bk'], 'L2_attn_Wv': _L2_attn_in['Wv'], 'L2_attn_bv': _L2_attn_in['bv'], 'L2_attn_Wo': _L2_attn_in['Wo'], 'L2_attn_bo': _L2_attn_in['bo'], 'L2_ffn_W_base': _L2_ffn_in['W_base'], 'L2_ffn_b_base': _L2_ffn_in['b_base'], 'L2_ffn_W_router': _L2_ffn_in['W_router'], 'L2_ffn_A': _L2_ffn_in['A'], 'L2_ffn_B': _L2_ffn_in['B'], 'L3_attn_Wqkv': _L3_attn_in['Wqkv'], 'L3_attn_bqkv': _L3_attn_in['bqkv'], 'L3_attn_Wo': _L3_attn_in['Wo'], 'L3_attn_bo': _L3_attn_in['bo'], 'L3_xattn_Wq': _L3_xattn_in['Wq'], 'L3_xattn_Wk': _L3_xattn_in['Wk'], 'L3_xattn_Wv': _L3_xattn_in['Wv'], 'L3_xattn_Wo': _L3_xattn_in['Wo'], 'L3_ffn_W_base': _L3_ffn_in['W_base'], 'L3_ffn_b_base': _L3_ffn_in['b_base'], 'L3_ffn_W_router': _L3_ffn_in['W_router'], 'L3_ffn_A': _L3_ffn_in['A'], 'L3_ffn_B': _L3_ffn_in['B']}

def reference(x, ctx_4096, mask_BxSxS2_ff0, L0_attn_wq, L0_attn_bq, L0_attn_wk, L0_attn_bk, L0_attn_wv, L0_attn_bv, L0_attn_wl, L0_attn_bl, L0_xattn_Wq, L0_xattn_Wk, L0_xattn_Wv, L0_xattn_Wd, L0_ffn_Wq, L0_ffn_Wr, L0_ffn_aux_keys, L0_ffn_aux_values, L0_ffn_Wvd, L0_ffn_Wvu, L0_ffn_Wu1, L0_ffn_bu1, L0_ffn_Wu2, L0_ffn_bu2, L0_ffn_gate_w1, L0_ffn_gate_bias, L0_ffn_log_rel, L1_attn_Wq, L1_attn_Wk, L1_attn_Wv, L1_attn_Wo, L1_xattn_wq, L1_xattn_wk, L1_xattn_wv, L1_xattn_wo, L1_ffn_W_base, L1_ffn_b_base, L1_ffn_W_gate, L1_ffn_W_thr, L1_ffn_b_thr, L1_ffn_A, L1_ffn_B, L2_attn_Wq, L2_attn_bq, L2_attn_Wk, L2_attn_bk, L2_attn_Wv, L2_attn_bv, L2_attn_Wo, L2_attn_bo, L2_ffn_W_base, L2_ffn_b_base, L2_ffn_W_router, L2_ffn_A, L2_ffn_B, L3_attn_Wqkv, L3_attn_bqkv, L3_attn_Wo, L3_attn_bo, L3_xattn_Wq, L3_xattn_Wk, L3_xattn_Wv, L3_xattn_Wo, L3_ffn_W_base, L3_ffn_b_base, L3_ffn_W_router, L3_ffn_A, L3_ffn_B):
    import jax
    import jax.numpy as jnp

    def _L0_attn_ref(hidden_states, wq, bq, wk, bk, wv, bv, wl, bl):
        import jax, jax.numpy as jnp
        import numpy as np
        HIDDEN = 512
        NUM_HEADS = 32
        HEAD_DIM = HIDDEN // NUM_HEADS

        def _fp8_roundtrip(x):
            return x.astype(jnp.float8_e4m3fn).astype(jnp.float32)
        B, S, E = hidden_states.shape
        H, D = (NUM_HEADS, HEAD_DIM)
        q = (hidden_states @ wq.T + bq).reshape(B, S, H, D)
        k = (hidden_states @ wk.T + bk).reshape(B, S, H, D)
        v = (hidden_states @ wv.T + bv).reshape(B, S, H, D)
        latent = hidden_states @ wl.T + bl
        scores = jnp.einsum('bshd,bstd->bsht', q, k) / np.sqrt(D).astype(np.float32)
        probs = jax.nn.softmax(scores, axis=-1)
        context = jnp.einsum('bsht,bstd->bshd', probs, v).reshape(B, S, E)
        return context

    def _L0_xattn_ref(q, k, v, Wq, Wk, Wv, Wd):
        import jax, jax.numpy as jnp
        import numpy as np
        EMB_DIM = 512
        NHEADS = 32
        KVHEADS = 8
        HEAD_DIM = 128
        ROPE_BASE = 10000.0

        def _rope(x):
            B, H, S, D = x.shape
            inv_freq = 1.0 / ROPE_BASE ** (jnp.arange(0, D, 2, dtype=jnp.float32) / D)
            ang = jnp.arange(S, dtype=jnp.float32)[:, None] * inv_freq[None, :]
            cos = jnp.concatenate([jnp.cos(ang), jnp.cos(ang)], axis=-1)
            sin = jnp.concatenate([jnp.sin(ang), jnp.sin(ang)], axis=-1)
            x1, x2 = (x[..., :D // 2], x[..., D // 2:])
            rot = jnp.concatenate([-x2, x1], axis=-1)
            return x * cos + rot * sin
        B, Sq, _ = q.shape
        Skv = k.shape[1]
        queries = (q @ Wq.T).reshape(B, Sq, NHEADS, HEAD_DIM).transpose(0, 2, 1, 3)
        keys = (k @ Wk.T).reshape(B, Skv, KVHEADS, HEAD_DIM).transpose(0, 2, 1, 3)
        values = (v @ Wv.T).reshape(B, Skv, KVHEADS, HEAD_DIM).transpose(0, 2, 1, 3)
        queries = _rope(queries)
        keys = _rope(keys)
        exp = NHEADS // KVHEADS
        keys = jnp.repeat(keys, exp, axis=1)
        values = jnp.repeat(values, exp, axis=1)
        scale = HEAD_DIM ** (-0.5)
        scores = jnp.einsum('bhqd,bhkd->bhqk', queries, keys) * scale
        causal = jnp.tril(jnp.ones((Sq, Skv), dtype=bool))
        scores = jnp.where(causal[None, None], scores, jnp.finfo(scores.dtype).min)
        attn = jax.nn.softmax(scores, axis=-1)
        ctx = jnp.einsum('bhqk,bhkd->bhqd', attn, values)
        ctx = ctx.transpose(0, 2, 1, 3).reshape(B, Sq, NHEADS * HEAD_DIM)
        return ctx @ Wd.T

    def _L0_ffn_ref(hidden_states, Wq, Wr, aux_keys, aux_values, Wvd, Wvu, Wu1, bu1, Wu2, bu2, gate_w1, gate_bias, log_rel):
        import jax, jax.numpy as jnp
        import numpy as np
        HID, BOT, RDIM, NSLOT, K, VB = (512, 64, 48, 128, 8, 32)
        TAU_LOW, TAU_HIGH, EARLY_EXIT = (0.5, 2.0, 0.05)

        def _uncertainty(h, Wu1, bu1, Wu2, bu2):
            var = jnp.var(h, axis=-1)
            log_var = jnp.log1p(var)
            norm_var = log_var / (jnp.mean(log_var) + 1e-06)
            learned = (jax.nn.gelu(h @ Wu1.T + bu1) @ Wu2.T + bu2)[..., 0]
            return jnp.clip(norm_var * 0.5 + jax.nn.sigmoid(learned) * 2.5, 0.0, 5.0)
        query = hidden_states @ Wq.T
        rq = query @ Wr.T
        rk = aux_keys @ Wr.T
        router_scores = jnp.einsum('bsr,nr->bsn', rq, rk) / np.sqrt(RDIM) + log_rel
        top_scores, top_idx = jax.lax.top_k(router_scores, K)
        sel_keys = aux_keys[top_idx]
        attn = jnp.einsum('bsd,bskd->bsk', query, sel_keys) / np.sqrt(BOT) + log_rel[top_idx]
        w = jax.nn.softmax(attn, axis=-1)
        sel_vals = aux_values[top_idx]
        aux_out = jnp.einsum('bsk,bskh->bsh', w, sel_vals)
        aux_out = aux_out @ Wvd.T @ Wvu.T
        u = _uncertainty(hidden_states, Wu1, bu1, Wu2, bu2)
        u_norm = jnp.clip((u - TAU_LOW) / (TAU_HIGH - TAU_LOW), 0.0, 1.0)
        gate = jax.nn.sigmoid(gate_w1 * u_norm + gate_bias)
        gate = jnp.where(gate < EARLY_EXIT, 0.0, gate)
        return hidden_states + gate[..., None] * aux_out

    def _L1_attn_ref(X, Wq, Wk, Wv, Wo):
        import jax, jax.numpy as jnp
        import numpy as np
        DIM = 512
        NUM_HEAD = 32
        NUM_KV_HEAD = 8
        ROPE_THETA = 10000.0
        B, T = (2, 256)

        def apply_rope(x, start_pos=0, theta=ROPE_THETA):
            d = x.shape[-1]
            half = d // 2
            inv_freq = 1.0 / theta ** (jnp.arange(0, half, dtype=jnp.float32) / half)
            pos = jnp.arange(x.shape[1], dtype=jnp.float32) + start_pos
            ang = pos[:, None] * inv_freq[None, :]
            cos = jnp.cos(ang)[None, :, None, :]
            sin = jnp.sin(ang)[None, :, None, :]
            x1, x2 = (x[..., :half], x[..., half:])
            return jnp.concatenate([x1 * cos - x2 * sin, x1 * sin + x2 * cos], axis=-1)
        Bs, Ts, C = X.shape
        H, Hkv = (NUM_HEAD, NUM_KV_HEAD)
        dh = C // H
        G = H // Hkv
        Q = apply_rope((X @ Wq).reshape(Bs, Ts, H, dh))
        K = apply_rope((X @ Wk).reshape(Bs, Ts, Hkv, dh))
        V = (X @ Wv).reshape(Bs, Ts, Hkv, dh)
        Qh = Q.transpose(0, 2, 1, 3).reshape(Bs, Hkv, G, Ts, dh)
        Kh = K.transpose(0, 2, 1, 3)
        Vh = V.transpose(0, 2, 1, 3)
        scores = jnp.einsum('bkgtd,bksd->bkgts', Qh, Kh) / jnp.sqrt(jnp.float32(dh))
        causal = jnp.tril(jnp.ones((Ts, Ts), dtype=bool))
        scores = jnp.where(causal[None, None, None], scores, -jnp.inf)
        attn = jax.nn.softmax(scores, axis=-1)
        out = jnp.einsum('bkgts,bksd->bkgtd', attn, Vh)
        out = out.reshape(Bs, H, Ts, dh).transpose(0, 2, 1, 3).reshape(Bs, Ts, C)
        return out @ Wo

    def _L1_xattn_ref(query, key, value, mask, wq, wk, wv, wo, curr_seq_pos):
        import jax, jax.numpy as jnp
        import numpy as np
        BS, SEQ, D_MODEL = (4, 128, 512)
        N_Q_HEADS, N_KV_HEADS, D_K, D_V = (32, 8, 128, 128)
        ROPE_BASE = 10000.0

        def _rotate_half(x):
            x1, x2 = jnp.split(x, 2, axis=-1)
            return jnp.concatenate([-x2, x1], axis=-1)

        def _apply_rope(x, pos0):
            d = x.shape[-1]
            seq = x.shape[2]
            inv_freq = 1.0 / ROPE_BASE ** (jnp.arange(0, d, 2, dtype=jnp.float32) / d)
            pos = (pos0 + jnp.arange(seq)).astype(jnp.float32)
            ang = pos[:, None] * inv_freq[None, :]
            cos = jnp.concatenate([jnp.cos(ang), jnp.cos(ang)], axis=-1)
            sin = jnp.concatenate([jnp.sin(ang), jnp.sin(ang)], axis=-1)
            return x * cos[None, None] + _rotate_half(x) * sin[None, None]
        bs, sq, _ = query.shape
        n_groups = N_Q_HEADS // N_KV_HEADS
        q = (query @ wq).reshape(bs, sq, N_Q_HEADS, D_K).transpose((0, 2, 1, 3))
        sk = key.shape[1]
        k = (key @ wk).reshape(bs, sk, N_KV_HEADS, 1, D_K)
        k = jnp.repeat(k, n_groups, axis=3).reshape(bs, sk, N_Q_HEADS, D_K).transpose((0, 2, 1, 3))
        v = (value @ wv).reshape(bs, sk, N_KV_HEADS, 1, D_V)
        v = jnp.repeat(v, n_groups, axis=3).reshape(bs, sk, N_Q_HEADS, D_V).transpose((0, 2, 1, 3))
        scale = jnp.sqrt(jnp.float32(D_K))
        q = _apply_rope(q, curr_seq_pos)
        k = _apply_rope(k, curr_seq_pos)
        raw = jnp.einsum('bhqd,bhkd->bhqk', q, k) / scale
        masked = raw + mask[:bs, None, curr_seq_pos:curr_seq_pos + sq, :sk]
        attn = jax.nn.softmax(masked, axis=-1)
        out = jnp.einsum('bhqk,bhkd->bhqd', attn, v)
        out = out.transpose((0, 2, 1, 3)).reshape(bs, sq, N_Q_HEADS * D_V)
        return out @ wo

    def _L1_ffn_ref(x, W_base, b_base, W_gate, W_thr, b_thr, A, B):
        import jax, jax.numpy as jnp
        import numpy as np
        MAX_THRESHOLD = 1.0 / 8.0
        SCALING = 32.0 / 16.0
        base = jnp.einsum('bsd,od->bso', x, W_base) + b_base
        D = x.shape[-1]
        xf = x.reshape(-1, D)
        gate_logits = jax.nn.softmax(xf @ W_gate.T, axis=-1)
        thresholds = jax.nn.sigmoid(xf @ W_thr.T + b_thr) * MAX_THRESHOLD
        adapted = gate_logits - thresholds
        selected = (adapted >= 0).astype(x.dtype)
        weights = adapted * selected
        wsum = jnp.sum(weights, axis=-1, keepdims=True)
        wsum = jnp.where(wsum == 0, jnp.ones_like(wsum), wsum)
        weights = weights / wsum
        h = jnp.einsum('nd,erd->ner', xf, A)
        moe = jnp.einsum('ner,ne,eor->no', h, weights, B) * SCALING
        out = base + moe.reshape(base.shape)
        return out

    def _L2_attn_ref(x, Wq, bq, Wk, bk, Wv, bv, Wo, bo):
        import jax, jax.numpy as jnp
        import numpy as np
        import math
        B, L, D, H = (32, 64, 512, 32)
        HD = D // H
        b, l, d = x.shape
        h, hd = (H, HD)
        q = (x @ Wq.T + bq).reshape(b, l, h, hd).transpose(0, 2, 1, 3)
        k = (x @ Wk.T + bk).reshape(b, l, h, hd).transpose(0, 2, 1, 3)
        v = (x @ Wv.T + bv).reshape(b, l, h, hd).transpose(0, 2, 1, 3)
        scores = jnp.einsum('bhqd,bhkd->bhqk', q, k) / math.sqrt(hd)
        causal = jnp.tril(jnp.ones((l, l), bool))
        scores = jnp.where(causal, scores, -jnp.inf)
        att = jax.nn.softmax(scores, axis=-1)
        out = jnp.einsum('bhqk,bhkd->bhqd', att, v)
        out = out.transpose(0, 2, 1, 3).reshape(b, l, d)
        return out @ Wo.T + bo

    def _L2_xattn_ref(k, q, v):
        import jax, jax.numpy as jnp
        import numpy as np
        B, C, N = (8, 64, 512)
        input_dim = k.shape[1]
        scores = jnp.einsum('bcn,bcm->bnm', k, q) / jnp.sqrt(jnp.float32(input_dim))
        attn = jax.nn.softmax(scores, axis=-1)
        out = jnp.einsum('bnm,bcm->bcn', attn, v)
        return out

    def _L2_ffn_ref(x, W_base, b_base, W_router, A, B):
        import jax, jax.numpy as jnp
        import numpy as np
        NUM_EXPERTS = 8
        TOP_K = 2
        RANK = 16
        LORA_ALPHA = 32
        SCALING = LORA_ALPHA / RANK
        bs, seq, d_in = x.shape
        T = bs * seq
        xf = x.reshape(T, d_in)
        base = xf @ W_base.T + b_base
        logits = xf @ W_router.T
        rw, sel = jax.lax.top_k(logits, TOP_K)
        rw = jax.nn.softmax(rw, axis=-1)
        onehot = jax.nn.one_hot(sel, NUM_EXPERTS, dtype=rw.dtype)
        w = jnp.einsum('tk,tke->te', rw, onehot)
        h = jnp.einsum('td,erd->ter', xf, A)
        lora = jnp.einsum('ter,te,eor->to', h, w, B) * SCALING
        return (base + lora).reshape(bs, seq, -1)

    def _L3_attn_ref(x, Wqkv, bqkv, Wo, bo):
        import jax, jax.numpy as jnp
        import numpy as np
        H = 512
        D = H // 4
        B, S, C = x.shape
        d = C // 4
        qkv = jnp.einsum('bsc,cf->bsf', x, Wqkv) + bqkv
        qkv = qkv.reshape(B, S, 3, d)
        q, k, v = (qkv[:, :, 0], qkv[:, :, 1], qkv[:, :, 2])
        scale = 1.0 / jnp.sqrt(jnp.float32(d)).astype(x.dtype)
        attn = jnp.einsum('bqd,bkd->bqk', q, k) * scale
        attn = jax.nn.softmax(attn, axis=-1)
        out = jnp.einsum('bqk,bkd->bqd', attn, v)
        return jnp.einsum('bqd,dc->bqc', out, Wo) + bo

    def _L3_xattn_ref(latents, context, Wq, Wk, Wv, Wo):
        import jax, jax.numpy as jnp
        import numpy as np
        B, Q, D = (8, 64, 512)
        CTX = 512
        H, KV, HD = (16, 4, 96)
        G = H // KV
        b, q_len, _ = latents.shape
        hidden = jnp.concatenate([context, latents], axis=1)
        s_len = hidden.shape[1]
        q = (latents @ Wq.T).reshape(b, q_len, H, HD)
        k = (hidden @ Wk.T).reshape(b, s_len, KV, HD)
        v = (hidden @ Wv.T).reshape(b, s_len, KV, HD)
        q = q.transpose(0, 2, 1, 3).reshape(b, KV, G, q_len, HD)
        k = k.transpose(0, 2, 1, 3)
        v = v.transpose(0, 2, 1, 3)
        scale = 1.0 / jnp.sqrt(jnp.asarray(HD, q.dtype))
        scores = jnp.einsum('bkgqd,bksd->bkgqs', q, k) * scale
        attn = jax.nn.softmax(scores.astype(jnp.float32), axis=-1).astype(q.dtype)
        out = jnp.einsum('bkgqs,bksd->bkgqd', attn, v)
        out = out.reshape(b, H, q_len, HD).transpose(0, 2, 1, 3).reshape(b, q_len, H * HD)
        return out @ Wo.T

    def _L3_ffn_ref(x, W_base, b_base, W_router, A, B):
        import jax, jax.numpy as jnp
        import numpy as np
        R = 16
        NUM_EXPERTS = 8
        TOP_K = 2
        LORA_ALPHA = 32
        SCALING = LORA_ALPHA / R
        orig_shape = x.shape
        d_in = x.shape[-1]
        x_flat = x.reshape(-1, d_in)
        logits = x_flat @ W_router.T
        probs = jax.nn.softmax(logits, axis=-1)
        topk_probs, topk_idx = jax.lax.top_k(probs, TOP_K)
        topk_probs = topk_probs / jnp.sum(topk_probs, axis=-1, keepdims=True)
        onehot = jax.nn.one_hot(topk_idx, NUM_EXPERTS, dtype=x.dtype)
        combine = jnp.einsum('nk,nke->ne', topk_probs, onehot)
        h = jnp.einsum('nd,erd->ner', x_flat, A)
        hw = h * combine[:, :, None]
        expert_out = jnp.einsum('ner,eor->no', hw, B) * SCALING
        base_out = x_flat @ W_base.T + b_base
        out = base_out + expert_out
        return out.reshape(*orig_shape[:-1], W_base.shape[0])
    x = _layernorm(x + _L0_attn_ref(x, L0_attn_wq, L0_attn_bq, L0_attn_wk, L0_attn_bk, L0_attn_wv, L0_attn_bv, L0_attn_wl, L0_attn_bl), axis=-1)
    x = _layernorm(x + _L0_xattn_ref(x, ctx_4096, ctx_4096, L0_xattn_Wq, L0_xattn_Wk, L0_xattn_Wv, L0_xattn_Wd), axis=-1)
    x = _layernorm(x + _L0_ffn_ref(x, L0_ffn_Wq, L0_ffn_Wr, L0_ffn_aux_keys, L0_ffn_aux_values, L0_ffn_Wvd, L0_ffn_Wvu, L0_ffn_Wu1, L0_ffn_bu1, L0_ffn_Wu2, L0_ffn_bu2, L0_ffn_gate_w1, L0_ffn_gate_bias, L0_ffn_log_rel), axis=-1)
    x = _layernorm(x + _L1_attn_ref(x, L1_attn_Wq, L1_attn_Wk, L1_attn_Wv, L1_attn_Wo), axis=-1)
    x = _layernorm(x + _L1_xattn_ref(x, ctx_4096, ctx_4096, mask_BxSxS2_ff0, L1_xattn_wq, L1_xattn_wk, L1_xattn_wv, L1_xattn_wo, 0), axis=-1)
    x = _layernorm(x + _L1_ffn_ref(x, L1_ffn_W_base, L1_ffn_b_base, L1_ffn_W_gate, L1_ffn_W_thr, L1_ffn_b_thr, L1_ffn_A, L1_ffn_B), axis=-1)
    x = _layernorm(x + _L2_attn_ref(x, L2_attn_Wq, L2_attn_bq, L2_attn_Wk, L2_attn_bk, L2_attn_Wv, L2_attn_bv, L2_attn_Wo, L2_attn_bo), axis=-1)
    x = _layernorm(x + _L2_xattn_ref(ctx_4096, x, ctx_4096), axis=-1)
    x = _layernorm(x + _L2_ffn_ref(x, L2_ffn_W_base, L2_ffn_b_base, L2_ffn_W_router, L2_ffn_A, L2_ffn_B), axis=-1)
    x = _layernorm(x + _L3_attn_ref(x, L3_attn_Wqkv, L3_attn_bqkv, L3_attn_Wo, L3_attn_bo), axis=-1)
    x = _layernorm(x + _L3_xattn_ref(x, ctx_4096, L3_xattn_Wq, L3_xattn_Wk, L3_xattn_Wv, L3_xattn_Wo), axis=-1)
    x = _layernorm(x + _L3_ffn_ref(x, L3_ffn_W_base, L3_ffn_b_base, L3_ffn_W_router, L3_ffn_A, L3_ffn_B), axis=-1)
    return x

_drawn_inputs = setup_inputs


def setup_inputs(seed=0):
    import zlib

    import numpy as np

    out = dict(_drawn_inputs(seed))
    spreads = {'L0_ffn_bu1': (0.0, 2.0), 'L0_ffn_log_rel': (0.0, 2.0)}
    factors = {'L0_attn_wq': 3.475,
     'L0_attn_bq': 8.0,
     'L0_attn_wk': 3.165,
     'L0_attn_bk': 8.0,
     'L0_attn_bv': 8.0,
     'L0_ffn_Wq': 41.58,
     'L0_ffn_Wr': 47.977,
     'L0_ffn_aux_keys': 41.026,
     'L0_ffn_aux_values': 39.028,
     'L0_ffn_Wvd': 37.739,
     'L0_ffn_Wvu': 38.941,
     'L0_ffn_Wu1': 64.0,
     'L0_ffn_Wu2': 64.0,
     'L1_attn_Wq': 7.886,
     'L1_attn_Wk': 7.634,
     'L1_ffn_b_base': 4.828,
     'L2_attn_bq': 6.784,
     'L2_attn_bk': 64.0,
     'L2_ffn_b_base': 3.106,
     'L3_attn_bqkv': 5.621,
     'L3_attn_bo': 6.673,
     'L3_xattn_Wq': 3.404,
     'L3_xattn_Wk': 3.7,
     'L3_ffn_b_base': 3.591}
    for name, (base, spread) in spreads.items():
        noise = np.random.default_rng([zlib.crc32(name.encode()), seed]).standard_normal(out[name].shape)
        drawn = base * np.exp(spread * noise) if base else spread * noise
        out[name] = jnp.asarray(drawn.astype(out[name].dtype))
    for name, factor in factors.items():
        out[name] = (out[name] * factor).astype(out[name].dtype)
    return out
```

```python
from contextlib import ExitStack

import numpy as np
import concourse.bass as bass
from concourse import mybir

STAGES = (0, 1, 2, 3, 4, 5, 6, 7, 8, 9, 10, 11)

F32 = mybir.dt.float32
ALU = mybir.AluOpType
ACT = mybir.ActivationFunctionType
AX = mybir.AxisListType

P = 128
B = 8
D = 512
KC = D // P
T = B * P
HALF = T // 2
NEG = -1e30
EPS = 1e-5
HEAD_START = 128


class Mark:

    def __init__(self, counter, value, loop):
        self.counter, self.value, self.loop = counter, value, loop

    def at(self, i):
        return self.value + i * self.loop.per(self.counter)


class Loop:
    def __init__(self, n, per):
        self.n, self.counts, self.i = n, per, None

    def per(self, counter):
        return self.counts.get(counter.name, 0) * counter.step


class Counter:

    def __init__(self, core, name, step=1, starter=None):
        self.core, self.name, self.step = core, name, step
        self.sem = core.stack.enter_context(core.nc.semaphore(name))
        self.count = 0
        core.counters.append(self)
        if starter is not None:
            starter.sem_inc(self.sem, HEAD_START)
            self.count = HEAD_START

    def add(self, instruction):
        instruction.then_inc(self.sem, self.step)
        self.count += self.step
        return Mark(self, self.count, self.core.loop)

    def first(self):
        return Mark(self, self.count, self.core.loop)

    def now(self):
        return Mark(self, self.count, self.core.loop)


class Core:

    def __init__(self, nc, stack, known):
        self.nc, self.stack, self.loop, self.counters = nc, stack, None, []
        self.known, self.noted, self.loops = known, {}, 0
        self.carrier = stack.enter_context(nc.semaphore("wait_carrier"))
        self.pe = Counter(self, "pe_done", starter=nc.tensor)
        self.act = Counter(self, "act_done", starter=nc.scalar)
        self.dve = Counter(self, "dve_done", starter=nc.vector)
        self.pool = Counter(self, "pool_done", starter=nc.gpsimd)

    def wait(self, engine, *marks, apart=False):
        for mark in marks:
            if mark is None:
                continue
            value = mark.value
            if mark.loop is not None:
                inside = mark.loop is self.loop
                value = mark.at(self.loop.i if inside else mark.loop.n - 1)
            if isinstance(value, int) and value == 0:
                continue
            engine.wait_ge(mark.counter.sem, value)
        if apart and self.loop is not None:
            engine.sem_inc(self.carrier)

    def wait_at(self, engine, i, *marks):
        for mark in marks:
            engine.wait_ge(mark.counter.sem, mark.at(i))
        engine.sem_inc(self.carrier)

    def done(self):
        return [c.now() for c in (self.pe, self.act, self.dve, self.pool)]

    def note(self, name, mark):
        self.noted[self.loop.number, name] = (mark.counter.name, mark.value - self.loop.starts[mark.counter.name])

    def last(self, *names):
        marks = []
        for name in names:
            if (self.loop.number, name) in self.known:
                counter, offset = self.known[self.loop.number, name]
                counter = next(c for c in self.counters if c.name == counter)
                marks.append(Mark(counter, self.loop.starts[counter.name] + offset - self.loop.per(counter), self.loop))
        return marks

    def repeat(self, n, streams=None):
        return _Repeat(self, n, streams or {})


class _Repeat:
    def __init__(self, core, n, streams):
        self.core, self.streams = core, streams
        number = core.loops = core.loops + 1
        self.loop = Loop(n, dict(core.known.get(number, {})))
        self.loop.number = number

    def __enter__(self):
        core, E = self.core, mybir.EngineType
        self.fori = core.nc.Fori(0, self.loop.n, engines=(E.Pool, E.Activation, E.PE, E.DVE))
        self.loop.i = self.fori.__enter__()
        self.loop.starts = {c.name: c.count for c in core.counters}
        core.loop = self.loop
        for c, n in self.streams.items():
            self.loop.counts[c.name] = n
        return self.loop.i

    def __exit__(self, *error):
        core, loop = self.core, self.loop
        if error[0] is None:
            streamed = [c.name for c in self.streams]
            counts = {c.name: (c.count - loop.starts[c.name]) // c.step for c in core.counters if c.name not in streamed}
            core.noted[loop.number] = counts
            if core.known:
                assert counts == {k: v for k, v in loop.counts.items() if k not in streamed}
            for c in core.counters:
                c.count += (loop.n - 1) * loop.per(c)
        core.loop = None
        return self.fori.__exit__(*error)


def build(nc, dram, out, known):
    with ExitStack() as stack:
        core = Core(nc, stack, known)
        pe, act, dve, pool = core.pe, core.act, core.dve, core.pool
        PE, AC, DV, PO, SP = nc.tensor, nc.scalar, nc.vector, nc.gpsimd, nc.sync
        wait = core.wait

        def sbuf(name, shape, scope=stack):
            return scope.enter_context(nc.sbuf_tensor(name, shape, F32))

        x = sbuf("x", [P, B, D])
        xT = sbuf("xT", [P, KC, T])
        ctxT = sbuf("ctxT", [P, KC, T])
        xn = sbuf("xn", [P, D])
        xTb = sbuf("xTb", [P, KC, P])
        y = sbuf("y", [P, D])
        stats = sbuf("stats", [P, 12])
        arenas = [sbuf(f"weights{n}", [P, (9240, 5632)[n]]) for n in range(2)]
        psum = [stack.enter_context(nc.psum_tensor(f"bank{n}", [P, 512], F32)) for n in range(8)]
        const = sbuf("const", [P, dram["const"].shape[1]])
        ident = const[:, 0:P]
        causal = const[:, P:2 * P]
        block_diagonal = const[:, 2 * P:3 * P]
        cos128, sin128 = const[:, 3 * P:4 * P], const[:, 4 * P:5 * P]
        cos16, sin16 = const[:, 5 * P:6 * P], const[:, 6 * P:7 * P]
        turn16 = const[:, 7 * P:8 * P]
        parity = const[:, 8 * P:8 * P + 2]
        ones = const[:, 8 * P + 2:8 * P + 4]
        eps_row, minus_half_row = const[:, 8 * P + 16:8 * P + 24], const[:, 8 * P + 24:8 * P + 32]
        eps, minus_half = const[:, 8 * P + 5:8 * P + 6], const[:, 8 * P + 6:8 * P + 7]

        loaded_x = Counter(core, "loaded_x", 16)
        loaded_ctx = Counter(core, "loaded_ctx", 16)
        stored = Counter(core, "stored", 16)
        loaded_w = [Counter(core, f"loaded_weights{n}", 16) for n in range(2)]

        loaded_x.add(SP.dma_start(const[:, :], dram["const"]))
        loaded_x.add(SP.dma_start(x[:, :, :], dram["x"]))
        x_here = loaded_x.add(SP.dma_start(xT[:, :, :], dram["xT"]))
        ctx_here = None

        def load_context():
            nonlocal ctx_here
            if ctx_here is None:
                ctx_here = loaded_ctx.add(SP.dma_start(ctxT[:, :, :], dram["ctxT"]))

        class Weights:

            def __init__(self, stage, free):
                self.arena, self.counter, self.at = arenas[stage % 2], loaded_w[stage % 2], 0
                wait(SP, *free)

            def load(self, name, *, broadcast=False):
                a = dram[name]
                rows, cols = (P, a.shape[0]) if broadcast else (a.shape[0], int(np.prod(a.shape[1:])))
                view = self.arena[0:rows, self.at:self.at + cols]
                self.at += cols
                assert self.at <= self.arena.shape[1], name
                if broadcast:
                    a = a.rearrange("(o n) -> o n", o=1).broadcast_to((P, cols))
                elif len(a.shape) == 3:
                    view = view.rearrange("p (k n) -> p k n", k=a.shape[1])
                self.counter.add(SP.dma_start(view, a))
                return view

            def here(self):
                return self.counter.now()

        def wide(t, b, width=P):
            return t[:, :, bass.ds(b * width, width)]

        def finish_rows(b, y_done, banks=(6,), free=()):
            wait(DV, y_done)
            m = dve.add(DV.bn_stats(stats[:, 0:6], y[:, :]))
            wait(DV, m, apart=True)
            m = dve.add(DV.bn_aggr(stats[:, 6:8], stats[:, 0:6]))
            wait(PO, m)
            m = pool.add(PO.tensor_tensor(stats[:, 8:9], stats[:, 7:8], eps, ALU.add))
            wait(PO, m)
            m = pool.add(PO.tensor_tensor(stats[:, 9:10], stats[:, 8:9], minus_half, ALU.pow))
            wait(DV, m, *free)
            normed = dve.add(DV.tensor_scalar(xn[:, :], y[:, :], stats[:, 6:7], stats[:, 9:10],
                                              ALU.subtract, ALU.mult))
            wait(PO, normed, apart=True)
            kept = pool.add(PO.tensor_copy(x[:, bass.ds(b, 1), :].rearrange("p o d -> p (o d)"), xn[:, :]))
            wait(PE, normed)
            bank = psum[banks[0]]
            for k in range(KC):
                turned = PE.transpose(bank[:, k * P:(k + 1) * P], xn[:, k * P:(k + 1) * P], ident)
            turned = pe.add(turned)
            wait(AC, turned, apart=True)
            act.add(AC.activation(wide(xT, b), bank[:, :].rearrange("p (k n) -> p k n", k=KC), ACT.Copy))
            return kept

        def load_experts(stage, free):
            w = Weights(stage, free)
            n = {5: "L1", 9: None}.get(stage)
            layer = {5: "L1", 8: "L2", 11: "L3"}[stage]
            parts = {
                "base": w.load(f"{layer}_ffn_W_base"),
                "route": w.load(f"{layer}_ffn_route"),
                "up": w.load(f"{layer}_ffn_B"),
                "bias": w.load(f"{layer}_ffn_b_base", broadcast=True),
            }
            if stage == 5:
                parts["b_thr"] = w.load("L1_ffn_b_thr", broadcast=True)
            return parts, w

        E_, R_ = 8, 16

        def experts(stage, parts, w):
            with ExitStack() as scope:
                hw = sbuf(f"hw{stage}", [P, E_, R_], scope)
                hwT = sbuf(f"hwT{stage}", [P, P], scope)
                xb = sbuf(f"xb{stage}", [P, D], scope)
                r = sbuf(f"r{stage}", [P, 64], scope)
                logits, probs, sel, wt = r[:, 0:8], r[:, 8:16], r[:, 16:24], r[:, 24:32]
                top8, one = r[:, 32:40], r[:, 40:48]
                for eng in (PE, DV, PO):
                    wait(eng, w.here())
                with core.repeat(B) as b:
                    start = core.done()
                    wait(AC, *start, apart=True)
                    staged = act.add(AC.activation(xTb[:, :, :], wide(xT, b), ACT.Copy))
                    wait(PO, *start)
                    biased = pool.add(PO.tensor_tensor(xb[:, :], x[:, bass.ds(b, 1), :].rearrange("p o d -> p (o d)"), parts["bias"], ALU.add))
                    wait(PE, staged)
                    nr = parts["route"].shape[2]
                    for k in range(KC):
                        mm = PE.matmul(psum[0][:, 0:nr], xTb[:, k, :], parts["route"][:, k, :], start=k == 0, stop=k == KC - 1)
                    routed = pe.add(mm)
                    for k in range(KC):
                        PE.matmul(psum[1][:, :], xTb[:, k, :], parts["base"][:, k, :], start=k == 0, stop=False)
                    lg = psum[0][:, P:P + E_]
                    wait(DV, routed)
                    if stage == 5:
                        m = dve.add(DV.tensor_reduce(r[:, 48:49], lg, AX.X, ALU.max, negate=True))
                        m2 = dve.add(DV.tensor_scalar(r[:, 51:52], psum[0][:, P + E_:P + E_ + 1], parts["b_thr"][:, 0:1], -80.0, ALU.add, ALU.max))
                        wait(AC, m2)
                        act.add(AC.activation(probs, lg, ACT.Exp, bias=r[:, 48:49], accum_out=r[:, 49:50]))
                        m = act.add(AC.activation(r[:, 52:53], r[:, 51:52], ACT.Exp, scale=-1.0))
                        wait(DV, m)
                        dve.add(DV.reciprocal(r[:, 50:51], r[:, 49:50]))
                        m = dve.add(DV.tensor_scalar(r[:, 53:54], r[:, 52:53], 1.0, None, ALU.add))
                        wait(DV, m)
                        m = dve.add(DV.reciprocal(r[:, 54:55], r[:, 53:54]))
                        wait(DV, m)
                        m = dve.add(DV.tensor_scalar(r[:, 55:56], r[:, 54:55], 1.0 / 8.0, None, ALU.mult))
                        wait(DV, m)
                        m = dve.add(DV.tensor_scalar(logits, probs, r[:, 50:51], r[:, 55:56], ALU.mult, ALU.subtract))
                        wait(DV, m)
                        m = dve.add(DV.tensor_scalar(wt, logits, 0.0, None, ALU.max))
                        wait(DV, m)
                        m = dve.add(DV.tensor_reduce(r[:, 56:57], wt, AX.X, ALU.add))
                        wait(DV, m)
                        m = dve.add(DV.tensor_scalar(r[:, 57:58], r[:, 56:57], 0.0, None, ALU.is_equal))
                        wait(DV, m)
                        m = dve.add(DV.tensor_tensor(r[:, 58:59], r[:, 56:57], r[:, 57:58], ALU.add))
                        wait(DV, m)
                        m = dve.add(DV.reciprocal(r[:, 59:60], r[:, 58:59]))
                    else:
                        dve.add(DV.tensor_copy(logits, lg))
                        m = dve.add(DV.max(top8, lg))
                        wait(DV, m)
                        dve.add(DV.memset(one, 3.0e38))
                        m = dve.now()
                        wait(DV, m)
                        m = dve.add(DV.tensor_copy(one[:, 0:2], top8[:, 0:2]))
                        dve.add(DV.tensor_scalar(r[:, 48:49], top8[:, 0:1], -1.0, None, ALU.mult))
                        m = dve.now()
                        wait(DV, m, apart=True)
                        m = dve.add(DV.match_replace(sel, one, logits, NEG))
                        wait(DV, m)
                        m = dve.add(DV.tensor_tensor(sel, sel, logits, ALU.not_equal))
                        wait(AC, m)
                        m = act.add(AC.activation(probs, logits, ACT.Exp, bias=r[:, 48:49]))
                        wait(DV, m)
                        m = dve.add(DV.tensor_tensor(wt, probs, sel, ALU.mult))
                        wait(DV, m)
                        m = dve.add(DV.tensor_reduce(r[:, 58:59], wt, AX.X, ALU.add))
                        wait(DV, m)
                        m = dve.add(DV.reciprocal(r[:, 59:60], r[:, 58:59]))
                    wait(DV, m)
                    m = dve.add(DV.tensor_scalar(probs, wt, r[:, 59:60], 2.0, ALU.mult, ALU.mult))
                    wait(DV, m)
                    m = dve.add(DV.tensor_tensor(hw[:, :, :], psum[0][:, 0:P].rearrange("p (e r) -> p e r", e=E_),
                                                 probs.rearrange("p (e o) -> p e o", o=1).broadcast_to((P, E_, R_)), ALU.mult))
                    wait(PE, m)
                    m = pe.add(PE.transpose(psum[2][:, 0:P], hw[:, :, :].rearrange("p e r -> p (e r)"), ident))
                    wait(AC, m)
                    m = act.add(AC.activation(hwT[:, :], psum[2][:, 0:P], ACT.Copy))
                    wait(PE, m)
                    m = pe.add(PE.matmul(psum[1][:, :], hwT[:, :], parts["up"], start=False, stop=True))
                    wait(DV, m, biased)
                    m = dve.add(DV.tensor_tensor(y[:, :], psum[1][:, :], xb[:, :], ALU.add))
                    finish_rows(b, m)

        engines = (PE, AC, DV, PO)

        def spread(t, n, at=1):
            if at == 1:
                return t.rearrange("p (o m) -> p o m", o=1).broadcast_to((t.shape[0], n, t.shape[1]))
            return t.rearrange("p (m o) -> p m o", o=1).broadcast_to((t.shape[0], t.shape[1], n))

        def four(t):
            return t.rearrange("p (a n) -> p a n", a=4)

        def finish_all():
            with ExitStack() as scope:
                st = sbuf("norm_stats%d" % core.pe.count, [P, B, 6], scope)
                mv = sbuf("norm_mv%d" % core.pe.count, [P, B, 2], scope)
                rs = sbuf("norm_rs%d" % core.pe.count, [P, 2, B], scope)
                for b in range(B):
                    m = dve.add(DV.bn_stats(st[:, b, :], x[:, b, :]))
                wait(DV, m)
                for b in range(B):
                    m = dve.add(DV.bn_aggr(mv[:, b, :], st[:, b, :]))
                wait(PO, m)
                m = pool.add(PO.tensor_tensor(rs[:, 0, :], mv[:, :, 1], eps_row, ALU.add))
                wait(PO, m)
                m = pool.add(PO.tensor_tensor(rs[:, 1, :], rs[:, 0, :], minus_half_row, ALU.pow))
                wait(DV, m)
                copied = []
                for b in range(B):
                    normed = dve.add(DV.tensor_scalar(x[:, b, :], x[:, b, :], mv[:, b, 0:1], rs[:, 1, b:b + 1],
                                                      ALU.subtract, ALU.mult))
                    wait(PE, normed, copied[b - 2] if b >= 2 else None)
                    bank = psum[b % 2]
                    for k in range(KC):
                        mm = PE.transpose(bank[:, k * P:(k + 1) * P], x[:, b, k * P:(k + 1) * P], ident)
                    turned = pe.add(mm)
                    wait(AC, turned)
                    copied.append(act.add(AC.activation(xT[:, :, b * P:(b + 1) * P], four(bank[:, :]), ACT.Copy)))

        class Softmax:

            def __init__(self, scope, tag, width=P, normalise=True, depth=2, masked=True):
                self.width, self.normalise, self.depth = width, normalise, depth
                self.S = [sbuf(f"S{n}_{tag}", [P, 4, width], scope) if masked else None for n in range(depth)]
                self.E = [sbuf(f"E{n}_{tag}", [P, 4, width], scope) for n in range(depth)]
                self.small = [sbuf(f"sm{n}_{tag}", [P, 3, 4], scope) for n in range(depth)]
                self.restart()

            def restart(self):
                before = core.last if core.loop else lambda name: []
                self.used = [before(f"used{n}") for n in range(self.depth)]
                self.read = [before(f"read{n}") for n in range(self.depth)]

            def note(self):
                for n in range(self.depth):
                    core.note(f"used{n}", self.used[n][0])
                    core.note(f"read{n}", self.read[n][0])

            def run(self, u, scored, tiles, scale, mask):
                n = u % self.depth
                s, e, small, slot = self.S[n], self.E[n], self.small[n], n
                top, total, inverse = small[:, 0, :], small[:, 1, :], small[:, 2, :]
                wait(DV, scored, *self.read[slot])
                at = 0
                if mask is not None:
                    for t in tiles:
                        n = t.shape[1]
                        m = dve.add(DV.scalar_tensor_tensor(s[:, at:at + n, :], t, float(scale), mask[:, at:at + n, :], ALU.mult, ALU.add))
                        at += n
                    freed = m
                    wait(DV, m)
                    m = dve.add(DV.tensor_reduce(top, s[:, :, :], AX.X, ALU.max, negate=True))
                    source = [s[:, j, :] for j in range(4)]
                    scale = 1.0
                else:
                    source = []
                    for t in tiles:
                        n = t.shape[1]
                        m = dve.add(DV.tensor_reduce(top[:, at:at + n], t, AX.X, ALU.max, negate=True))
                        source += [t[:, j, :] for j in range(n)]
                        at += n
                    if scale != 1.0:
                        wait(DV, m)
                        m = dve.add(DV.tensor_scalar(inverse, top, float(scale), None, ALU.mult))
                        top = inverse
                wait(AC, m, *self.used[slot])
                for j in range(4):
                    if self.normalise:
                        m = act.add(AC.activation(e[:, j, :], source[j], ACT.Exp, bias=top[:, j:j + 1], scale=float(scale), accum_out=total[:, j:j + 1]))
                    else:
                        m = act.add(AC.activation(e[:, j, :], source[j], ACT.Exp, bias=top[:, j:j + 1], scale=float(scale)))
                self.read[slot] = [m]
                if mask is None:
                    freed = m
                if self.normalise:
                    wait(DV, m)
                    m = dve.add(DV.reciprocal(inverse, total))
                    wait(DV, m)
                    m = dve.add(DV.tensor_tensor(e[:, :, :], e[:, :, :], spread(inverse, self.width, at=2), ALU.mult))
                return m, freed

        G8 = 8

        def load_cross(stage, free):
            layer = {1: "L0", 4: "L1"}[stage]
            w = Weights(stage, free)
            load_context()
            qkv, o = Counter(core, f"stream_qkv{stage}", 16), Counter(core, f"stream_out{stage}", 16)
            views = {}
            for name, shape in (("wq", (KC, D)), ("wk", (KC, P)), ("wv", (KC, P)), ("wo", (4, D))):
                n = shape[0] * shape[1]
                views[name] = w.arena[:, w.at:w.at + n].rearrange("p (k n) -> p k n", k=shape[0])
                w.at += n
                (o if name == "wo" else qkv).add(SP.dma_start(views[name], dram[f"{layer}_x{name}"][0]))
            if stage == 4:
                views["mask"] = w.load("mask")
            return layer, views, w, qkv, o

        def cross(stage, layer, views, w, qkv, o):
            wq, wk, wv, wo = (views[n] for n in ("wq", "wk", "wv", "wo"))
            with ExitStack() as scope:
                QT = sbuf(f"QT{stage}", [P, 4, T], scope)
                KT = sbuf(f"KT{stage}", [P, T], scope)
                V = sbuf(f"V{stage}", [P, B, P], scope)
                turned = [sbuf(f"turned{n}_{stage}", [P, 4, P], scope) for n in range(2)]
                soft = Softmax(scope, f"x{stage}", depth=3)
                PT = [sbuf(f"PT{n}_{stage}", [P, 4, P], scope) for n in range(2)]
                OT = [sbuf(f"OT{n}_{stage}", [P, 4, P], scope) for n in range(2)]
                for eng in engines:
                    wait(eng, ctx_here, *([w.here()] if stage == 4 else []))
                with core.repeat(G8, streams={qkv: 3, o: 1}) as g:
                    wait(PE, qkv.first(), *core.last("bank0_free", "bank1_free"))
                    wait(DV, *core.last("scored"))
                    wait(AC, *core.last("mixed"))
                    soft.restart()
                    freed, added, jobs = [None, None], [None, None], []
                    for dst, source, weight in [(KT[:, :], ctxT, wk[:, :, :])] + [(QT[:, h, :], xT, wq[:, :, h * P:(h + 1) * P]) for h in range(4)]:
                        for half in range(2):
                            jobs.append((dst[:, half * HALF:(half + 1) * HALF], source[:, :, half * HALF:(half + 1) * HALF], weight))
                    for n, (dst, source, weight) in enumerate(jobs):
                        bank, t = psum[n % 2], turned[n % 2]
                        wait(PE, freed[n % 2])
                        for k in range(KC):
                            mm = PE.matmul(bank[:, :], weight[:, k, :], source[:, k, :], start=k == 0, stop=k == KC - 1)
                        m = pe.add(mm)
                        wait(DV, m, added[n % 2])
                        lo, hi = slice(0, P // 2), slice(P // 2, P)
                        dve.add(DV.tensor_tensor(t[hi, :, :], four(bank[lo, :]), spread(sin128[lo, :], 4), ALU.mult))
                        dve.add(DV.tensor_tensor(t[lo, :, :], four(bank[hi, :]), spread(sin128[hi, :], 4), ALU.mult))
                        freed[n % 2] = dve.add(DV.tensor_tensor(four(dst), four(bank[:, :]), spread(cos128, 4), ALU.mult))
                        wait(PO, freed[n % 2])
                        added[n % 2] = rotated = pool.add(PO.tensor_tensor(four(dst), four(dst), t[:, :, :], ALU.add))
                    for half in range(2):
                        bank = psum[half]
                        wait(PE, freed[half])
                        for b in range(4 * half, 4 * half + 4):
                            for k in range(KC):
                                mm = PE.matmul(bank[:, (b % 4) * P:(b % 4 + 1) * P], ctxT[:, k, b * P:(b + 1) * P], wv[:, k, :], start=k == 0, stop=k == KC - 1)
                        m = projected = pe.add(mm)
                        wait(AC, m)
                        valued = act.add(AC.activation(V[:, 4 * half:4 * half + 4, :], four(bank[:, :]), ACT.Copy))
                    wait(PE, rotated, valued)
                    for half in range(2):
                        core.note(f"bank{half}_free", valued)
                    scored_free, soft_done = [core.last(f"score_free{n}") for n in range(2)], {}
                    pt_free, ot_free = ([core.last(f"{t}_free{n}") for n in range(2)] for t in ("pt", "ot"))
                    bank_free = {n: core.last(f"bank{n}_free") for n in (4, 5, 6, 7)}
                    copied = {}
                    for step in range(B + 3):
                        if 2 <= step < B + 2:
                            b = step - 2
                            bank = psum[4 + b % 2]
                            wait(PE, soft_done[b], *bank_free[4 + b % 2])
                            for h in range(4):
                                mm = PE.transpose(bank[:, h * P:(h + 1) * P], soft.E[b % 3][:, h, :], ident)
                            m = pe.add(mm)
                            soft.used[b % 3] = [m]
                            wait(AC, m, *pt_free[b % 2])
                            pt_copied = act.add(AC.activation(PT[b % 2][:, :, :], four(bank[:, :]), ACT.Copy))
                            bank_free[4 + b % 2] = [pt_copied]
                        if step < B:
                            b = step
                            bank = psum[2 + b % 2]
                            wait(PE, *scored_free[b % 2])
                            for h in range(4):
                                mm = PE.matmul(bank[:, h * P:(h + 1) * P], QT[:, h, b * P:(b + 1) * P], KT[:, b * P:(b + 1) * P], start=True, stop=True)
                            m = pe.add(mm)
                            core.note("scored", m)
                            mask = spread(causal, 4) if stage == 1 else spread(views["mask"][:, b, :], 4)
                            soft_done[b], freed_ = soft.run(b, m, [four(bank[:, :])], P ** -0.5, mask)
                            scored_free[b % 2] = [freed_]
                        if step >= 3:
                            b = step - 3
                            bank = psum[7]
                            if b == 0:
                                wait(PE, o.first())
                            wait(PE, copied[b], *bank_free[7])
                            for h in range(4):
                                mm = PE.matmul(bank[:, :], OT[b % 2][:, h, :], wo[:, h, :], start=h == 0, stop=h == 3)
                            m = pe.add(mm)
                            ot_free[b % 2] = [m]
                            wait(DV, m)
                            bank_free[7] = [dve.add(DV.tensor_tensor(x[:, b, :], bank[:, :], x[:, b, :], ALU.add))]
                        if 2 <= step < B + 2:
                            b = step - 2
                            wait(PE, pt_copied, *bank_free[6])
                            m = pe.add(PE.matmul(psum[6][:, :], V[:, b, :], PT[b % 2][:, :, :], start=True, stop=True))
                            pt_free[b % 2] = [m]
                            core.note("mixed", m)
                            wait(DV, m, *ot_free[b % 2])
                            copied[b] = dve.add(DV.tensor_copy(OT[b % 2][:, :, :], four(psum[6][:, :])))
                            bank_free[6] = [copied[b]]
                    last = ot_free[(B - 1) % 2][0]
                    soft.note()
                    for n in range(2):
                        core.note(f"score_free{n}", scored_free[n][0])
                        core.note(f"pt_free{n}", pt_free[n][0])
                        core.note(f"ot_free{n}", ot_free[n][0])
                    for n in (4, 5, 6, 7):
                        core.note(f"bank{n}_free", bank_free[n][0])
                with SP.Fori(0, G8 - 1) as i:
                    core.wait_at(SP, i, projected)
                    for name in ("wq", "wk", "wv"):
                        SP.dma_start(views[name], dram[f"{layer}_x{name}"][bass.ds(i + 1, 1)].rearrange("o p k n -> (o p) k n")).then_inc(qkv.sem, 16)
                    core.wait_at(SP, i, last)
                    SP.dma_start(wo, dram[f"{layer}_xwo"][bass.ds(i + 1, 1)].rearrange("o p k n -> (o p) k n")).then_inc(o.sem, 16)
                for eng in engines:
                    wait(eng, *core.done())
            finish_all()

        HEADS, HD = 32, 16

        class Small:

            def __init__(self, scope, tag, masked):
                self.soft = Softmax(scope, tag, normalise=False, depth=3, masked=masked)
                self.PT = [sbuf(f"PT{n}_{tag}", [P, 4, P], scope) for n in range(2)]
                self.sums = sbuf(f"sums_{tag}", [P, 2, 16], scope)
                self.restart()

            def restart(self):
                before = core.last if core.loop else lambda name: []
                self.soft.restart()
                self.pt_free = [before(f"pt_free{n}") for n in range(2)]
                self.score_free = [before(f"score_free{n}") for n in range(3)]
                self.t_free = [before(f"t_free{n}") for n in range(2)]
                self.o_free = [before(f"o_free{n}") for n in range(2)]

            def note(self):
                self.soft.note()
                for name, marks in (("pt_free", self.pt_free), ("score_free", self.score_free), ("t_free", self.t_free), ("o_free", self.o_free)):
                    for n, mark in enumerate(marks):
                        core.note(f"{name}{n}", mark[0])

            def run(self, quads, mask, scale, before_scores, after_products):
                soft, n, ready = self.soft, len(quads), {}
                self.scored_marks = {}
                for step in range(n + 3):
                    if 2 <= step < n + 2:
                        u = step - 2
                        bank = psum[2 + u % 2]
                        wait(PE, ready[u], *self.t_free[u % 2])
                        for j in range(4):
                            mm = PE.transpose(bank[:, j * P:(j + 1) * P], soft.E[u % 3][:, j, :], ident)
                        m = pe.add(mm)
                        soft.used[u % 3] = [m]
                        wait(DV if u % 2 else AC, m, *self.pt_free[u % 2])
                        if u % 2:
                            m = dve.add(DV.tensor_copy(self.PT[u % 2][:, :, :], four(bank[:, :])))
                        else:
                            m = act.add(AC.activation(self.PT[u % 2][:, :, :], four(bank[:, :]), ACT.Copy))
                        self.t_free[u % 2] = [m]
                    if step < n:
                        u = step
                        bank = psum[(0, 1, 6)[u % 3]]
                        wait(PE, *self.score_free[u % 3], *(before_scores[u]() if u in before_scores else []))
                        for j, (lhsT, rhs, _, _) in enumerate(quads[u]):
                            mm = PE.matmul(bank[:, j * P:(j + 1) * P], lhsT, rhs, start=True, stop=True)
                        m = self.scored = self.scored_marks[u] = pe.add(mm)
                        ready[u], freed = soft.run(u, m, [four(bank[:, :])], scale, mask)
                        self.score_free[u % 3] = [freed]
                    if step >= 3:
                        u = step - 3
                        half = quads[u][0][3] // 16
                        wait(PE, *self.t_free[u % 2], *self.o_free[half])
                        for j, (_, _, values, column) in enumerate(quads[u]):
                            o = psum[4 + half][:, column % 16 * 17:column % 16 * 17 + 17]
                            mm = PE.matmul(o, self.PT[u % 2][:, j, :], values, start=True, stop=True)
                        m = pe.add(mm)
                        self.pt_free[u % 2] = [m]
                        if u in after_products:
                            after_products[u](m)

            def divide(self, m, half, O, *free):
                bank = psum[4 + half][:, 0:272].rearrange("p (h e) -> p h e", e=17)
                sums = self.sums[:, half, :]
                wait(DV, m, *free)
                r = dve.add(DV.reciprocal(sums, bank[:, :, 16]))
                wait(DV, r)
                r = dve.add(DV.tensor_tensor(O, bank[:, :, 0:HD], spread(sums, HD, at=2), ALU.mult))
                self.o_free[half] = [r]
                return r

        def load_rotary16(stage, free):
            w = Weights(stage, free)
            return {n: w.load(f"L1_attn_{n}") for n in ("Wq", "Wk", "Wv", "Wo")}, w

        def load_bias16(stage, free):
            w = Weights(stage, free)
            v = {n: w.load(f"L2_attn_{n}") for n in ("Wq", "Wk", "Wv", "Wo", "bq", "bk")}
            v.update({n: w.load(f"L2_attn_{n}", broadcast=True) for n in ("bv", "bo")})
            return v, w

        def small_attention(stage, v, w):
            rotary = stage == 3
            kt = 1 if rotary else 4
            kv = 8 * kt
            with ExitStack() as scope:
                QT = sbuf(f"QT{stage}", [P, 4, T], scope)
                KT = sbuf(f"KT{stage}", [P, kt, T], scope)
                QTb = [sbuf(f"QTb{c}_{stage}", [P, 4, P], scope) for c in range(2)]
                KTb = [[sbuf(f"KTb{c}{n}_{stage}", [P, kt, P], scope) for n in range(2)] for c in range(2)]
                V = [sbuf(f"V{c}_{stage}", [P, kv, 17], scope) for c in range(2)]
                xTb2 = [xTb, sbuf(f"xTb_{stage}", [P, KC, P], scope)]
                O = [sbuf(f"O{c}_{stage}", [P, HEADS, HD], scope) for c in range(2)]
                inner = ExitStack()
                if rotary:
                    raw = [sbuf(f"raw{n}_{stage}", [P, D], inner) for n in range(2)]
                    turned = [sbuf(f"turned{n}_{stage}", [P, D], inner) for n in range(2)]
                for eng in engines:
                    wait(eng, w.here())
                for c in range(2):
                    pool.add(PO.memset(V[c][:, :, :], 1.0))
                free, freed_raw, added, n = [None, None], [None, None], [None, None], 0
                for dst, weight, bias, tiles in ((QT, v["Wq"], v.get("bq"), 4), (KT, v["Wk"], v.get("bk"), kt)):
                    for t in range(tiles):
                        for half in range(2):
                            cols = slice(half * HALF, (half + 1) * HALF)
                            bank = psum[n % 2]
                            wait(PE, free[n % 2])
                            for k in range(KC):
                                mm = PE.matmul(bank[:, :], weight[:, k, t * P:(t + 1) * P], xT[:, k, cols], start=k == 0, stop=k == KC - 1)
                            m = pe.add(mm)
                            if rotary:
                                wait(AC, m, freed_raw[n % 2])
                                m2 = act.add(AC.activation(raw[n % 2][:, :], bank[:, :], ACT.Copy))
                                wait(DV, m2)
                                wait(PE, m2, free[(n + 1) % 2] if n else None, free[n % 2])
                                freed_raw[n % 2] = m3 = pe.add(PE.matmul(psum[2 + n % 2][:, :], turn16, raw[n % 2][:, :], start=True, stop=True))
                                dve.add(DV.tensor_tensor(four(dst[:, t, cols]), four(bank[:, :]), spread(cos16, 4), ALU.mult))
                                wait(DV, m3, added[n % 2])
                                free[n % 2] = m = dve.add(DV.tensor_tensor(four(turned[n % 2][:, :]), four(psum[2 + n % 2][:, :]), spread(sin16, 4), ALU.mult))
                                wait(PO, m)
                                added[n % 2] = pool.add(PO.tensor_tensor(dst[:, t, cols], dst[:, t, cols], turned[n % 2][:, :], ALU.add))
                            else:
                                wait(DV, m)
                                free[n % 2] = dve.add(DV.tensor_scalar(dst[:, t, cols], bank[:, :], bias[:, t:t + 1], None, ALU.add))
                            n += 1
                inner.close()
                small = Small(scope, f"s{stage}", masked=True)
                if not rotary:
                    for b in range(B):
                        pool.add(PO.tensor_tensor(x[:, b, :], x[:, b, :], v["bo"], ALU.add))
                for eng in engines:
                    wait(eng, *core.done())
                with core.repeat(B // 2) as i:
                    small.restart()
                    staged, quads, before, after, O_free = [], [], {}, {}, [core.last(f"O_free{c}") for c in range(2)]
                    for c in range(2):
                        b = 2 * i + c
                        wait(AC, *core.last(f"scored{c}", f"valued{c}"), apart=True)
                        staged_x = act.add(AC.activation(xTb2[c][:, :, :], wide(xT, b), ACT.Copy))
                        staged_q = act.add(AC.activation(QTb[c][:, :, :], wide(QT, b), ACT.Copy))
                        wait(DV, *core.last(f"scored{c}"), apart=True)
                        for n in range(2):
                            staged_k = dve.add(DV.tensor_scalar(KTb[c][n][:, :, :], wide(KT, b), parity[:, n:n + 1], None, ALU.mult))
                        staged.append((staged_x, staged_q, staged_k))
                        for pair in range(4):
                            rows = slice(32 * pair, 32 * pair + 32)
                            for second in range(2):
                                quad = []
                                for j in range(4):
                                    if rotary:
                                        t, par, head, key, kt_ = j, second, 4 * (2 * pair + second) + j, 2 * pair + second, 0
                                    else:
                                        t, par = 2 * second + j // 2, j % 2
                                        head = key = 8 * t + 2 * pair + par
                                        kt_ = t
                                    quad.append((QTb[c][rows, t, :], KTb[c][par][rows, kt_, :], V[c][:, key, :], head))
                                quads.append(quad)
                        if not rotary:
                            quads[8 * c:] = quads[8 * c::2] + quads[8 * c + 1::2]

                    def value_product(c):
                        nv = kv * HD
                        wait(PE, staged[c][0], *core.last("seven_free") if c == 0 else value_product.free)
                        for k in range(KC):
                            mm = PE.matmul(psum[7][:, 0:nv], xTb2[c][:, k, :], v["Wv"][:, k, :], start=k == 0, stop=k == KC - 1)
                        m = pe.add(mm)
                        core.note(f"valued{c}", m)
                        values = psum[7][:, 0:nv].rearrange("p (h d) -> p h d", d=HD)
                        wait(DV, m, *core.last(f"produced{c}"))
                        if rotary:
                            m = dve.add(DV.tensor_copy(V[c][:, :, 0:HD], values))
                        else:
                            m = dve.add(DV.tensor_tensor(V[c][:, :, 0:HD], values, v["bv"].rearrange("p (h d) -> p h d", d=HD), ALU.add))
                        value_product.free = [m]
                        return m

                    def heads_done(c):
                        def halves(half):
                            def end(m):
                                core.note(f"produced{c}", m)
                                m = small.divide(m, half, O[c][:, 16 * half:16 * half + 16, :], *(O_free[c] if half == 0 else []))
                                if half == 0:
                                    return
                                wait(PE, m, *value_product.free)
                                heads = O[c][:, :, :].rearrange("p h d -> p (h d)")
                                for k in range(KC):
                                    mm = PE.transpose(psum[7][:, k * P:(k + 1) * P], heads[:, k * P:(k + 1) * P], ident)
                                m = pe.add(mm)
                                core.note(f"O_free{c}", m)
                                wait(AC, m, staged[c][0], apart=True)
                                m = act.add(AC.activation(wide(xT, 2 * i + c), four(psum[7][:, :]), ACT.Copy))
                                value_product.free = [m]
                                core.note("seven_free", m)
                            return end
                        return halves

                    valued = [value_product(0), value_product(1)]
                    for c in range(2):
                        before[8 * c] = lambda c=c: [*staged[c][1:], valued[c]]
                        after[8 * c + 3] = heads_done(c)(0)
                        after[8 * c + 7] = heads_done(c)(1)
                    small.run(quads, spread(causal, 4), 0.25, before, after)
                    for c in range(2):
                        core.note(f"scored{c}", small.scored)
                    small.note()
                for eng in engines:
                    wait(eng, *core.done())
                free = [None, None]
                for b in range(B):
                    wait(PE, free[b % 2])
                    for k in range(KC):
                        mm = PE.matmul(psum[b % 2][:, :], xT[:, k, b * P:(b + 1) * P], v["Wo"][:, k, :], start=k == 0, stop=k == KC - 1)
                    m = pe.add(mm)
                    wait(DV, m)
                    free[b % 2] = dve.add(DV.tensor_tensor(x[:, b, :], psum[b % 2][:, :], x[:, b, :], ALU.add))
                for eng in engines:
                    wait(eng, *core.done())
            finish_all()

        def load_feature(stage, free):
            w = Weights(stage, free)
            load_context()
            return w.load("ctx"), w

        def feature_attention(stage, ctx, w):
            scale = float(P) ** -0.5
            with ExitStack() as scope:
                kb = sbuf("kb", [P, D], scope)
                vTb = sbuf("vTb", [P, KC, P], scope)
                E = [sbuf(f"E_feature{n}", [P, D], scope) for n in range(2)]
                PT = sbuf("PT_feature", [P, KC, D], scope)
                small = sbuf("small_feature", [P, 4, 4], scope)
                for eng in engines:
                    wait(eng, w.here(), ctx_here)
                with core.repeat(B) as b:
                    start = core.done()
                    xrow = x[:, bass.ds(b, 1), :].rearrange("p o d -> p (o d)")
                    wait(AC, *start, apart=True)
                    staged = act.add(AC.activation(kb[:, :], ctx[:, bass.ds(b, 1), :].rearrange("p o d -> p (o d)"), ACT.Copy))
                    wait(PO, *start, apart=True)
                    staged_v = pool.add(PO.tensor_copy(vTb[:, :, :], wide(ctxT, b)))
                    wait(DV, *start)
                    wait(PE, *start)
                    wait(PE, staged, apart=True)
                    exps, t_free, e_free, copied = {}, {}, {}, None
                    for step in range(KC + 1):
                        if step < KC:
                            j = step
                            m = pe.add(PE.matmul(psum[j][:, :], kb[:, j * P:(j + 1) * P], xrow, start=True, stop=True))
                            wait(DV, m)
                            m = dve.add(DV.tensor_reduce(small[:, 0, j:j + 1], psum[j][:, :], AX.X, ALU.max, negate=True))
                            wait(DV, m)
                            m = dve.add(DV.tensor_scalar(small[:, 1, j:j + 1], small[:, 0, j:j + 1], scale, None, ALU.mult))
                            wait(AC, m, e_free.get(j - 2))
                            m = act.add(AC.activation(E[j % 2][:, :], psum[j][:, :], ACT.Exp, bias=small[:, 1, j:j + 1], scale=scale, accum_out=small[:, 2, j:j + 1]))
                            wait(DV, m)
                            m = dve.add(DV.reciprocal(small[:, 3, j:j + 1], small[:, 2, j:j + 1]))
                            wait(DV, m)
                            exps[j] = dve.add(DV.tensor_scalar(E[j % 2][:, :], E[j % 2][:, :], small[:, 3, j:j + 1], None, ALU.mult))
                        if step >= 1:
                            j = step - 1
                            bank = psum[4 + j % 2]
                            wait(PE, exps[j], t_free.get(j - 2))
                            for k in range(KC):
                                mm = PE.transpose(bank[:, k * P:(k + 1) * P], E[j % 2][:, k * P:(k + 1) * P], ident)
                            m = e_free[j] = pe.add(mm)
                            wait(AC, m)
                            copied = t_free[j] = act.add(AC.activation(PT[:, :, j * P:(j + 1) * P], four(bank[:, :]), ACT.Copy))
                    wait(PE, copied, staged_v)
                    for k in range(KC):
                        mm = PE.matmul(psum[7][:, :], vTb[:, k, :], PT[:, k, :], start=k == 0, stop=k == KC - 1)
                    m = pe.add(mm)
                    wait(DV, m, apart=True)
                    m = dve.add(DV.tensor_tensor(y[:, :], psum[7][:, :], xrow, ALU.add))
                    finish_rows(b, m)

        def load_single(stage, free):
            w = Weights(stage, free)
            v = {n: w.load(f"L3_attn_{n}") for n in ("Wqkv", "bqk", "Wo")}
            v.update({n: w.load(f"L3_attn_{n}", broadcast=True) for n in ("bv", "bo")})
            return v, w

        def single_head(stage, v, w):
            with ExitStack() as scope:
                QK = sbuf("QK9", [P, 2, T], scope)
                V = sbuf("V9", [P, B, P], scope)
                soft = Softmax(scope, "s9")
                PT = [sbuf(f"PT{n}_9", [P, 4, P], scope) for n in range(2)]
                OT = [sbuf(f"OT{n}_9", [P, 4, P], scope) for n in range(2)]
                for eng in engines:
                    wait(eng, w.here())
                for b in range(B):
                    biased = pool.add(PO.tensor_tensor(x[:, b, :], x[:, b, :], v["bo"], ALU.add))
                free = [None, None]
                for n in range(4):
                    which, half = n // 2, n % 2
                    cols, bank = slice(half * HALF, (half + 1) * HALF), psum[n % 2]
                    wait(PE, free[n % 2])
                    for k in range(KC):
                        mm = PE.matmul(bank[:, :], v["Wqkv"][:, k, which * P:(which + 1) * P], xT[:, k, cols], start=k == 0, stop=k == KC - 1)
                    m = pe.add(mm)
                    wait(DV, m)
                    free[n % 2] = keyed = dve.add(DV.tensor_scalar(QK[:, which, cols], bank[:, :], v["bqk"][:, which:which + 1], None, ALU.add))
                for half in range(2):
                    bank = psum[2 + half]
                    for b in range(4 * half, 4 * half + 4):
                        for k in range(KC):
                            mm = PE.matmul(bank[:, b % 4 * P:(b % 4 + 1) * P], xT[:, k, b * P:(b + 1) * P], v["Wqkv"][:, k, 2 * P:3 * P], start=k == 0, stop=k == KC - 1)
                    m = pe.add(mm)
                    wait(DV, m)
                    valued = dve.add(DV.tensor_tensor(V[:, 4 * half:4 * half + 4, :], four(bank[:, :]), spread(v["bv"], 4), ALU.add))
                wait(PE, keyed)
                soft_done = []
                for u in range(2):
                    bank = psum[4 + u]
                    for j in range(4):
                        cols = slice((4 * u + j) * P, (4 * u + j + 1) * P)
                        mm = PE.matmul(bank[:, j * P:(j + 1) * P], QK[:, 0, cols], QK[:, 1, cols], start=True, stop=True)
                    m = pe.add(mm)
                    soft_done.append(soft.run(u, m, [four(bank[:, :])], float(P) ** -0.5, None)[0])
                y_free = {}
                for u in range(2):
                    bank = psum[6 + u]
                    wait(PE, soft_done[u])
                    for j in range(4):
                        mm = PE.transpose(bank[:, j * P:(j + 1) * P], soft.E[u][:, j, :], ident)
                    m = pe.add(mm)
                    wait(AC, m)
                    m = act.add(AC.activation(PT[u][:, :, :], four(bank[:, :]), ACT.Copy))
                    wait(PE, m, valued)
                    for j in range(4):
                        mm = PE.matmul(bank[:, j * P:(j + 1) * P], V[:, 4 * u + j, :], PT[u][:, j, :], start=True, stop=True)
                    m = pe.add(mm)
                    wait(AC, m)
                    m = act.add(AC.activation(OT[u][:, :, :], four(bank[:, :]), ACT.Copy))
                    wait(PE, m)
                    wait(DV, biased)
                    for j in range(4):
                        b = 4 * u + j
                        wait(PE, y_free.get(b - 2))
                        m = pe.add(PE.matmul(psum[b % 2][:, :], OT[u][:, j, :], v["Wo"], start=True, stop=True))
                        wait(DV, m)
                        y_free[b] = dve.add(DV.tensor_tensor(x[:, b, :], psum[b % 2][:, :], x[:, b, :], ALU.add))
                for eng in engines:
                    wait(eng, *core.done())
            finish_all()

        CH = 64
        UN = CH // 4

        def load_heads(stage, free):
            w = Weights(stage, free)
            v = {n: w.load(f"L0_attn_{n}") for n in ("wq", "wk", "wv", "bq", "bk")}
            v["bv"] = w.load("L0_attn_bv", broadcast=True)
            return v, w

        def between_heads(stage, v, w):
            scratch = {n: nc.dram_tensor(f"scratch_{n}", (T * D,), F32, kind="Internal").ap() for n in "qkvo"}
            stores = [Counter(core, f"scratch_stored{n}", 16) for n in range(4)]
            with ExitStack() as scope:
                QK = [sbuf(f"QK{n}_0", [P, T], scope) for n in range(2)]
                Vr = [sbuf(f"Vr{n}_0", [P, D], scope) for n in range(2)]
                for eng in engines:
                    wait(eng, w.here())
                free, stored_, n = [None, None], [None] * 4, 0
                for which, (weight, bias) in enumerate(((v["wq"], v["bq"]), (v["wk"], v["bk"]))):
                    view = scratch["qk"[which]].rearrange("(m p t) -> m p t", p=P, t=T)
                    for t in range(4):
                        buffer = QK[t % 2]
                        for half in range(2):
                            bank, cols = psum[n % 2], slice(half * HALF, (half + 1) * HALF)
                            wait(PE, free[n % 2])
                            for k in range(KC):
                                mm = PE.matmul(bank[:, :], weight[:, k, t * P:(t + 1) * P], xT[:, k, cols], start=k == 0, stop=k == KC - 1)
                            m = pe.add(mm)
                            wait(DV, m, stored_[t % 2])
                            m = free[n % 2] = dve.add(DV.tensor_scalar(buffer[:, cols], bank[:, :], bias[:, t:t + 1], 1.0 if which else 0.25, ALU.add, ALU.mult))
                            n += 1
                        wait(SP, m)
                        stored_[t % 2] = stores[t % 2].add(SP.dma_start(view[t], buffer[:, :]))
                view = scratch["v"].rearrange("(n u q d) -> n q u d", u=UN, q=4, d=D)
                for b in range(B):
                    bank = psum[n % 2]
                    wait(PE, free[n % 2])
                    for k in range(KC):
                        mm = PE.matmul(bank[:, :], xT[:, k, b * P:(b + 1) * P], v["wv"][:, k, :], start=k == 0, stop=k == KC - 1)
                    m = pe.add(mm)
                    wait(DV, m, stored_[2 + b % 2])
                    m = free[n % 2] = dve.add(DV.tensor_tensor(Vr[b % 2][:, :], bank[:, :], v["bv"], ALU.add))
                    n += 1
                    wait(SP, m)
                    for c in range(2):
                        stored_[2 + b % 2] = stores[2 + b % 2].add(SP.dma_start(view[2 * b + c], Vr[b % 2][c * CH:(c + 1) * CH, :]))
                for eng in engines:
                    wait(eng, *core.done())
            with ExitStack() as scope:
                q16 = [sbuf(f"q16_{c}", [HD + 4, HEADS, CH], scope) for c in range(2)]
                k16 = [sbuf(f"k16_{c}", [HD + 4, HEADS, CH], scope) for c in range(2)]
                V17 = [sbuf(f"V17_{c}", [P, UN, 17], scope) for c in range(2)]
                O = [sbuf(f"O0_{c}", [P, UN, HD], scope) for c in range(2)]
                small = Small(scope, "s0", masked=False)
                qk_in = [Counter(core, f"stream_qk{c}", 16) for c in range(2)]
                v_in = [Counter(core, f"stream_v{c}", 16) for c in range(2)]
                rows_in = Counter(core, "stream_mask_rows", 16)
                o_out = [Counter(core, f"o_stored{c}", 16, starter=AC) for c in range(2)]
                view = {n: scratch[n].rearrange("(h d t) -> d h t", d=HD, t=T) for n in "qk"}
                view["v"] = scratch["v"].rearrange("(n u p d) -> n p u d", u=UN, p=P, d=HD)
                view["o"] = scratch["o"].rearrange("(n q u h d) -> n q h u d", q=4, u=UN, h=HEADS, d=HD)
                wait(SP, *core.done())
                wait(SP, *stored_)
                for c in range(2):
                    rows_in.add(SP.dma_start(q16[c][HD:HD + 4, :, :], dram["mask_rows"][0]))
                    rows_in.add(SP.dma_start(k16[c][HD:HD + 4, :, :], dram["mask_rows"][1]))
                    ones_set = pool.add(PO.memset(V17[c][:, :, :], 1.0))

                def load_qk(c, i):
                    for n, buffer in (("q", q16[c]), ("k", k16[c])):
                        yield SP.dma_start(buffer[0:HD, :, :], view[n][:, :, bass.ds(i * P + c * CH, CH)])

                def load_v(c, i):
                    return SP.dma_start(V17[c][:, :, 0:HD], view["v"][bass.ds(2 * i + c, 1)].rearrange("o p u d -> (o p) u d"))

                wait(SP, ones_set)
                for c in range(2):
                    for d in load_qk(c, 0):
                        qk_in[c].add(d)
                    v_in[c].add(load_v(c, 0))
                wait(PE, rows_in.now())
                with core.repeat(B, streams={qk_in[0]: 2, qk_in[1]: 2, v_in[0]: 1, v_in[1]: 1}) as b:
                    stored_before = [o.now() for o in o_out]
                    small.restart()
                    scored, summed, quads, before, after = [], [], [], {}, {}
                    for c in range(2):
                        q = q16[c][:, :, :].rearrange("d h (q u) -> d u (h q)", u=UN)
                        k = k16[c][:, :, :].rearrange("d h (q u) -> d u q h", u=UN)
                        quads += [[(q[:, 4 * u + j, :], k[:, 4 * u + j, :, :],
                                    V17[c][:, 4 * u + j, :], 16 * c + 4 * u + j) for j in range(4)] for u in range(4)]

                        def end(m, c=c):
                            summed.append(m)
                            m = small.divide(m, c, O[c][:, :, :], stored_before[c])
                            wait(AC, m)
                            for q in range(4):
                                o_out[c].add(AC.dma_start(view["o"][bass.ds(2 * b + c, 1), q].rearrange("o h u d -> (o h) u d"),
                                                          O[c][q:P:4, :, :]))

                        before[4 * c] = lambda c=c: [qk_in[c].first(), v_in[c].first()]
                        after[4 * c + 3] = end
                    small.run(quads, None, 1.0, before, after)
                    scored = [small.scored_marks[3], small.scored_marks[7]]
                    small.note()
                with SP.Fori(0, B - 1) as i:
                    for c in range(2):
                        core.wait_at(SP, i, scored[c])
                        for d in load_qk(c, i + 1):
                            d.then_inc(qk_in[c].sem, 16)
                        core.wait_at(SP, i, summed[c])
                        load_v(c, i + 1).then_inc(v_in[c].sem, 16)
                for eng in engines:
                    wait(eng, *core.done())
                wait(SP, *core.done())
                wait(SP, *[o.now() for o in o_out])
            with ExitStack() as scope:
                rows = sbuf("O_rows", [P, B, D], scope)
                back = Counter(core, "o_loaded", 16)
                back.add(SP.dma_start(rows[:, :, :], scratch["o"].rearrange("(b p d) -> p b d", p=P, d=D)))
                wait(DV, back.now())
                for b in range(B):
                    dve.add(DV.tensor_tensor(x[:, b, :], x[:, b, :], rows[:, b, :], ALU.add))
                for eng in engines:
                    wait(eng, *core.done())
            finish_all()

        SLOTS, BOT, RD, VB = 128, 64, 48, 32

        def load_slots(stage, free):
            w = Weights(stage, free)
            v = {n: w.load(f"L0_ffn_{n}") for n in ("Wq", "WrT", "Wr", "aux_keysT", "aux_valuesT", "WvdT", "WvuT", "Wu1T")}
            v.update({n: w.load(f"L0_ffn_{n}", broadcast=True) for n in ("bu1", "Wu2", "bu2", "gate_w1", "gate_bias", "log_rel")})
            return v, w

        def slots(stage, v, w):
            with ExitStack() as scope:
                G = sbuf("G", [P, KC, 2 * SLOTS], scope)
                values = sbuf("slot_values", [SLOTS, D], scope)
                rkT = sbuf("rkT", [RD, SLOTS], scope)
                H = sbuf("H", [BOT, SLOTS], scope)
                avT = sbuf("avT", [VB, SLOTS], scope)
                ones_sq = sbuf("ones_sq", [P, P], scope)
                st = sbuf("slot_stats", [P, B, 6], scope)
                mv = sbuf("slot_mv", [P, B, 2], scope)
                lv = sbuf("slot_lv", [P, B], scope)
                nv = sbuf("slot_nv", [P, B], scope)
                c = sbuf("slot_small", [P, 32], scope)
                sc, at, rep, sel, E, h, p, g = (sbuf(f"slot_{n}", [P, SLOTS], scope) for n in ("sc", "at", "rep", "sel", "E", "h", "p", "g"))
                ET = sbuf("slot_ET", [SLOTS, P], scope)
                x2 = sbuf("slot_x2", [P, D], scope)
                for eng in engines:
                    wait(eng, w.here())
                m = pe.add(PE.matmul(psum[0][0:RD, 0:SLOTS], v["WrT"], v["aux_keysT"], start=True, stop=True))
                wait(DV, m)
                m = dve.add(DV.tensor_copy(rkT[:, :], psum[0][0:RD, 0:SLOTS]))
                wait(PE, m)
                m = pe.add(PE.matmul(psum[0][0:BOT, 0:SLOTS], v["Wr"], rkT[:, :], start=True, stop=True))
                wait(DV, m)
                m = dve.add(DV.tensor_copy(H[:, :], psum[0][0:BOT, 0:SLOTS]))
                wait(PE, m)
                for k in range(KC):
                    cols = slice(k * P, (k + 1) * P)
                    PE.matmul(psum[1][:, cols], v["Wq"][:, cols], H[:, :], start=True, stop=True)
                    mm = PE.matmul(psum[2][:, cols], v["Wq"][:, cols], v["aux_keysT"], start=True, stop=True)
                m = pe.add(mm)
                wait(DV, m)
                dve.add(DV.tensor_copy(G[:, :, 0:SLOTS], four(psum[1][:, :])))
                dve.add(DV.tensor_copy(G[:, :, SLOTS:], four(psum[2][:, :])))
                for k in range(KC):
                    mm = PE.matmul(psum[3][0:VB, 0:SLOTS], v["WvdT"][:, k, :], v["aux_valuesT"][:, k, :], start=k == 0, stop=k == KC - 1)
                m = pe.add(mm)
                wait(DV, m)
                m = dve.add(DV.tensor_copy(avT[:, :], psum[3][0:VB, 0:SLOTS]))
                wait(PE, m)
                m = pe.add(PE.matmul(psum[4][:, :], avT[:, :], v["WvuT"], start=True, stop=True))
                wait(DV, m)
                dve.add(DV.tensor_copy(values[:, :], psum[4][:, :]))
                s1 = pool.add(PO.memset(ones_sq[:, :], 1.0))
                for b in range(B):
                    m = dve.add(DV.bn_stats(st[:, b, :], x[:, b, :]))
                wait(DV, m)
                for b in range(B):
                    m = dve.add(DV.bn_aggr(mv[:, b, :], st[:, b, :]))
                wait(AC, m)
                m = act.add(AC.activation(lv[:, :], mv[:, :, 1], ACT.Ln, bias=ones[:, 0:1]))
                wait(DV, m)
                m = dve.add(DV.tensor_reduce(c[:, 0:1], lv[:, :], AX.X, ALU.add))
                wait(PE, m, s1)
                m = pe.add(PE.matmul(psum[5][:, 0:1], ones_sq[:, :], c[:, 0:1], start=True, stop=True))
                wait(DV, m)
                m = dve.add(DV.tensor_scalar(c[:, 1:2], psum[5][:, 0:1], 1.0 / T, 1e-6, ALU.mult, ALU.add))
                wait(DV, m)
                m = dve.add(DV.reciprocal(c[:, 2:3], c[:, 1:2]))
                wait(DV, m)
                dve.add(DV.tensor_scalar(nv[:, :], lv[:, :], c[:, 2:3], 0.5, ALU.mult, ALU.mult))
                for eng in engines:
                    wait(eng, *core.done())
                with core.repeat(B) as b:
                    start = core.done()
                    xrow = x[:, bass.ds(b, 1), :].rearrange("p o d -> p (o d)")
                    wait(AC, *start, apart=True)
                    m = act.add(AC.activation(xTb[:, :, :], wide(xT, b), ACT.Copy))
                    wait(PO, *start)
                    doubled = pool.add(PO.tensor_tensor(x2[:, :], xrow, xrow, ALU.add))
                    wait(PE, *start)
                    wait(PE, m)
                    for k in range(KC):
                        mm = PE.matmul(psum[0][:, 0:2 * SLOTS], xTb[:, k, :], G[:, k, :], start=k == 0, stop=k == KC - 1)
                    m = pe.add(mm)
                    for k in range(KC):
                        mm = PE.matmul(psum[1][:, 0:P], xTb[:, k, :], v["Wu1T"][:, k, :], start=k == 0, stop=k == KC - 1)
                    hidden = pe.add(mm)
                    wait(DV, *start)
                    wait(DV, m)
                    m = dve.add(DV.scalar_tensor_tensor(sc[:, :], psum[0][:, 0:SLOTS], float(RD) ** -0.5, v["log_rel"], ALU.mult, ALU.add))
                    dve.add(DV.scalar_tensor_tensor(at[:, :], psum[0][:, SLOTS:2 * SLOTS], float(BOT) ** -0.5, v["log_rel"], ALU.mult, ALU.add))
                    wait(DV, m, apart=True)
                    m = dve.add(DV.max(c[:, 8:16], sc[:, :]))
                    wait(DV, m, apart=True)
                    m = dve.add(DV.match_replace(rep[:, :], c[:, 8:16], sc[:, :], -3.0e38))
                    wait(DV, m)
                    m = dve.add(DV.tensor_tensor(sel[:, :], rep[:, :], sc[:, :], ALU.not_equal))
                    wait(DV, m)
                    m = dve.add(DV.tensor_scalar(sel[:, :], sel[:, :], -1.0, -NEG, ALU.add, ALU.mult))
                    wait(DV, m)
                    m = dve.add(DV.tensor_tensor(at[:, :], at[:, :], sel[:, :], ALU.add))
                    wait(DV, m)
                    m = dve.add(DV.tensor_reduce(c[:, 16:17], at[:, :], AX.X, ALU.max, negate=True))
                    wait(AC, m)
                    m = act.add(AC.activation(E[:, :], at[:, :], ACT.Exp, bias=c[:, 16:17], accum_out=c[:, 17:18]))
                    wait(PE, m)
                    m = pe.add(PE.transpose(psum[2][:, 0:P], E[:, :], ident))
                    wait(AC, m)
                    m = act.add(AC.activation(ET[:, :], psum[2][:, 0:P], ACT.Copy))
                    wait(PE, m)
                    mixed = pe.add(PE.matmul(psum[3][:, :], ET[:, :], values[:, :], start=True, stop=True))
                    wait(DV, hidden)
                    m = dve.add(DV.tensor_tensor(h[:, :], psum[1][:, 0:P], v["bu1"], ALU.add))
                    wait(DV, m)
                    m = dve.add(DV.tensor_tensor(p[:, :], h[:, :], h[:, :], ALU.mult))
                    wait(DV, m)
                    m = dve.add(DV.tensor_scalar(p[:, :], p[:, :], 0.044715, 1.0, ALU.mult, ALU.add))
                    wait(DV, m)
                    m = dve.add(DV.tensor_tensor(p[:, :], p[:, :], h[:, :], ALU.mult))
                    wait(DV, m)
                    m = dve.add(DV.tensor_scalar(p[:, :], p[:, :], -50.0, None, ALU.max))
                    wait(AC, m)
                    m = act.add(AC.activation(g[:, :], p[:, :], ACT.Exp, scale=-2.0 * float(np.sqrt(2.0 / np.pi))))
                    wait(DV, m)
                    m = dve.add(DV.tensor_scalar(g[:, :], g[:, :], 1.0, None, ALU.add))
                    wait(DV, m)
                    m = dve.add(DV.reciprocal(g[:, :], g[:, :]))
                    wait(DV, m)
                    m = dve.add(DV.tensor_tensor(g[:, :], g[:, :], h[:, :], ALU.mult))
                    wait(DV, m)
                    m = dve.add(DV.tensor_tensor(g[:, :], g[:, :], v["Wu2"], ALU.mult))
                    wait(DV, m)
                    m = dve.add(DV.tensor_reduce(c[:, 18:19], g[:, :], AX.X, ALU.add))
                    wait(DV, m)

                    def sigmoid(at, source):
                        m = act.add(AC.activation(c[:, at:at + 1], source, ACT.Exp, scale=-1.0))
                        wait(DV, m)
                        m = dve.add(DV.tensor_scalar(c[:, at:at + 1], c[:, at:at + 1], 1.0, None, ALU.add))
                        wait(DV, m)
                        m = dve.add(DV.reciprocal(c[:, at:at + 1], c[:, at:at + 1]))
                        wait(DV, m)
                        return m

                    m = dve.add(DV.tensor_scalar(c[:, 19:20], c[:, 18:19], v["bu2"][:, 0:1], -80.0, ALU.add, ALU.max))
                    wait(AC, m)
                    sigmoid(20, c[:, 19:20])
                    m = dve.add(DV.tensor_scalar(c[:, 21:22], c[:, 20:21], 2.5, None, ALU.mult))
                    wait(DV, m)
                    m = dve.add(DV.tensor_tensor(c[:, 21:22], c[:, 21:22], nv[:, bass.ds(b, 1)], ALU.add))
                    wait(DV, m)
                    m = dve.add(DV.tensor_scalar(c[:, 21:22], c[:, 21:22], 0.0, 5.0, ALU.max, ALU.min))
                    wait(DV, m)
                    m = dve.add(DV.tensor_scalar(c[:, 21:22], c[:, 21:22], -0.5, 1.0 / 1.5, ALU.add, ALU.mult))
                    wait(DV, m)
                    m = dve.add(DV.tensor_scalar(c[:, 21:22], c[:, 21:22], 0.0, 1.0, ALU.max, ALU.min))
                    wait(DV, m)
                    m = dve.add(DV.tensor_scalar(c[:, 22:23], c[:, 21:22], v["gate_w1"][:, 0:1], v["gate_bias"][:, 0:1], ALU.mult, ALU.add))
                    wait(DV, m)
                    m = dve.add(DV.tensor_scalar(c[:, 22:23], c[:, 22:23], -80.0, None, ALU.max))
                    wait(AC, m)
                    sigmoid(23, c[:, 22:23])
                    m = dve.add(DV.tensor_scalar(c[:, 24:25], c[:, 23:24], 0.05, None, ALU.is_ge))
                    r = dve.add(DV.reciprocal(c[:, 25:26], c[:, 17:18]))
                    wait(DV, r)
                    m = dve.add(DV.tensor_tensor(c[:, 26:27], c[:, 23:24], c[:, 24:25], ALU.mult))
                    wait(DV, m)
                    m = dve.add(DV.tensor_tensor(c[:, 27:28], c[:, 26:27], c[:, 25:26], ALU.mult))
                    wait(DV, m, mixed, doubled)
                    m = dve.add(DV.scalar_tensor_tensor(y[:, :], psum[3][:, :], c[:, 27:28], x2[:, :], ALU.mult, ALU.add))
                    finish_rows(b, m)

        H96, G4 = 96, 4

        def load_latent(stage, free):
            w = Weights(stage, free)
            load_context()
            qkv, o = Counter(core, "stream_qkv10", 16), Counter(core, "stream_out10", 16)
            views = {}
            for name, rows, shape in (("wq", P, (KC, 4 * H96)), ("wk", P, (KC, H96)), ("wv", P, (KC, H96)), ("wo", H96, (4, D))):
                n = shape[0] * shape[1]
                views[name] = w.arena[0:rows, w.at:w.at + n].rearrange("p (k n) -> p k n", k=shape[0])
                w.at += n
                (o if name == "wo" else qkv).add(SP.dma_start(views[name], dram[f"L3_x{name}"][0]))
            return views, w, qkv, o

        def latent(stage, views, w, qkv, o):
            wq, wk, wv, wo = (views[n] for n in ("wq", "wk", "wv", "wo"))
            with ExitStack() as scope:
                QT = sbuf("QT10", [H96, 4, T], scope)
                KT = sbuf("KT10", [H96, B, 2, P], scope)
                V = sbuf("V10", [P, 2, B, H96], scope)
                soft = Softmax(scope, "s10", width=2 * P, depth=3, masked=False)
                PT = sbuf("PT10", [P, 2, 4, P], scope)
                OT = [sbuf(f"OT{n}_10", [H96, 4, P], scope) for n in range(2)]
                for eng in engines:
                    wait(eng, ctx_here)
                with core.repeat(G4, streams={qkv: 3, o: 1}) as g:
                    wait(PE, qkv.first())
                    for eng in (DV, AC):
                        wait(eng, *core.last("scored", "mixed"))
                    soft.restart()
                    bank_free = {n: core.last(f"bank{n}_free") for n in (6, 7)}
                    free, n, jobs = [bank_free[6], bank_free[7]], 0, []
                    for s_, source in ((0, ctxT), (1, xT)):
                        for half in range(2):
                            jobs.append((KT[:, 4 * half:4 * half + 4, s_, :], source, half, wk[:, :, :]))
                    for h in range(4):
                        for half in range(2):
                            jobs.append((four(QT[:, h, half * HALF:(half + 1) * HALF]), xT, half, wq[:, :, h * H96:(h + 1) * H96]))
                    for dst, source, half, weight in jobs:
                        bank = psum[6 + n % 2]
                        wait(PE, *free[n % 2])
                        for k in range(KC):
                            mm = PE.matmul(bank[0:H96, :], weight[:, k, :], source[:, k, half * HALF:(half + 1) * HALF], start=k == 0, stop=k == KC - 1)
                        m = pe.add(mm)
                        wait(AC if n % 2 else DV, m)
                        if n % 2:
                            free[1] = [act.add(AC.activation(dst, four(bank[0:H96, :]), ACT.Copy))]
                        else:
                            free[0] = [dve.add(DV.tensor_copy(dst, four(bank[0:H96, :])))]
                        n += 1
                    for s_, source in ((0, ctxT), (1, xT)):
                        for half in range(2):
                            bank = psum[6 + n % 2]
                            wait(PE, *free[n % 2])
                            for b in range(4 * half, 4 * half + 4):
                                for k in range(KC):
                                    mm = PE.matmul(bank[:, b % 4 * H96:(b % 4 + 1) * H96], source[:, k, b * P:(b + 1) * P], wv[:, k, :], start=k == 0, stop=k == KC - 1)
                            m = projected = pe.add(mm)
                            wait(AC if n % 2 else DV, m)
                            dst = V[:, s_, 4 * half:4 * half + 4, :]
                            source4 = four(bank[:, 0:4 * H96])
                            if n % 2:
                                free[1] = [act.add(AC.activation(dst, source4, ACT.Copy))]
                            else:
                                free[0] = [dve.add(DV.tensor_copy(dst, source4))]
                            n += 1
                    bank_free = {6: free[0], 7: free[1]}
                    score_free, t_free, ot_free = ([core.last(f"{t}{n}_free") for n in range(2)] for t in ("score", "t", "ot"))
                    pt_read, done, copied = core.last("mixed"), {}, {}
                    wait(PE, *free[0], *free[1])
                    for step in range(B + 3):
                        if 2 <= step < B + 2:
                            b = step - 2
                            wait(PE, done[b])
                            E = soft.E[b % 3]
                            for s_ in range(2):
                                bank = psum[4 + s_]
                                wait(PE, *t_free[s_])
                                for h in range(4):
                                    mm = PE.transpose(bank[:, h * P:(h + 1) * P], E[:, h, s_ * P:(s_ + 1) * P], ident)
                                m = pe.add(mm)
                                soft.used[b % 3] = [m]
                                wait(DV if s_ else AC, m, *pt_read)
                                if s_:
                                    t_free[s_] = [dve.add(DV.tensor_copy(PT[:, s_, :, :], four(bank[:, :])))]
                                else:
                                    t_free[s_] = [act.add(AC.activation(PT[:, s_, :, :], four(bank[:, :]), ACT.Copy))]
                        if step < B:
                            b = step
                            banks = psum[2 * (b % 2):2 * (b % 2) + 2]
                            wait(PE, *score_free[b % 2])
                            for h in range(4):
                                mm = PE.matmul(banks[h // 2][:, h % 2 * 256:(h % 2 + 1) * 256], QT[:, h, b * P:(b + 1) * P],
                                               KT[:, b, :, :].rearrange("p s n -> p (s n)"), start=True, stop=True)
                            m = pe.add(mm)
                            core.note("scored", m)
                            tiles = [t[:, :].rearrange("p (a n) -> p a n", a=2) for t in banks]
                            done[b], freed_ = soft.run(b, m, tiles, float(H96) ** -0.5, None)
                            score_free[b % 2] = [freed_]
                        if step >= 3:
                            b = step - 3
                            if b == 0:
                                wait(PE, o.first())
                            wait(PE, copied[b], *bank_free[7])
                            for h in range(4):
                                mm = PE.matmul(psum[7][:, :], OT[b % 2][:, h, :], wo[:, h, :], start=h == 0, stop=h == 3)
                            m = last = pe.add(mm)
                            ot_free[b % 2] = [m]
                            wait(DV, m)
                            bank_free[7] = [dve.add(DV.tensor_tensor(x[:, b, :], psum[7][:, :], x[:, b, :], ALU.add))]
                        if 2 <= step < B + 2:
                            b = step - 2
                            wait(PE, *t_free[0], *t_free[1], *bank_free[6])
                            for s_ in range(2):
                                mm = PE.matmul(psum[6][0:H96, :], V[:, s_, b, :], PT[:, s_, :, :], start=s_ == 0, stop=s_ == 1)
                            m = pe.add(mm)
                            pt_read = [m]
                            core.note("mixed", m)
                            wait(DV, m, *ot_free[b % 2])
                            copied[b] = dve.add(DV.tensor_copy(OT[b % 2][:, :, :], four(psum[6][0:H96, :])))
                            bank_free[6] = [copied[b]]
                    soft.note()
                    for n in range(2):
                        for name, marks in (("score", score_free), ("t", t_free), ("ot", ot_free)):
                            core.note(f"{name}{n}_free", marks[n][0])
                        core.note(f"bank{6 + n}_free", bank_free[6 + n][0])
                with SP.Fori(0, G4 - 1) as i:
                    core.wait_at(SP, i, projected)
                    for name in ("wq", "wk", "wv"):
                        SP.dma_start(views[name], dram[f"L3_x{name}"][bass.ds(i + 1, 1)].rearrange("o p k n -> (o p) k n")).then_inc(qkv.sem, 16)
                    core.wait_at(SP, i, last)
                    SP.dma_start(wo, dram["L3_xwo"][bass.ds(i + 1, 1)].rearrange("o p k n -> (o p) k n")).then_inc(o.sem, 16)
                for eng in engines:
                    wait(eng, *core.done())
            finish_all()

        LOAD = {0: load_heads, 2: load_slots, 10: load_latent, 3: load_rotary16, 6: load_bias16, 7: load_feature, 9: load_single, 1: load_cross, 4: load_cross, 5: load_experts, 8: load_experts, 11: load_experts}
        RUN = {0: between_heads, 2: slots, 10: latent, 3: small_attention, 6: small_attention, 7: feature_attention, 9: single_head, 1: cross, 4: cross, 5: experts, 8: experts, 11: experts}
        wait_for = [x_here]
        for eng in (PE, AC, DV, PO):
            wait(eng, x_here)
        todo = list(STAGES)
        ready = LOAD[todo[0]](todo[0], [])
        ended = {0: [], 1: []}
        for n, stage in enumerate(todo):
            here = ready
            if n + 1 < len(todo):
                nxt = todo[n + 1]
                ready = LOAD[nxt](nxt, ended[nxt % 2] if (nxt % 2) != (stage % 2) else [])
            RUN[stage](stage, *here)
            end = core.done()
            ended[stage % 2] = end
            for eng in (PE, AC, DV, PO):
                wait(eng, *end)
        wait(SP, *core.done())
        kept = stored.add(SP.dma_start(out, x[:, :, :]))
        wait(SP, kept)
        return core.noted


def chunks(w):
    k, n = w.shape
    return np.ascontiguousarray(w.reshape(k // P, P, n).transpose(1, 0, 2))


def rope(dim, positions):
    f = np.float32
    inv = (f(1.0) / f(10000.0) ** (np.arange(0, dim, 2, dtype=f) / f(dim))).astype(f)
    ang = np.arange(positions, dtype=f)[None, :] * inv[:, None]
    return np.cos(ang).astype(f), np.sin(ang).astype(f)


def constants():
    f = np.float32
    c = np.zeros((P, 8 * P + 32), f)
    c[:, 0:P] = np.eye(P)
    c[:, P:2 * P] = np.where(np.tril(np.ones((P, P), bool)), 0, NEG)
    c[:, 2 * P:3 * P] = np.where(np.kron(np.eye(4), np.ones((32, 32))) > 0, 0, NEG)
    cos, sin = rope(P, P)
    c[:, 3 * P:4 * P] = np.concatenate([cos, cos])
    c[:, 4 * P:5 * P] = np.concatenate([sin, -sin])
    cos, sin = rope(16, P)
    c[:, 5 * P:6 * P] = np.tile(np.concatenate([cos, cos]), (8, 1))
    c[:, 6 * P:7 * P] = np.tile(np.concatenate([-sin, sin]), (8, 1))
    partner = np.array([16 * (p // 16) + (p % 16 + 8) % 16 for p in range(P)])
    c[partner, 7 * P + np.arange(P)] = 1
    c[:, 8 * P] = (np.arange(P) // 16) % 2 == 0
    c[:, 8 * P + 1] = (np.arange(P) // 16) % 2 == 1
    c[:, 8 * P + 2:8 * P + 4] = 1
    c[:, 8 * P + 5] = EPS
    c[:, 8 * P + 6] = -0.5
    c[:, 8 * P + 16:8 * P + 24], c[:, 8 * P + 24:8 * P + 32] = EPS, -0.5
    return c


def layout(i):
    a = {"const": constants()}
    a["x"] = i["x"].transpose(1, 0, 2)
    a["xT"] = chunks(i["x"].reshape(T, D).T)
    for layer, stage in (("L1", 5), ("L2", 8), ("L3", 11)):
        f = f"{layer}_ffn_"
        a[f + "W_base"] = chunks(i[f + "W_base"].T)
        low = i[f + "A"].reshape(P, D).T
        if layer == "L1":
            parts = [low, i[f + "W_gate"].T, i[f + "W_thr"].T]
            a[f + "b_thr"] = i[f + "b_thr"]
        else:
            parts = [low, i[f + "W_router"].T]
        a[f + "route"] = chunks(np.concatenate(parts, axis=1))
        a[f + "B"] = i[f + "B"].transpose(0, 2, 1).reshape(P, D)
        a[f + "b_base"] = i[f + "b_base"]
    for layer, names, flip in (("L0", ("Wq", "Wk", "Wv", "Wd"), True), ("L1", ("wq", "wk", "wv", "wo"), False)):
        for out, name in zip(("wq", "wk", "wv"), names):
            w = i[f"{layer}_xattn_{name}"]
            w = w.T if flip else w
            a[f"{layer}_x{out}"] = w.reshape(KC, P, 8, -1).transpose(2, 1, 0, 3)
        w = i[f"{layer}_xattn_{names[3]}"]
        w = w.T if flip else w
        a[f"{layer}_xwo"] = w.reshape(8, 4, P, D).transpose(0, 2, 1, 3)
    order = np.array([(4 * j + t) * 16 + d for t in range(4) for j in range(8) for d in range(16)])
    a["L1_attn_Wq"] = chunks(i["L1_attn_Wq"][:, order])
    for n in ("Wk", "Wv", "Wo"):
        a[f"L1_attn_{n}"] = chunks(i[f"L1_attn_{n}"])
    for n in ("Wq", "Wk", "Wv", "Wo"):
        a[f"L2_attn_{n}"] = chunks(i[f"L2_attn_{n}"].T)
    a["L2_attn_bq"], a["L2_attn_bk"] = (i[f"L2_attn_{n}"].reshape(4, P).T for n in ("bq", "bk"))
    a["L2_attn_bv"], a["L2_attn_bo"] = i["L2_attn_bv"], i["L2_attn_bo"]
    a["L3_attn_Wqkv"], a["L3_attn_Wo"] = chunks(i["L3_attn_Wqkv"]), i["L3_attn_Wo"]
    a["L3_attn_bqk"] = i["L3_attn_bqkv"][0:2 * P].reshape(2, P).T
    a["L3_attn_bv"], a["L3_attn_bo"] = i["L3_attn_bqkv"][2 * P:], i["L3_attn_bo"]
    for n in "qkv":
        a[f"L0_attn_w{n}"] = chunks(i[f"L0_attn_w{n}"].T)
    a["L0_attn_bq"], a["L0_attn_bk"] = (i[f"L0_attn_{n}"].reshape(4, P).T for n in ("bq", "bk"))
    a["L0_attn_bv"] = i["L0_attn_bv"]
    same = (np.arange(64)[None, None, :] // 16 == np.arange(4)[:, None, None]) & np.ones((4, 32, 64), bool)
    a["mask_rows"] = np.stack([same, np.where(same, 0, NEG)]).astype(np.float32)
    f = "L0_ffn_"
    a[f + "Wq"], a[f + "Wr"], a[f + "WrT"] = i[f + "Wq"], i[f + "Wr"], i[f + "Wr"].T
    a[f + "aux_keysT"], a[f + "aux_valuesT"] = i[f + "aux_keys"].T, chunks(i[f + "aux_values"].T)
    a[f + "WvdT"], a[f + "WvuT"], a[f + "Wu1T"] = chunks(i[f + "Wvd"].T), i[f + "Wvu"].T, chunks(i[f + "Wu1"].T)
    for n in ("bu1", "Wu2", "bu2", "gate_w1", "gate_bias", "log_rel"):
        a[f + n] = i[f + n].reshape(-1)
    for n in ("q", "k", "v"):
        a[f"L3_xw{n}"] = i[f"L3_xattn_W{n}"].T.reshape(KC, P, 4, -1).transpose(2, 1, 0, 3)
    a["L3_xwo"] = i["L3_xattn_Wo"].T.reshape(4, 4, 96, D).transpose(0, 2, 1, 3)
    a["ctx"] = i["ctx_4096"].transpose(1, 0, 2)
    a["ctxT"] = chunks(i["ctx_4096"].reshape(T, D).T)
    a["mask"] = i["mask_BxSxS2_ff0"].transpose(1, 0, 2)
    return {k: np.ascontiguousarray(v) for k, v in a.items()}


def kernel(**inputs):
    import concourse.bacc as bacc
    from concourse.bass_utils import run_bass_kernel_spmd

    arrays = layout({k: np.asarray(v) for k, v in inputs.items()})
    known = {}
    for _ in range(2):
        nc = bacc.Bacc("TRN2", target_bir_lowering=False, num_devices=1)
        dram = {k: nc.dram_tensor(f"in_{k}", v.shape, mybir.dt.from_np(v.dtype), kind="ExternalInput").ap() for k, v in arrays.items()}
        out = nc.dram_tensor("out_x", (P, B, D), F32, kind="ExternalOutput").ap()
        known = build(nc, dram, out, known)
    result = run_bass_kernel_spmd(nc, [{f"in_{k}": v for k, v in arrays.items()}], core_ids=[0])
    return result.results[0]["out_x"].transpose(1, 0, 2)
```

```python
from contextlib import ExitStack

import numpy as np
import concourse.bass as bass
from concourse import mybir

STAGES = (0, 1, 2, 3, 4, 5, 6, 7, 8, 9, 10, 11)

F32 = mybir.dt.float32
ALU = mybir.AluOpType
ACT = mybir.ActivationFunctionType
AX = mybir.AxisListType

P = 128
B = 8
D = 512
KC = D // P
T = B * P
HALF = T // 2
NEG = -1e30
EPS = 1e-5
HEAD_START = 128


class Mark:

    def __init__(self, counter, value, loop):
        self.counter, self.value, self.loop = counter, value, loop

    def at(self, i):
        return self.value + i * self.loop.per(self.counter)


class Loop:
    def __init__(self, n, per):
        self.n, self.counts, self.i = n, per, None

    def per(self, counter):
        return self.counts.get(counter.name, 0) * counter.step


class Counter:

    def __init__(self, core, name, step=1, starter=None):
        self.core, self.name, self.step = core, name, step
        self.sem = core.stack.enter_context(core.nc.semaphore(name))
        self.count = 0
        core.counters.append(self)
        if starter is not None:
            starter.sem_inc(self.sem, HEAD_START)
            self.count = HEAD_START

    def add(self, instruction):
        instruction.then_inc(self.sem, self.step)
        self.count += self.step
        return Mark(self, self.count, self.core.loop)

    def first(self):
        return Mark(self, self.count, self.core.loop)

    def now(self):
        return Mark(self, self.count, self.core.loop)


class Core:

    def __init__(self, nc, stack, known):
        self.nc, self.stack, self.loop, self.counters = nc, stack, None, []
        self.known, self.noted, self.loops = known, {}, 0
        self.carrier = stack.enter_context(nc.semaphore("wait_carrier"))
        self.pe = Counter(self, "pe_done", starter=nc.tensor)
        self.act = Counter(self, "act_done", starter=nc.scalar)
        self.dve = Counter(self, "dve_done", starter=nc.vector)
        self.pool = Counter(self, "pool_done", starter=nc.gpsimd)

    def wait(self, engine, *marks, apart=False):
        for mark in marks:
            if mark is None:
                continue
            value = mark.value
            if mark.loop is not None:
                inside = mark.loop is self.loop
                value = mark.at(self.loop.i if inside else mark.loop.n - 1)
            if isinstance(value, int) and value == 0:
                continue
            engine.wait_ge(mark.counter.sem, value)
        if apart and self.loop is not None:
            engine.sem_inc(self.carrier)

    def carry(self, engine):
        engine.sem_inc(self.carrier)

    def wait_at(self, engine, i, *marks):
        for mark in marks:
            engine.wait_ge(mark.counter.sem, mark.at(i))
        engine.sem_inc(self.carrier)

    def done(self):
        return [c.now() for c in (self.pe, self.act, self.dve, self.pool)]

    def note(self, name, mark):
        self.noted[self.loop.number, name] = (mark.counter.name, mark.value - self.loop.starts[mark.counter.name])

    def last(self, *names):
        marks = []
        for name in names:
            if (self.loop.number, name) in self.known:
                counter, offset = self.known[self.loop.number, name]
                counter = next(c for c in self.counters if c.name == counter)
                marks.append(Mark(counter, self.loop.starts[counter.name] + offset - self.loop.per(counter), self.loop))
        return marks

    def repeat(self, n, streams=None):
        return _Repeat(self, n, streams or {})


class _Repeat:
    def __init__(self, core, n, streams):
        self.core, self.streams = core, streams
        number = core.loops = core.loops + 1
        self.loop = Loop(n, dict(core.known.get(number, {})))
        self.loop.number = number

    def __enter__(self):
        core, E = self.core, mybir.EngineType
        self.fori = core.nc.Fori(0, self.loop.n, engines=(E.Pool, E.Activation, E.PE, E.DVE))
        self.loop.i = self.fori.__enter__()
        self.loop.starts = {c.name: c.count for c in core.counters}
        core.loop = self.loop
        for c, n in self.streams.items():
            self.loop.counts[c.name] = n
        return self.loop.i

    def __exit__(self, *error):
        core, loop = self.core, self.loop
        if error[0] is None:
            streamed = [c.name for c in self.streams]
            counts = {c.name: (c.count - loop.starts[c.name]) // c.step for c in core.counters if c.name not in streamed}
            core.noted[loop.number] = counts
            if core.known:
                assert counts == {k: v for k, v in loop.counts.items() if k not in streamed}
            for c in core.counters:
                c.count += (loop.n - 1) * loop.per(c)
        core.loop = None
        return self.fori.__exit__(*error)


def build(nc, dram, out, known):
    with ExitStack() as stack:
        core = Core(nc, stack, known)
        pe, act, dve, pool = core.pe, core.act, core.dve, core.pool
        PE, AC, DV, PO, SP = nc.tensor, nc.scalar, nc.vector, nc.gpsimd, nc.sync
        wait = core.wait

        def sbuf(name, shape, scope=stack):
            return scope.enter_context(nc.sbuf_tensor(name, shape, F32))

        x = sbuf("x", [P, B, D])
        xT = sbuf("xT", [P, KC, T])
        ctxT = sbuf("ctxT", [P, KC, T])
        xTb = sbuf("xTb", [P, KC, P])
        arenas = [sbuf(f"weights{n}", [P, (9240, 5632)[n]]) for n in range(2)]
        psum = [stack.enter_context(nc.psum_tensor(f"bank{n}", [P, 512], F32)) for n in range(8)]
        const = sbuf("const", [P, dram["const"].shape[1]])
        ident = const[:, 0:P]
        causal = const[:, P:2 * P]
        block_diagonal = const[:, 2 * P:3 * P]
        cos128, sin128 = const[:, 3 * P:4 * P], const[:, 4 * P:5 * P]
        cos16, sin16 = const[:, 5 * P:6 * P], const[:, 6 * P:7 * P]
        turn16 = const[:, 7 * P:8 * P]
        parity = const[:, 8 * P:8 * P + 2]
        ones = const[:, 8 * P + 2:8 * P + 4]
        eps_row, minus_half_row = const[:, 8 * P + 16:8 * P + 24], const[:, 8 * P + 24:8 * P + 32]

        loaded_x = Counter(core, "loaded_x", 16)
        loaded_ctx = Counter(core, "loaded_ctx", 16)
        stored = Counter(core, "stored", 16)
        loaded_w = [Counter(core, f"loaded_weights{n}", 16) for n in range(2)]

        loaded_x.add(SP.dma_start(const[:, :], dram["const"]))
        x_here = loaded_x.add(SP.dma_start(xT[:, :, :], dram["xT"]))
        loaded_rows = Counter(core, "loaded_rows", 16)
        ctx_here = None

        def load_context():
            nonlocal ctx_here
            if ctx_here is None:
                ctx_here = loaded_ctx.add(SP.dma_start(ctxT[:, :, :], dram["ctxT"]))

        class Weights:

            def __init__(self, stage, free):
                self.arena, self.counter, self.at = arenas[stage % 2], loaded_w[stage % 2], 0
                wait(SP, *free)

            def load(self, name, *, broadcast=False):
                a = dram[name]
                rows, cols = (P, a.shape[0]) if broadcast else (a.shape[0], int(np.prod(a.shape[1:])))
                view = self.arena[0:rows, self.at:self.at + cols]
                self.at += cols
                assert self.at <= self.arena.shape[1], name
                if broadcast:
                    a = a.rearrange("(o n) -> o n", o=1).broadcast_to((P, cols))
                elif len(a.shape) == 3:
                    view = view.rearrange("p (k n) -> p k n", k=a.shape[1])
                self.counter.add(SP.dma_start(view, a))
                return view

            def here(self):
                return self.counter.now()

        def wide(t, b, width=P):
            return t[:, :, bass.ds(b * width, width)]

        def load_experts(stage, free):
            w = Weights(stage, free)
            layer = {5: "L1", 8: "L2", 11: "L3"}[stage]
            parts = {
                "base": w.load(f"{layer}_ffn_W_base"),
                "route": w.load(f"{layer}_ffn_route"),
                "up": w.load(f"{layer}_ffn_B"),
                "bias": w.load(f"{layer}_ffn_b_base", broadcast=True),
            }
            if stage == 5:
                parts["b_thr"] = w.load("L1_ffn_b_thr", broadcast=True)
            return parts, w

        E_, R_ = 8, 16

        def experts(stage, parts, w):
            with ExitStack() as scope:
                xTb2 = [xTb, sbuf(f"xTb_{stage}", [P, KC, P], scope)]
                hw = [sbuf(f"hw{c}_{stage}", [P, E_, R_], scope) for c in range(2)]
                hwT = [sbuf(f"hwT{c}_{stage}", [P, P], scope) for c in range(2)]
                logits, probs, sel, wt, top8, pair = (sbuf(f"{n}_{stage}", [P, 2, E_], scope) for n in ("logits", "probs", "sel", "wt", "top8", "pair"))
                top, total, inverse, thr, zero = (sbuf(f"{n}_{stage}", [P, 2], scope) for n in ("top", "total", "inverse", "thr", "zero"))

                def every(t):
                    return spread(t[:, :], E_, at=2)

                def step(instruction):
                    m = dve.add(instruction)
                    wait(DV, m)
                    return m

                for eng in (PE, DV, PO):
                    wait(eng, w.here())
                for b in range(B):
                    pool.add(PO.tensor_tensor(x[:, b, :], x[:, b, :], parts["bias"], ALU.add))
                if stage != 5:
                    dve.add(DV.memset(pair[:, :, :], 3.0e38))
                for eng in engines:
                    wait(eng, *core.done())
                nr = parts["route"].shape[2]
                with core.repeat(B // 2) as i:
                    staged = []
                    for c in range(2):
                        wait(AC, *core.last(f"based{c}"), apart=True)
                        staged.append(act.add(AC.activation(xTb2[c][:, :, :], wide(xT, 2 * i + c), ACT.Copy)))
                    for c in range(2):
                        wait(PE, staged[c], *core.last(f"weighted{c}"))
                        for k in range(KC):
                            mm = PE.matmul(psum[c][:, 0:nr], xTb2[c][:, k, :], parts["route"][:, k, :], start=k == 0, stop=k == KC - 1)
                        routed = pe.add(mm)
                    for c in range(2):
                        wait(PE, *core.last(f"summed{c}"))
                        for k in range(KC):
                            mm = PE.matmul(psum[2 + c][:, :], xTb2[c][:, k, :], parts["base"][:, k, :], start=k == 0, stop=False)
                        core.note(f"based{c}", pe.add(mm))
                    wait(DV, routed)
                    for c in range(2):
                        m = dve.add(DV.tensor_copy(logits[:, c, :], psum[c][:, P:P + E_]))
                        if stage == 5:
                            m = dve.add(DV.tensor_scalar(thr[:, c:c + 1], psum[c][:, P + E_:P + E_ + 1], parts["b_thr"][:, 0:1], -80.0, ALU.add, ALU.max))
                    wait(DV, m)
                    m = step(DV.tensor_reduce(top[:, :], logits[:, :, :], AX.X, ALU.max))
                    if stage != 5:
                        core.carry(DV)
                        largest = [dve.add(DV.max(top8[:, c, :], logits[:, c, :])) for c in range(2)]
                        wait(DV, largest[-1])
                        step(DV.tensor_copy(pair[:, :, 0:2], top8[:, :, 0:2]))
                        core.carry(DV)
                        for c in range(2):
                            m = dve.add(DV.match_replace(sel[:, c, :], pair[:, c, :], logits[:, c, :], NEG))
                        wait(DV, m)
                        step(DV.tensor_tensor(sel[:, :, :], sel[:, :, :], logits[:, :, :], ALU.not_equal))
                    m = step(DV.tensor_tensor(logits[:, :, :], logits[:, :, :], every(top), ALU.subtract))
                    wait(AC, m)
                    m = act.add(AC.activation(probs[:, :, :], logits[:, :, :], ACT.Exp))
                    if stage == 5:
                        m = act.add(AC.activation(thr[:, :], thr[:, :], ACT.Exp, scale=-1.0))
                        wait(DV, m)
                        step(DV.tensor_reduce(total[:, :], probs[:, :, :], AX.X, ALU.add))
                        step(DV.reciprocal(inverse[:, :], total[:, :]))
                        step(DV.tensor_tensor(probs[:, :, :], probs[:, :, :], every(inverse), ALU.mult))
                        step(DV.tensor_scalar(thr[:, :], thr[:, :], 1.0, None, ALU.add))
                        step(DV.reciprocal(thr[:, :], thr[:, :]))
                        step(DV.tensor_scalar(thr[:, :], thr[:, :], 1.0 / 8.0, None, ALU.mult))
                        step(DV.tensor_tensor(wt[:, :, :], probs[:, :, :], every(thr), ALU.subtract))
                        step(DV.tensor_scalar(wt[:, :, :], wt[:, :, :], 0.0, None, ALU.max))
                        step(DV.tensor_reduce(total[:, :], wt[:, :, :], AX.X, ALU.add))
                        step(DV.tensor_scalar(zero[:, :], total[:, :], 0.0, None, ALU.is_equal))
                        step(DV.tensor_tensor(total[:, :], total[:, :], zero[:, :], ALU.add))
                    else:
                        wait(DV, m)
                        step(DV.tensor_tensor(wt[:, :, :], probs[:, :, :], sel[:, :, :], ALU.mult))
                        step(DV.tensor_reduce(total[:, :], wt[:, :, :], AX.X, ALU.add))
                    step(DV.reciprocal(inverse[:, :], total[:, :]))
                    step(DV.tensor_scalar(inverse[:, :], inverse[:, :], 2.0, None, ALU.mult))
                    step(DV.tensor_tensor(wt[:, :, :], wt[:, :, :], every(inverse), ALU.mult))
                    turned = []
                    for c in range(2):
                        wait(DV, *core.last(f"hw_turned{c}"))
                        m = dve.add(DV.tensor_tensor(hw[c][:, :, :], psum[c][:, 0:P].rearrange("p (e r) -> p e r", e=E_),
                                                     spread(wt[:, c, :], R_, at=2), ALU.mult))
                        core.note(f"weighted{c}", m)
                        wait(PE, m, *core.last(f"hwT_copied{c}"))
                        turned.append(pe.add(PE.transpose(psum[4 + c][:, 0:P], hw[c][:, :, :].rearrange("p e r -> p (e r)"), ident)))
                        core.note(f"hw_turned{c}", turned[c])
                    for c in range(2):
                        wait(AC, turned[c], *core.last(f"raised{c}"))
                        m = act.add(AC.activation(hwT[c][:, :], psum[4 + c][:, 0:P], ACT.Copy))
                        core.note(f"hwT_copied{c}", m)
                        wait(PE, m)
                        m = pe.add(PE.matmul(psum[2 + c][:, :], hwT[c][:, :], parts["up"], start=False, stop=True))
                        core.note(f"raised{c}", m)
                        wait(DV, m)
                        row = x[:, bass.ds(2 * i + c, 1), :].rearrange("p o d -> p (o d)")
                        core.note(f"summed{c}", dve.add(DV.tensor_tensor(row, psum[2 + c][:, :], row, ALU.add)))
                for eng in engines:
                    wait(eng, *core.done())
            finish_all()

        engines = (PE, AC, DV, PO)

        def spread(t, n, at=1):
            if at == 1:
                return t.rearrange("p (o m) -> p o m", o=1).broadcast_to((t.shape[0], n, t.shape[1]))
            return t.rearrange("p (m o) -> p m o", o=1).broadcast_to((t.shape[0], t.shape[1], n))

        def four(t):
            return t.rearrange("p (a n) -> p a n", a=4)

        def finish_all():
            with ExitStack() as scope:
                st = sbuf("norm_stats%d" % core.pe.count, [P, B, 6], scope)
                mv = sbuf("norm_mv%d" % core.pe.count, [P, B, 2], scope)
                rs = sbuf("norm_rs%d" % core.pe.count, [P, 2, B], scope)
                for b in range(B):
                    m = dve.add(DV.bn_stats(st[:, b, :], x[:, b, :]))
                wait(DV, m)
                for b in range(B):
                    m = dve.add(DV.bn_aggr(mv[:, b, :], st[:, b, :]))
                wait(PO, m)
                m = pool.add(PO.tensor_tensor(rs[:, 0, :], mv[:, :, 1], eps_row, ALU.add))
                wait(PO, m)
                m = pool.add(PO.tensor_tensor(rs[:, 1, :], rs[:, 0, :], minus_half_row, ALU.pow))
                wait(DV, m)
                copied = []
                for b in range(B):
                    normed = dve.add(DV.tensor_scalar(x[:, b, :], x[:, b, :], mv[:, b, 0:1], rs[:, 1, b:b + 1],
                                                      ALU.subtract, ALU.mult))
                    wait(PE, normed, copied[b - 2] if b >= 2 else None)
                    bank = psum[b % 2]
                    for k in range(KC):
                        mm = PE.transpose(bank[:, k * P:(k + 1) * P], x[:, b, k * P:(k + 1) * P], ident)
                    turned = pe.add(mm)
                    wait(AC, turned)
                    copied.append(act.add(AC.activation(xT[:, :, b * P:(b + 1) * P], four(bank[:, :]), ACT.Copy)))

        class Softmax:

            def __init__(self, scope, tag, width=P, normalise=True, depth=2, masked=True):
                self.width, self.normalise, self.depth = width, normalise, depth
                self.S = [sbuf(f"S{n}_{tag}", [P, 4, width], scope) if masked else None for n in range(depth)]
                self.E = [sbuf(f"E{n}_{tag}", [P, 4, width], scope) for n in range(depth)]
                self.small = [sbuf(f"sm{n}_{tag}", [P, 3, 4], scope) for n in range(depth)]
                self.restart()

            def restart(self):
                before = core.last if core.loop else lambda name: []
                self.used = [before(f"used{n}") for n in range(self.depth)]
                self.read = [before(f"read{n}") for n in range(self.depth)]

            def note(self):
                for n in range(self.depth):
                    core.note(f"used{n}", self.used[n][0])
                    core.note(f"read{n}", self.read[n][0])

            def run(self, u, scored, tiles, scale, mask):
                n = u % self.depth
                s, e, small, slot = self.S[n], self.E[n], self.small[n], n
                top, total, inverse = small[:, 0, :], small[:, 1, :], small[:, 2, :]
                wait(DV, scored, *self.read[slot])
                at = 0
                if mask is not None:
                    for t in tiles:
                        n = t.shape[1]
                        m = dve.add(DV.scalar_tensor_tensor(s[:, at:at + n, :], t, float(scale), mask[:, at:at + n, :], ALU.mult, ALU.add))
                        at += n
                    freed = m
                    wait(DV, m)
                    m = dve.add(DV.tensor_reduce(top, s[:, :, :], AX.X, ALU.max, negate=True))
                    source = [s[:, j, :] for j in range(4)]
                    scale = 1.0
                else:
                    source = []
                    for t in tiles:
                        n = t.shape[1]
                        m = dve.add(DV.tensor_reduce(top[:, at:at + n], t, AX.X, ALU.max, negate=True))
                        source += [t[:, j, :] for j in range(n)]
                        at += n
                    if scale != 1.0:
                        wait(DV, m)
                        m = dve.add(DV.tensor_scalar(inverse, top, float(scale), None, ALU.mult))
                        top = inverse
                wait(AC, m, *self.used[slot])
                for j in range(4):
                    if self.normalise:
                        m = act.add(AC.activation(e[:, j, :], source[j], ACT.Exp, bias=top[:, j:j + 1], scale=float(scale), accum_out=total[:, j:j + 1]))
                    else:
                        m = act.add(AC.activation(e[:, j, :], source[j], ACT.Exp, bias=top[:, j:j + 1], scale=float(scale)))
                self.read[slot] = [m]
                if mask is None:
                    freed = m
                if self.normalise:
                    wait(DV, m)
                    m = dve.add(DV.reciprocal(inverse, total))
                    wait(DV, m)
                    m = dve.add(DV.tensor_tensor(e[:, :, :], e[:, :, :], spread(inverse, self.width, at=2), ALU.mult))
                return m, freed

        G8 = 8

        def load_cross(stage, free):
            layer = {1: "L0", 4: "L1"}[stage]
            w = Weights(stage, free)
            load_context()
            qkv, o = Counter(core, f"stream_qkv{stage}", 16), Counter(core, f"stream_out{stage}", 16)
            views = {}
            for name, shape in (("wq", (KC, D)), ("wk", (KC, P)), ("wv", (KC, P)), ("wo", (4, D))):
                n = shape[0] * shape[1]
                views[name] = w.arena[:, w.at:w.at + n].rearrange("p (k n) -> p k n", k=shape[0])
                w.at += n
                (o if name == "wo" else qkv).add(SP.dma_start(views[name], dram[f"{layer}_x{name}"][0]))
            if stage == 4:
                views["mask"] = w.load("mask")
            return layer, views, w, qkv, o

        def cross(stage, layer, views, w, qkv, o):
            wq, wk, wv, wo = (views[n] for n in ("wq", "wk", "wv", "wo"))
            with ExitStack() as scope:
                QT = sbuf(f"QT{stage}", [P, 4, T], scope)
                KT = sbuf(f"KT{stage}", [P, T], scope)
                V = sbuf(f"V{stage}", [P, B, P], scope)
                turned = [sbuf(f"turned{n}_{stage}", [P, 4, P], scope) for n in range(2)]
                soft = Softmax(scope, f"x{stage}", depth=3)
                PT = [sbuf(f"PT{n}_{stage}", [P, 4, P], scope) for n in range(2)]
                OT = [sbuf(f"OT{n}_{stage}", [P, 4, P], scope) for n in range(2)]
                for eng in engines:
                    wait(eng, ctx_here, *([w.here()] if stage == 4 else []))
                with core.repeat(G8, streams={qkv: 3, o: 1}) as g:
                    wait(PE, qkv.first(), *core.last("bank0_free", "bank1_free"))
                    wait(DV, *core.last("scored"))
                    wait(AC, *core.last("mixed"))
                    soft.restart()
                    freed, added, jobs = [None, None], [None, None], []
                    for dst, source, weight in [(KT[:, :], ctxT, wk[:, :, :])] + [(QT[:, h, :], xT, wq[:, :, h * P:(h + 1) * P]) for h in range(4)]:
                        for half in range(2):
                            jobs.append((dst[:, half * HALF:(half + 1) * HALF], source[:, :, half * HALF:(half + 1) * HALF], weight))
                    for n, (dst, source, weight) in enumerate(jobs):
                        bank, t = psum[n % 2], turned[n % 2]
                        wait(PE, freed[n % 2])
                        for k in range(KC):
                            mm = PE.matmul(bank[:, :], weight[:, k, :], source[:, k, :], start=k == 0, stop=k == KC - 1)
                        m = pe.add(mm)
                        wait(DV, m, added[n % 2])
                        lo, hi = slice(0, P // 2), slice(P // 2, P)
                        dve.add(DV.tensor_tensor(t[hi, :, :], four(bank[lo, :]), spread(sin128[lo, :], 4), ALU.mult))
                        dve.add(DV.tensor_tensor(t[lo, :, :], four(bank[hi, :]), spread(sin128[hi, :], 4), ALU.mult))
                        freed[n % 2] = dve.add(DV.tensor_tensor(four(dst), four(bank[:, :]), spread(cos128, 4), ALU.mult))
                        wait(PO, freed[n % 2])
                        added[n % 2] = rotated = pool.add(PO.tensor_tensor(four(dst), four(dst), t[:, :, :], ALU.add))
                    for half in range(2):
                        bank = psum[half]
                        wait(PE, freed[half])
                        for b in range(4 * half, 4 * half + 4):
                            for k in range(KC):
                                mm = PE.matmul(bank[:, (b % 4) * P:(b % 4 + 1) * P], ctxT[:, k, b * P:(b + 1) * P], wv[:, k, :], start=k == 0, stop=k == KC - 1)
                        m = projected = pe.add(mm)
                        wait(AC, m)
                        valued = act.add(AC.activation(V[:, 4 * half:4 * half + 4, :], four(bank[:, :]), ACT.Copy))
                    wait(PE, rotated, valued)
                    for half in range(2):
                        core.note(f"bank{half}_free", valued)
                    scored_free, soft_done = [core.last(f"score_free{n}") for n in range(2)], {}
                    pt_free, ot_free = ([core.last(f"{t}_free{n}") for n in range(2)] for t in ("pt", "ot"))
                    bank_free = {n: core.last(f"bank{n}_free") for n in (4, 5, 6, 7)}
                    copied = {}
                    for step in range(B + 3):
                        if 2 <= step < B + 2:
                            b = step - 2
                            bank = psum[4 + b % 2]
                            wait(PE, soft_done[b], *bank_free[4 + b % 2])
                            for h in range(4):
                                mm = PE.transpose(bank[:, h * P:(h + 1) * P], soft.E[b % 3][:, h, :], ident)
                            m = pe.add(mm)
                            soft.used[b % 3] = [m]
                            wait(AC, m, *pt_free[b % 2])
                            pt_copied = act.add(AC.activation(PT[b % 2][:, :, :], four(bank[:, :]), ACT.Copy))
                            bank_free[4 + b % 2] = [pt_copied]
                        if step < B:
                            b = step
                            bank = psum[2 + b % 2]
                            wait(PE, *scored_free[b % 2])
                            for h in range(4):
                                mm = PE.matmul(bank[:, h * P:(h + 1) * P], QT[:, h, b * P:(b + 1) * P], KT[:, b * P:(b + 1) * P], start=True, stop=True)
                            m = pe.add(mm)
                            core.note("scored", m)
                            mask = spread(causal, 4) if stage == 1 else spread(views["mask"][:, b, :], 4)
                            soft_done[b], freed_ = soft.run(b, m, [four(bank[:, :])], P ** -0.5, mask)
                            scored_free[b % 2] = [freed_]
                        if step >= 3:
                            b = step - 3
                            bank = psum[7]
                            if b == 0:
                                wait(PE, o.first())
                            wait(PE, copied[b], *bank_free[7])
                            for h in range(4):
                                mm = PE.matmul(bank[:, :], OT[b % 2][:, h, :], wo[:, h, :], start=h == 0, stop=h == 3)
                            m = pe.add(mm)
                            ot_free[b % 2] = [m]
                            wait(DV, m)
                            bank_free[7] = [dve.add(DV.tensor_tensor(x[:, b, :], bank[:, :], x[:, b, :], ALU.add))]
                        if 2 <= step < B + 2:
                            b = step - 2
                            wait(PE, pt_copied, *bank_free[6])
                            m = pe.add(PE.matmul(psum[6][:, :], V[:, b, :], PT[b % 2][:, :, :], start=True, stop=True))
                            pt_free[b % 2] = [m]
                            core.note("mixed", m)
                            wait(DV, m, *ot_free[b % 2])
                            copied[b] = dve.add(DV.tensor_copy(OT[b % 2][:, :, :], four(psum[6][:, :])))
                            bank_free[6] = [copied[b]]
                    last = ot_free[(B - 1) % 2][0]
                    soft.note()
                    for n in range(2):
                        core.note(f"score_free{n}", scored_free[n][0])
                        core.note(f"pt_free{n}", pt_free[n][0])
                        core.note(f"ot_free{n}", ot_free[n][0])
                    for n in (4, 5, 6, 7):
                        core.note(f"bank{n}_free", bank_free[n][0])
                with SP.Fori(0, G8 - 1) as i:
                    core.wait_at(SP, i, projected)
                    for name in ("wq", "wk", "wv"):
                        SP.dma_start(views[name], dram[f"{layer}_x{name}"][bass.ds(i + 1, 1)].rearrange("o p k n -> (o p) k n")).then_inc(qkv.sem, 16)
                    core.wait_at(SP, i, last)
                    SP.dma_start(wo, dram[f"{layer}_xwo"][bass.ds(i + 1, 1)].rearrange("o p k n -> (o p) k n")).then_inc(o.sem, 16)
                for eng in engines:
                    wait(eng, *core.done())
            finish_all()

        HEADS, HD = 32, 16

        class Small:

            def __init__(self, scope, tag, masked):
                self.soft = Softmax(scope, tag, normalise=False, depth=3, masked=masked)
                self.PT = [sbuf(f"PT{n}_{tag}", [P, 4, P], scope) for n in range(2)]
                self.sums = sbuf(f"sums_{tag}", [P, 2, 16], scope)
                self.OT = sbuf(f"OT_{tag}", [P, 4, P], scope)
                self.restart()

            def restart(self):
                before = core.last if core.loop else lambda name: []
                self.soft.restart()
                self.pt_free = [before(f"pt_free{n}") for n in range(2)]
                self.score_free = [before(f"score_free{n}") for n in range(3)]
                self.t_free = [before(f"t_free{n}") for n in range(2)]
                self.o_free = [before(f"o_free{n}") for n in range(2)]
                self.OT_free, self.seven_free = before("OT_free"), before("seven_free")

            def note(self):
                self.soft.note()
                for name, marks in (("pt_free", self.pt_free), ("score_free", self.score_free), ("t_free", self.t_free), ("o_free", self.o_free)):
                    for n, mark in enumerate(marks):
                        core.note(f"{name}{n}", mark[0])
                core.note("OT_free", self.OT_free[0])
                core.note("seven_free", self.seven_free[0])

            def run(self, quads, mask, scale, before_scores, after_half):
                soft, n, ready = self.soft, len(quads), {}
                self.scored_marks = {}
                pending = []
                for step in range(n + 3 + 4):
                    for item in list(pending):
                        item[1] = item[0].pop(0)(item[1])
                        if not item[0]:
                            pending.remove(item)
                    if 2 <= step < n + 2:
                        u = step - 2
                        bank = psum[2 + u % 2]
                        wait(PE, ready[u], *self.t_free[u % 2])
                        for j in range(4):
                            mm = PE.transpose(bank[:, j * P:(j + 1) * P], soft.E[u % 3][:, j, :], ident)
                        m = pe.add(mm)
                        soft.used[u % 3] = [m]
                        wait(DV if u % 2 else AC, m, *self.pt_free[u % 2])
                        if u % 2:
                            m = dve.add(DV.tensor_copy(self.PT[u % 2][:, :, :], four(bank[:, :])))
                        else:
                            m = act.add(AC.activation(self.PT[u % 2][:, :, :], four(bank[:, :]), ACT.Copy))
                        self.t_free[u % 2] = [m]
                    if step < n:
                        u = step
                        bank = psum[(0, 1, 6)[u % 3]]
                        wait(PE, *self.score_free[u % 3], *(before_scores[u]() if u in before_scores else []))
                        products, _ = quads[u]
                        n_ = 4 * P // len(products)
                        for j, (lhsT, rhs) in enumerate(products):
                            mm = PE.matmul(bank[:, j * n_:(j + 1) * n_], lhsT, rhs, start=True, stop=True)
                        m = self.scored = self.scored_marks[u] = pe.add(mm)
                        ready[u], freed = soft.run(u, m, [four(bank[:, :])], scale, mask)
                        self.score_free[u % 3] = [freed]
                    if 3 <= step < n + 3:
                        u = step - 3
                        half = u // 4
                        wait(PE, *self.t_free[u % 2], *(self.o_free[half % 2] if u % 4 == 0 else []))
                        for j, values in enumerate(quads[u][1]):
                            mm = PE.matmul(psum[4 + half % 2][32 * j:32 * j + 32, u % 4 * P:(u % 4 + 1) * P], values, self.PT[u % 2][:, j, :], start=True, stop=True)
                        m = pe.add(mm)
                        self.pt_free[u % 2] = [m]
                        if u % 4 == 3:
                            def copy(m, half=half):
                                wait(AC, m, *self.OT_free)
                                m = act.add(AC.activation(self.OT[:, :, :], four(psum[4 + half % 2][:, :]), ACT.Copy))
                                self.o_free[half % 2] = [m]
                                return m

                            def turn(m):
                                wait(PE, m, *self.seven_free)
                                for q in range(4):
                                    mm = PE.transpose(psum[7][:, q * P:(q + 1) * P], self.OT[:, q, :], ident)
                                m = pe.add(mm)
                                self.OT_free = [m]
                                return m

                            pending.append([[copy, turn] + after_half[half], m])
                assert not pending

            def divide(self, m, half, O, *free):
                bank = psum[7][:, :].rearrange("p (h e) -> p h e", e=32)
                sums = self.sums[:, half % 2, :]
                wait(DV, m, *free)
                r = dve.add(DV.reciprocal(sums, bank[:, :, 16]))
                wait(DV, r)
                r = dve.add(DV.tensor_tensor(O, bank[:, :, 0:HD], spread(sums, HD, at=2), ALU.mult))
                self.seven_free = [r]
                return r

        def load_rotary16(stage, free):
            w = Weights(stage, free)
            return {n: w.load(f"L1_attn_{n}") for n in ("Wq", "Wk", "Wv", "Wo")}, w

        def load_bias16(stage, free):
            w = Weights(stage, free)
            v = {n: w.load(f"L2_attn_{n}") for n in ("Wq", "Wk", "Wv", "Wo", "bq", "bk")}
            v.update({n: w.load(f"L2_attn_{n}", broadcast=True) for n in ("bv", "bo")})
            return v, w

        def small_attention(stage, v, w):
            rotary = stage == 3
            kt = 1 if rotary else 4
            kv = 8 * kt
            with ExitStack() as scope:
                QT = sbuf(f"QT{stage}", [P, 4, T], scope)
                KT = sbuf(f"KT{stage}", [P, kt, T], scope)
                QTb = [sbuf(f"QTb{c}_{stage}", [P, 4, P], scope) for c in range(2)]
                KTb = [sbuf(f"KTb{c}_{stage}", [P, kt, 2, P], scope) for c in range(2)]
                V = [sbuf(f"V{c}_{stage}", [P, kv, 32], scope) for c in range(2)]
                xTb2 = [xTb, sbuf(f"xTb_{stage}", [P, KC, P], scope)]
                O = [sbuf(f"O{c}_{stage}", [P, HEADS, HD], scope) for c in range(2)]
                inner = ExitStack()
                if rotary:
                    raw = [sbuf(f"raw{n}_{stage}", [P, D], inner) for n in range(2)]
                    turned = [sbuf(f"turned{n}_{stage}", [P, D], inner) for n in range(2)]
                for eng in engines:
                    wait(eng, w.here())
                for c in range(2):
                    zeroed = pool.add(PO.memset(V[c][:, :, :], 0.0))
                wait(PO, zeroed)
                for c in range(2):
                    pool.add(PO.memset(V[c][:, :, HD:HD + 1], 1.0))
                free, freed_raw, added, n = [None, None], [None, None], [None, None], 0
                for dst, weight, bias, tiles in ((QT, v["Wq"], v.get("bq"), 4), (KT, v["Wk"], v.get("bk"), kt)):
                    for t in range(tiles):
                        for half in range(2):
                            cols = slice(half * HALF, (half + 1) * HALF)
                            bank = psum[n % 2]
                            wait(PE, free[n % 2])
                            for k in range(KC):
                                mm = PE.matmul(bank[:, :], weight[:, k, t * P:(t + 1) * P], xT[:, k, cols], start=k == 0, stop=k == KC - 1)
                            m = pe.add(mm)
                            if rotary:
                                wait(AC, m, freed_raw[n % 2])
                                m2 = act.add(AC.activation(raw[n % 2][:, :], bank[:, :], ACT.Copy))
                                wait(DV, m2)
                                wait(PE, m2, free[(n + 1) % 2] if n else None, free[n % 2])
                                freed_raw[n % 2] = m3 = pe.add(PE.matmul(psum[2 + n % 2][:, :], turn16, raw[n % 2][:, :], start=True, stop=True))
                                dve.add(DV.tensor_tensor(four(dst[:, t, cols]), four(bank[:, :]), spread(cos16, 4), ALU.mult))
                                wait(DV, m3, added[n % 2])
                                free[n % 2] = m = dve.add(DV.tensor_tensor(four(turned[n % 2][:, :]), four(psum[2 + n % 2][:, :]), spread(sin16, 4), ALU.mult))
                                wait(PO, m)
                                added[n % 2] = pool.add(PO.tensor_tensor(dst[:, t, cols], dst[:, t, cols], turned[n % 2][:, :], ALU.add))
                            else:
                                wait(DV, m)
                                free[n % 2] = dve.add(DV.tensor_scalar(dst[:, t, cols], bank[:, :], bias[:, t:t + 1], None, ALU.add))
                            n += 1
                inner.close()
                small = Small(scope, f"s{stage}", masked=True)
                if not rotary:
                    for b in range(B):
                        pool.add(PO.tensor_tensor(x[:, b, :], x[:, b, :], v["bo"], ALU.add))
                for eng in engines:
                    wait(eng, *core.done())
                with core.repeat(B // 2) as i:
                    small.restart()
                    staged, quads, before, after, O_free = [], [], {}, {}, [core.last(f"O_free{c}") for c in range(2)]
                    for c in range(2):
                        b = 2 * i + c
                        wait(AC, *core.last(f"scored{c}", f"valued{c}"), apart=True)
                        staged_x = act.add(AC.activation(xTb2[c][:, :, :], wide(xT, b), ACT.Copy))
                        staged_q = act.add(AC.activation(QTb[c][:, :, :], wide(QT, b), ACT.Copy))
                        wait(DV, *core.last(f"scored{c}"), apart=True)
                        for n in range(2):
                            staged_k = dve.add(DV.tensor_scalar(KTb[c][:, :, n, :], wide(KT, b), parity[:, n:n + 1], None, ALU.mult))
                        staged.append((staged_x, staged_q, staged_k))
                        for pair in range(4):
                            rows = slice(32 * pair, 32 * pair + 32)
                            for second in range(2):
                                products, values = [], []
                                for t in (2 * second, 2 * second + 1):
                                    keys = KTb[c][rows, 0 if rotary else t, :, :].rearrange("p o n -> p (o n)")
                                    products.append((QTb[c][rows, t, :], keys))
                                    for par in range(2):
                                        j = 2 * pair + par
                                        values.append(V[c][:, j if rotary else 8 * t + j, :])
                                quads.append((products, values))

                    def value_product(c):
                        nv = kv * HD
                        wait(PE, staged[c][0], *small.seven_free)
                        for k in range(KC):
                            mm = PE.matmul(psum[7][:, 0:nv], xTb2[c][:, k, :], v["Wv"][:, k, :], start=k == 0, stop=k == KC - 1)
                        m = pe.add(mm)
                        core.note(f"valued{c}", m)
                        values = psum[7][:, 0:nv].rearrange("p (h d) -> p h d", d=HD)
                        wait(DV, m, *core.last(f"produced{c}"))
                        if rotary:
                            m = dve.add(DV.tensor_copy(V[c][:, :, 0:HD], values))
                        else:
                            m = dve.add(DV.tensor_tensor(V[c][:, :, 0:HD], values, v["bv"].rearrange("p (h d) -> p h d", d=HD), ALU.add))
                        small.seven_free = [m]
                        return m

                    def divide(c, half):
                        def step(m):
                            core.note(f"produced{c}", m)
                            return small.divide(m, half, O[c][:, 16 * half:16 * half + 16, :], *(O_free[c] if half == 0 else []))
                        return step

                    def turn_heads(c):
                        def step(m):
                            wait(PE, m)
                            heads = O[c][:, :, :].rearrange("p h d -> p (h d)")
                            for k in range(KC):
                                mm = PE.transpose(psum[7][:, k * P:(k + 1) * P], heads[:, k * P:(k + 1) * P], ident)
                            m = pe.add(mm)
                            core.note(f"O_free{c}", m)
                            wait(AC, m, staged[c][0], apart=True)
                            m = act.add(AC.activation(wide(xT, 2 * i + c), four(psum[7][:, :]), ACT.Copy))
                            small.seven_free = [m]
                            return m
                        return step

                    valued = [value_product(0), value_product(1)]
                    for c in range(2):
                        before[8 * c] = lambda c=c: [*staged[c][1:], valued[c]]
                        after[2 * c] = [divide(c, 0)]
                        after[2 * c + 1] = [divide(c, 1), turn_heads(c)]
                    small.run(quads, spread(causal, 4), 0.25, before, after)
                    for c in range(2):
                        core.note(f"scored{c}", small.scored)
                    small.note()
                for eng in engines:
                    wait(eng, *core.done())
                free = [None, None]
                for b in range(B):
                    wait(PE, free[b % 2])
                    for k in range(KC):
                        mm = PE.matmul(psum[b % 2][:, :], xT[:, k, b * P:(b + 1) * P], v["Wo"][:, k, :], start=k == 0, stop=k == KC - 1)
                    m = pe.add(mm)
                    wait(DV, m)
                    free[b % 2] = dve.add(DV.tensor_tensor(x[:, b, :], psum[b % 2][:, :], x[:, b, :], ALU.add))
                for eng in engines:
                    wait(eng, *core.done())
            finish_all()

        def load_feature(stage, free):
            w = Weights(stage, free)
            load_context()
            return w.load("ctx"), w

        def feature_attention(stage, ctx, w):
            scale = float(P) ** -0.5
            with ExitStack() as scope:
                kb = [sbuf(f"kb{c}", [P, D], scope) for c in range(2)]
                vTb = [sbuf(f"vTb{c}", [P, KC, P], scope) for c in range(2)]
                E = [sbuf(f"E_feature{n}", [P, D], scope) for n in range(3)]
                PT = [sbuf(f"PT_feature{c}", [P, KC, D], scope) for c in range(2)]
                small = sbuf("small_feature", [P, 4, 8], scope)
                for eng in engines:
                    wait(eng, w.here(), ctx_here)
                with core.repeat(B // 2) as i:
                    rows, staged, staged_v = [], [], []
                    for c in range(2):
                        b = 2 * i + c
                        rows.append(x[:, bass.ds(b, 1), :].rearrange("p o d -> p (o d)"))
                        wait(AC, *core.last(f"scored{c}"), apart=True)
                        staged.append(act.add(AC.activation(kb[c][:, :], ctx[:, bass.ds(b, 1), :].rearrange("p o d -> p (o d)"), ACT.Copy)))
                        wait(PO, *core.last(f"mixed{c}"), apart=True)
                        staged_v.append(pool.add(PO.tensor_copy(vTb[c][:, :, :], wide(ctxT, b))))
                    score_free = [core.last(f"score_free{n}") for n in range(3)]
                    t_free = [core.last(f"t_free{n}") for n in range(2)]
                    e_free = [core.last(f"e_free{n}") for n in range(3)]
                    exps = {}
                    for step in range(2 * KC + 2):
                        if step >= 2:
                            u = step - 2
                            c, j = divmod(u, KC)
                            bank = psum[4 + u % 2]
                            wait(PE, exps[u], *t_free[u % 2])
                            for k in range(KC):
                                mm = PE.transpose(bank[:, k * P:(k + 1) * P], E[u % 3][:, k * P:(k + 1) * P], ident)
                            m = pe.add(mm)
                            e_free[u % 3] = [m]
                            wait(AC, m, *(core.last(f"mixed{c}") if j == 0 else []))
                            m = act.add(AC.activation(PT[c][:, :, j * P:(j + 1) * P], four(bank[:, :]), ACT.Copy))
                            t_free[u % 2] = [m]
                            if j == KC - 1:
                                wait(PE, m, staged_v[c], *core.last(f"summed{c}"))
                                for k in range(KC):
                                    mm = PE.matmul(psum[6 + c][:, :], vTb[c][:, k, :], PT[c][:, k, :], start=k == 0, stop=k == KC - 1)
                                m = pe.add(mm)
                                core.note(f"mixed{c}", m)
                                wait(DV, m, apart=True)
                                core.note(f"summed{c}", dve.add(DV.tensor_tensor(rows[c], psum[6 + c][:, :], rows[c], ALU.add)))
                        if step < 2 * KC:
                            u = step
                            c, j = divmod(u, KC)
                            bank = psum[u % 3]
                            wait(PE, staged[c], *score_free[u % 3], apart=True)
                            m = pe.add(PE.matmul(bank[:, :], kb[c][:, j * P:(j + 1) * P], rows[c], start=True, stop=True))
                            core.note(f"scored{c}", m)
                            wait(DV, m, *score_free[u % 3])
                            m = dve.add(DV.tensor_reduce(small[:, 0, u:u + 1], bank[:, :], AX.X, ALU.max, negate=True))
                            wait(DV, m)
                            m = dve.add(DV.tensor_scalar(small[:, 1, u:u + 1], small[:, 0, u:u + 1], scale, None, ALU.mult))
                            wait(AC, m, *e_free[u % 3])
                            m = act.add(AC.activation(E[u % 3][:, :], bank[:, :], ACT.Exp, bias=small[:, 1, u:u + 1], scale=scale, accum_out=small[:, 2, u:u + 1]))
                            score_free[u % 3] = [m]
                            wait(DV, m)
                            m = dve.add(DV.reciprocal(small[:, 3, u:u + 1], small[:, 2, u:u + 1]))
                            wait(DV, m)
                            exps[u] = dve.add(DV.tensor_scalar(E[u % 3][:, :], E[u % 3][:, :], small[:, 3, u:u + 1], None, ALU.mult))
                    for n in range(3):
                        core.note(f"score_free{n}", score_free[n][0])
                        core.note(f"e_free{n}", e_free[n][0])
                    for n in range(2):
                        core.note(f"t_free{n}", t_free[n][0])
                for eng in engines:
                    wait(eng, *core.done())
            finish_all()

        def load_single(stage, free):
            w = Weights(stage, free)
            v = {n: w.load(f"L3_attn_{n}") for n in ("Wqkv", "bqk", "Wo")}
            v.update({n: w.load(f"L3_attn_{n}", broadcast=True) for n in ("bv", "bo")})
            return v, w

        def single_head(stage, v, w):
            with ExitStack() as scope:
                QK = sbuf("QK9", [P, 2, T], scope)
                V = sbuf("V9", [P, B, P], scope)
                soft = Softmax(scope, "s9")
                PT = [sbuf(f"PT{n}_9", [P, 4, P], scope) for n in range(2)]
                OT = [sbuf(f"OT{n}_9", [P, 4, P], scope) for n in range(2)]
                for eng in engines:
                    wait(eng, w.here())
                for b in range(B):
                    biased = pool.add(PO.tensor_tensor(x[:, b, :], x[:, b, :], v["bo"], ALU.add))
                free = [None, None]
                for n in range(4):
                    which, half = n // 2, n % 2
                    cols, bank = slice(half * HALF, (half + 1) * HALF), psum[n % 2]
                    wait(PE, free[n % 2])
                    for k in range(KC):
                        mm = PE.matmul(bank[:, :], v["Wqkv"][:, k, which * P:(which + 1) * P], xT[:, k, cols], start=k == 0, stop=k == KC - 1)
                    m = pe.add(mm)
                    wait(DV, m)
                    free[n % 2] = keyed = dve.add(DV.tensor_scalar(QK[:, which, cols], bank[:, :], v["bqk"][:, which:which + 1], None, ALU.add))
                for half in range(2):
                    bank = psum[2 + half]
                    for b in range(4 * half, 4 * half + 4):
                        for k in range(KC):
                            mm = PE.matmul(bank[:, b % 4 * P:(b % 4 + 1) * P], xT[:, k, b * P:(b + 1) * P], v["Wqkv"][:, k, 2 * P:3 * P], start=k == 0, stop=k == KC - 1)
                    m = pe.add(mm)
                    wait(DV, m)
                    valued = dve.add(DV.tensor_tensor(V[:, 4 * half:4 * half + 4, :], four(bank[:, :]), spread(v["bv"], 4), ALU.add))
                wait(PE, keyed)
                soft_done = []
                for u in range(2):
                    bank = psum[4 + u]
                    for j in range(4):
                        cols = slice((4 * u + j) * P, (4 * u + j + 1) * P)
                        mm = PE.matmul(bank[:, j * P:(j + 1) * P], QK[:, 0, cols], QK[:, 1, cols], start=True, stop=True)
                    m = pe.add(mm)
                    soft_done.append(soft.run(u, m, [four(bank[:, :])], float(P) ** -0.5, None)[0])
                y_free = {}
                for u in range(2):
                    bank = psum[6 + u]
                    wait(PE, soft_done[u])
                    for j in range(4):
                        mm = PE.transpose(bank[:, j * P:(j + 1) * P], soft.E[u][:, j, :], ident)
                    m = pe.add(mm)
                    wait(AC, m)
                    m = act.add(AC.activation(PT[u][:, :, :], four(bank[:, :]), ACT.Copy))
                    wait(PE, m, valued)
                    for j in range(4):
                        mm = PE.matmul(bank[:, j * P:(j + 1) * P], V[:, 4 * u + j, :], PT[u][:, j, :], start=True, stop=True)
                    m = pe.add(mm)
                    wait(AC, m)
                    m = act.add(AC.activation(OT[u][:, :, :], four(bank[:, :]), ACT.Copy))
                    wait(PE, m)
                    wait(DV, biased)
                    for j in range(4):
                        b = 4 * u + j
                        wait(PE, y_free.get(b - 2))
                        m = pe.add(PE.matmul(psum[b % 2][:, :], OT[u][:, j, :], v["Wo"], start=True, stop=True))
                        wait(DV, m)
                        y_free[b] = dve.add(DV.tensor_tensor(x[:, b, :], psum[b % 2][:, :], x[:, b, :], ALU.add))
                for eng in engines:
                    wait(eng, *core.done())
            finish_all()

        CH = 64
        UN = CH // 4

        def load_heads(stage, free):
            w = Weights(stage, free)
            v = {n: w.load(f"L0_attn_{n}") for n in ("wq", "wk", "wv", "bq", "bk")}
            v["bv"] = w.load("L0_attn_bv", broadcast=True)
            return v, w

        def between_heads(stage, v, w):
            scratch = {n: nc.dram_tensor(f"scratch_{n}", (T * D,), F32, kind="Internal").ap() for n in "qkvo"}
            stores = [Counter(core, f"scratch_stored{n}", 16) for n in range(4)]
            with ExitStack() as scope:
                QK = [sbuf(f"QK{n}_0", [P, T], scope) for n in range(2)]
                Vr = [sbuf(f"Vr{n}_0", [P, D], scope) for n in range(2)]
                for eng in engines:
                    wait(eng, w.here())
                free, stored_, n = [None, None], [None] * 4, 0
                for which, (weight, bias) in enumerate(((v["wq"], v["bq"]), (v["wk"], v["bk"]))):
                    view = scratch["qk"[which]].rearrange("(m p t) -> m p t", p=P, t=T)
                    for t in range(4):
                        buffer = QK[t % 2]
                        for half in range(2):
                            bank, cols = psum[n % 2], slice(half * HALF, (half + 1) * HALF)
                            wait(PE, free[n % 2])
                            for k in range(KC):
                                mm = PE.matmul(bank[:, :], weight[:, k, t * P:(t + 1) * P], xT[:, k, cols], start=k == 0, stop=k == KC - 1)
                            m = pe.add(mm)
                            wait(DV, m, stored_[t % 2])
                            m = free[n % 2] = dve.add(DV.tensor_scalar(buffer[:, cols], bank[:, :], bias[:, t:t + 1], 1.0 if which else 0.25, ALU.add, ALU.mult))
                            n += 1
                        wait(SP, m)
                        stored_[t % 2] = stores[t % 2].add(SP.dma_start(view[t], buffer[:, :]))
                view = scratch["v"].rearrange("(n u q d) -> n q u d", u=UN, q=4, d=D)
                for b in range(B):
                    bank = psum[n % 2]
                    wait(PE, free[n % 2])
                    for k in range(KC):
                        mm = PE.matmul(bank[:, :], xT[:, k, b * P:(b + 1) * P], v["wv"][:, k, :], start=k == 0, stop=k == KC - 1)
                    m = pe.add(mm)
                    wait(DV, m, stored_[2 + b % 2])
                    m = free[n % 2] = dve.add(DV.tensor_tensor(Vr[b % 2][:, :], bank[:, :], v["bv"], ALU.add))
                    n += 1
                    wait(SP, m)
                    for c in range(2):
                        stored_[2 + b % 2] = stores[2 + b % 2].add(SP.dma_start(view[2 * b + c], Vr[b % 2][c * CH:(c + 1) * CH, :]))
                for eng in engines:
                    wait(eng, *core.done())
            with ExitStack() as scope:
                q16 = [sbuf(f"q16_{c}", [HD + 4, HEADS, CH], scope) for c in range(2)]
                k16 = [sbuf(f"k16_{c}", [HD + 4, HEADS, CH], scope) for c in range(2)]
                V32 = [sbuf(f"V32_{c}", [P, UN, 32], scope) for c in range(2)]
                O = [sbuf(f"O0_{c}", [P, UN, HD], scope) for c in range(2)]
                small = Small(scope, "s0", masked=False)
                qk_in = [Counter(core, f"stream_qk{c}", 16) for c in range(2)]
                v_in = [Counter(core, f"stream_v{c}", 16) for c in range(2)]
                rows_in = Counter(core, "stream_mask_rows", 16)
                o_out = [Counter(core, f"o_stored{c}", 16, starter=AC) for c in range(2)]
                view = {n: scratch[n].rearrange("(h d t) -> d h t", d=HD, t=T) for n in "qk"}
                view["v"] = scratch["v"].rearrange("(n u p d) -> n p u d", u=UN, p=P, d=HD)
                view["o"] = scratch["o"].rearrange("(n q u h d) -> n q h u d", q=4, u=UN, h=HEADS, d=HD)
                wait(SP, *core.done())
                wait(SP, *stored_)
                for c in range(2):
                    zeroed = pool.add(PO.memset(V32[c][:, :, :], 0.0))
                wait(PO, zeroed)
                for c in range(2):
                    rows_in.add(SP.dma_start(q16[c][HD:HD + 4, :, :], dram["mask_rows"][0]))
                    rows_in.add(SP.dma_start(k16[c][HD:HD + 4, :, :], dram["mask_rows"][1]))
                    ones_set = pool.add(PO.memset(V32[c][:, :, HD:HD + 1], 1.0))

                def load_qk(c, i):
                    for n, buffer in (("q", q16[c]), ("k", k16[c])):
                        yield SP.dma_start(buffer[0:HD, :, :], view[n][:, :, bass.ds(i * P + c * CH, CH)])

                def load_v(c, i):
                    return SP.dma_start(V32[c][:, :, 0:HD], view["v"][bass.ds(2 * i + c, 1)].rearrange("o p u d -> (o p) u d"))

                wait(SP, ones_set)
                for c in range(2):
                    for d in load_qk(c, 0):
                        qk_in[c].add(d)
                    v_in[c].add(load_v(c, 0))
                wait(PE, rows_in.now())
                with core.repeat(B, streams={qk_in[0]: 2, qk_in[1]: 2, v_in[0]: 1, v_in[1]: 1}) as b:
                    stored_before = [o.now() for o in o_out]
                    small.restart()
                    scored, summed, quads, before, after = [], [], [], {}, {}
                    for c in range(2):
                        q = q16[c][:, :, :].rearrange("d h (q u) -> d u (h q)", u=UN)
                        k = k16[c][:, :, :].rearrange("d h (q u) -> d u q h", u=UN)
                        quads += [([(q[:, n, :], k[:, n, :, :]) for n in range(4 * u, 4 * u + 4)],
                                   [V32[c][:, n, :] for n in range(4 * u, 4 * u + 4)]) for u in range(4)]

                        def end(m, c=c):
                            summed.append(m)
                            m = small.divide(m, c, O[c][:, :, :], stored_before[c])
                            wait(AC, m)
                            for q in range(4):
                                o_out[c].add(AC.dma_start(view["o"][bass.ds(2 * b + c, 1), q].rearrange("o h u d -> (o h) u d"),
                                                          O[c][q:P:4, :, :]))
                            return m

                        before[4 * c] = lambda c=c: [qk_in[c].first(), v_in[c].first()]
                        after[c] = [end]
                    small.run(quads, None, 1.0, before, after)
                    scored = [small.scored_marks[3], small.scored_marks[7]]
                    small.note()
                with SP.Fori(0, B - 1) as i:
                    for c in range(2):
                        core.wait_at(SP, i, scored[c])
                        for d in load_qk(c, i + 1):
                            d.then_inc(qk_in[c].sem, 16)
                        core.wait_at(SP, i, summed[c])
                        load_v(c, i + 1).then_inc(v_in[c].sem, 16)
                for eng in engines:
                    wait(eng, *core.done())
                wait(SP, *core.done())
                wait(SP, *[o.now() for o in o_out])
            with ExitStack() as scope:
                rows = sbuf("O_rows", [P, B, D], scope)
                back = Counter(core, "o_loaded", 16)
                back.add(SP.dma_start(rows[:, :, :], scratch["o"].rearrange("(b p d) -> p b d", p=P, d=D)))
                wait(DV, back.now(), rows_here)
                for b in range(B):
                    dve.add(DV.tensor_tensor(x[:, b, :], x[:, b, :], rows[:, b, :], ALU.add))
                for eng in engines:
                    wait(eng, *core.done())
            finish_all()

        SLOTS, BOT, RD, VB = 128, 64, 48, 32

        def load_slots(stage, free):
            w = Weights(stage, free)
            v = {n: w.load(f"L0_ffn_{n}") for n in ("Wq", "WrT", "Wr", "aux_keysT", "aux_valuesT", "WvdT", "WvuT", "Wu1T")}
            v.update({n: w.load(f"L0_ffn_{n}", broadcast=True) for n in ("bu1", "Wu2", "bu2", "gate_w1", "gate_bias", "log_rel")})
            return v, w

        def slots(stage, v, w):
            with ExitStack() as scope:
                G = sbuf("G", [P, KC, 2 * SLOTS], scope)
                values = sbuf("slot_values", [SLOTS, D], scope)
                rkT = sbuf("rkT", [RD, SLOTS], scope)
                H = sbuf("H", [BOT, SLOTS], scope)
                avT = sbuf("avT", [VB, SLOTS], scope)
                ones_sq = sbuf("ones_sq", [P, P], scope)
                st = sbuf("slot_stats", [P, B, 6], scope)
                mv = sbuf("slot_mv", [P, B, 2], scope)
                lv = sbuf("slot_lv", [P, B], scope)
                nv = sbuf("slot_nv", [P, B], scope)
                c = sbuf("slot_small", [P, 32], scope)
                sc, at, rep, sel, E, h, p, g = (sbuf(f"slot_{n}", [P, SLOTS], scope) for n in ("sc", "at", "rep", "sel", "E", "h", "p", "g"))
                ET = sbuf("slot_ET", [SLOTS, P], scope)
                x2 = sbuf("slot_x2", [P, D], scope)
                for eng in engines:
                    wait(eng, w.here())
                m = pe.add(PE.matmul(psum[0][0:RD, 0:SLOTS], v["WrT"], v["aux_keysT"], start=True, stop=True))
                wait(DV, m)
                m = dve.add(DV.tensor_copy(rkT[:, :], psum[0][0:RD, 0:SLOTS]))
                wait(PE, m)
                m = pe.add(PE.matmul(psum[0][0:BOT, 0:SLOTS], v["Wr"], rkT[:, :], start=True, stop=True))
                wait(DV, m)
                m = dve.add(DV.tensor_copy(H[:, :], psum[0][0:BOT, 0:SLOTS]))
                wait(PE, m)
                for k in range(KC):
                    cols = slice(k * P, (k + 1) * P)
                    PE.matmul(psum[1][:, cols], v["Wq"][:, cols], H[:, :], start=True, stop=True)
                    mm = PE.matmul(psum[2][:, cols], v["Wq"][:, cols], v["aux_keysT"], start=True, stop=True)
                m = pe.add(mm)
                wait(DV, m)
                dve.add(DV.tensor_copy(G[:, :, 0:SLOTS], four(psum[1][:, :])))
                dve.add(DV.tensor_copy(G[:, :, SLOTS:], four(psum[2][:, :])))
                for k in range(KC):
                    mm = PE.matmul(psum[3][0:VB, 0:SLOTS], v["WvdT"][:, k, :], v["aux_valuesT"][:, k, :], start=k == 0, stop=k == KC - 1)
                m = pe.add(mm)
                wait(DV, m)
                m = dve.add(DV.tensor_copy(avT[:, :], psum[3][0:VB, 0:SLOTS]))
                wait(PE, m)
                m = pe.add(PE.matmul(psum[4][:, :], avT[:, :], v["WvuT"], start=True, stop=True))
                wait(DV, m)
                dve.add(DV.tensor_copy(values[:, :], psum[4][:, :]))
                s1 = pool.add(PO.memset(ones_sq[:, :], 1.0))
                for b in range(B):
                    m = dve.add(DV.bn_stats(st[:, b, :], x[:, b, :]))
                wait(DV, m)
                for b in range(B):
                    m = dve.add(DV.bn_aggr(mv[:, b, :], st[:, b, :]))
                wait(AC, m)
                m = act.add(AC.activation(lv[:, :], mv[:, :, 1], ACT.Ln, bias=ones[:, 0:1]))
                wait(DV, m)
                m = dve.add(DV.tensor_reduce(c[:, 0:1], lv[:, :], AX.X, ALU.add))
                wait(PE, m, s1)
                m = pe.add(PE.matmul(psum[5][:, 0:1], ones_sq[:, :], c[:, 0:1], start=True, stop=True))
                wait(DV, m)
                m = dve.add(DV.tensor_scalar(c[:, 1:2], psum[5][:, 0:1], 1.0 / T, 1e-6, ALU.mult, ALU.add))
                wait(DV, m)
                m = dve.add(DV.reciprocal(c[:, 2:3], c[:, 1:2]))
                wait(DV, m)
                dve.add(DV.tensor_scalar(nv[:, :], lv[:, :], c[:, 2:3], 0.5, ALU.mult, ALU.mult))
                for eng in engines:
                    wait(eng, *core.done())
                with core.repeat(B) as b:
                    start = core.done()
                    xrow = x[:, bass.ds(b, 1), :].rearrange("p o d -> p (o d)")
                    wait(AC, *start, apart=True)
                    m = act.add(AC.activation(xTb[:, :, :], wide(xT, b), ACT.Copy))
                    wait(PO, *start)
                    doubled = pool.add(PO.tensor_tensor(x2[:, :], xrow, xrow, ALU.add))
                    wait(PE, *start)
                    wait(PE, m)
                    for k in range(KC):
                        mm = PE.matmul(psum[0][:, 0:2 * SLOTS], xTb[:, k, :], G[:, k, :], start=k == 0, stop=k == KC - 1)
                    m = pe.add(mm)
                    for k in range(KC):
                        mm = PE.matmul(psum[1][:, 0:P], xTb[:, k, :], v["Wu1T"][:, k, :], start=k == 0, stop=k == KC - 1)
                    hidden = pe.add(mm)
                    wait(DV, *start)
                    wait(DV, m)
                    m = dve.add(DV.scalar_tensor_tensor(sc[:, :], psum[0][:, 0:SLOTS], float(RD) ** -0.5, v["log_rel"], ALU.mult, ALU.add))
                    dve.add(DV.scalar_tensor_tensor(at[:, :], psum[0][:, SLOTS:2 * SLOTS], float(BOT) ** -0.5, v["log_rel"], ALU.mult, ALU.add))
                    wait(DV, m, apart=True)
                    m = dve.add(DV.max(c[:, 8:16], sc[:, :]))
                    wait(DV, m, apart=True)
                    m = dve.add(DV.match_replace(rep[:, :], c[:, 8:16], sc[:, :], -3.0e38))
                    wait(DV, m)
                    m = dve.add(DV.tensor_tensor(sel[:, :], rep[:, :], sc[:, :], ALU.not_equal))
                    wait(DV, m)
                    m = dve.add(DV.tensor_scalar(sel[:, :], sel[:, :], -1.0, -NEG, ALU.add, ALU.mult))
                    wait(DV, m)
                    m = dve.add(DV.tensor_tensor(at[:, :], at[:, :], sel[:, :], ALU.add))
                    wait(DV, m)
                    m = dve.add(DV.tensor_reduce(c[:, 16:17], at[:, :], AX.X, ALU.max, negate=True))
                    wait(AC, m)
                    m = act.add(AC.activation(E[:, :], at[:, :], ACT.Exp, bias=c[:, 16:17], accum_out=c[:, 17:18]))
                    wait(PE, m)
                    m = pe.add(PE.transpose(psum[2][:, 0:P], E[:, :], ident))
                    wait(AC, m)
                    m = act.add(AC.activation(ET[:, :], psum[2][:, 0:P], ACT.Copy))
                    wait(PE, m)
                    mixed = pe.add(PE.matmul(psum[3][:, :], ET[:, :], values[:, :], start=True, stop=True))
                    wait(DV, hidden)
                    m = dve.add(DV.tensor_tensor(h[:, :], psum[1][:, 0:P], v["bu1"], ALU.add))
                    wait(DV, m)
                    m = dve.add(DV.tensor_tensor(p[:, :], h[:, :], h[:, :], ALU.mult))
                    wait(DV, m)
                    m = dve.add(DV.tensor_scalar(p[:, :], p[:, :], 0.044715, 1.0, ALU.mult, ALU.add))
                    wait(DV, m)
                    m = dve.add(DV.tensor_tensor(p[:, :], p[:, :], h[:, :], ALU.mult))
                    wait(DV, m)
                    m = dve.add(DV.tensor_scalar(p[:, :], p[:, :], -50.0, None, ALU.max))
                    wait(AC, m)
                    m = act.add(AC.activation(g[:, :], p[:, :], ACT.Exp, scale=-2.0 * float(np.sqrt(2.0 / np.pi))))
                    wait(DV, m)
                    m = dve.add(DV.tensor_scalar(g[:, :], g[:, :], 1.0, None, ALU.add))
                    wait(DV, m)
                    m = dve.add(DV.reciprocal(g[:, :], g[:, :]))
                    wait(DV, m)
                    m = dve.add(DV.tensor_tensor(g[:, :], g[:, :], h[:, :], ALU.mult))
                    wait(DV, m)
                    m = dve.add(DV.tensor_tensor(g[:, :], g[:, :], v["Wu2"], ALU.mult))
                    wait(DV, m)
                    m = dve.add(DV.tensor_reduce(c[:, 18:19], g[:, :], AX.X, ALU.add))
                    wait(DV, m)

                    def sigmoid(at, source):
                        m = act.add(AC.activation(c[:, at:at + 1], source, ACT.Exp, scale=-1.0))
                        wait(DV, m)
                        m = dve.add(DV.tensor_scalar(c[:, at:at + 1], c[:, at:at + 1], 1.0, None, ALU.add))
                        wait(DV, m)
                        m = dve.add(DV.reciprocal(c[:, at:at + 1], c[:, at:at + 1]))
                        wait(DV, m)
                        return m

                    m = dve.add(DV.tensor_scalar(c[:, 19:20], c[:, 18:19], v["bu2"][:, 0:1], -80.0, ALU.add, ALU.max))
                    wait(AC, m)
                    sigmoid(20, c[:, 19:20])
                    m = dve.add(DV.tensor_scalar(c[:, 21:22], c[:, 20:21], 2.5, None, ALU.mult))
                    wait(DV, m)
                    m = dve.add(DV.tensor_tensor(c[:, 21:22], c[:, 21:22], nv[:, bass.ds(b, 1)], ALU.add))
                    wait(DV, m)
                    m = dve.add(DV.tensor_scalar(c[:, 21:22], c[:, 21:22], 0.0, 5.0, ALU.max, ALU.min))
                    wait(DV, m)
                    m = dve.add(DV.tensor_scalar(c[:, 21:22], c[:, 21:22], -0.5, 1.0 / 1.5, ALU.add, ALU.mult))
                    wait(DV, m)
                    m = dve.add(DV.tensor_scalar(c[:, 21:22], c[:, 21:22], 0.0, 1.0, ALU.max, ALU.min))
                    wait(DV, m)
                    m = dve.add(DV.tensor_scalar(c[:, 22:23], c[:, 21:22], v["gate_w1"][:, 0:1], v["gate_bias"][:, 0:1], ALU.mult, ALU.add))
                    wait(DV, m)
                    m = dve.add(DV.tensor_scalar(c[:, 22:23], c[:, 22:23], -80.0, None, ALU.max))
                    wait(AC, m)
                    sigmoid(23, c[:, 22:23])
                    m = dve.add(DV.tensor_scalar(c[:, 24:25], c[:, 23:24], 0.05, None, ALU.is_ge))
                    r = dve.add(DV.reciprocal(c[:, 25:26], c[:, 17:18]))
                    wait(DV, r)
                    m = dve.add(DV.tensor_tensor(c[:, 26:27], c[:, 23:24], c[:, 24:25], ALU.mult))
                    wait(DV, m)
                    m = dve.add(DV.tensor_tensor(c[:, 27:28], c[:, 26:27], c[:, 25:26], ALU.mult))
                    wait(DV, m, mixed, doubled)
                    core.carry(DV)
                    dve.add(DV.scalar_tensor_tensor(xrow, psum[3][:, :], c[:, 27:28], x2[:, :], ALU.mult, ALU.add))
                for eng in engines:
                    wait(eng, *core.done())
            finish_all()

        H96, G4 = 96, 4

        def load_latent(stage, free):
            w = Weights(stage, free)
            load_context()
            qkv, o = Counter(core, "stream_qkv10", 16), Counter(core, "stream_out10", 16)
            views = {}
            for name, rows, shape in (("wq", P, (KC, 4 * H96)), ("wk", P, (KC, H96)), ("wv", P, (KC, H96)), ("wo", H96, (4, D))):
                n = shape[0] * shape[1]
                views[name] = w.arena[0:rows, w.at:w.at + n].rearrange("p (k n) -> p k n", k=shape[0])
                w.at += n
                (o if name == "wo" else qkv).add(SP.dma_start(views[name], dram[f"L3_x{name}"][0]))
            return views, w, qkv, o

        def latent(stage, views, w, qkv, o):
            wq, wk, wv, wo = (views[n] for n in ("wq", "wk", "wv", "wo"))
            with ExitStack() as scope:
                QT = sbuf("QT10", [H96, 4, T], scope)
                KT = sbuf("KT10", [H96, B, 2, P], scope)
                V = sbuf("V10", [P, 2, B, H96], scope)
                soft = Softmax(scope, "s10", width=2 * P, depth=3, masked=False)
                PT = sbuf("PT10", [P, 2, 4, P], scope)
                OT = [sbuf(f"OT{n}_10", [H96, 4, P], scope) for n in range(2)]
                for eng in engines:
                    wait(eng, ctx_here)
                with core.repeat(G4, streams={qkv: 3, o: 1}) as g:
                    wait(PE, qkv.first())
                    for eng in (DV, AC):
                        wait(eng, *core.last("scored", "mixed"))
                    soft.restart()
                    bank_free = {n: core.last(f"bank{n}_free") for n in (6, 7)}
                    free, n, jobs = [bank_free[6], bank_free[7]], 0, []
                    for s_, source in ((0, ctxT), (1, xT)):
                        for half in range(2):
                            jobs.append((KT[:, 4 * half:4 * half + 4, s_, :], source, half, wk[:, :, :]))
                    for h in range(4):
                        for half in range(2):
                            jobs.append((four(QT[:, h, half * HALF:(half + 1) * HALF]), xT, half, wq[:, :, h * H96:(h + 1) * H96]))
                    for dst, source, half, weight in jobs:
                        bank = psum[6 + n % 2]
                        wait(PE, *free[n % 2])
                        for k in range(KC):
                            mm = PE.matmul(bank[0:H96, :], weight[:, k, :], source[:, k, half * HALF:(half + 1) * HALF], start=k == 0, stop=k == KC - 1)
                        m = pe.add(mm)
                        wait(AC if n % 2 else DV, m)
                        if n % 2:
                            free[1] = [act.add(AC.activation(dst, four(bank[0:H96, :]), ACT.Copy))]
                        else:
                            free[0] = [dve.add(DV.tensor_copy(dst, four(bank[0:H96, :])))]
                        n += 1
                    for s_, source in ((0, ctxT), (1, xT)):
                        for half in range(2):
                            bank = psum[6 + n % 2]
                            wait(PE, *free[n % 2])
                            for b in range(4 * half, 4 * half + 4):
                                for k in range(KC):
                                    mm = PE.matmul(bank[:, b % 4 * H96:(b % 4 + 1) * H96], source[:, k, b * P:(b + 1) * P], wv[:, k, :], start=k == 0, stop=k == KC - 1)
                            m = projected = pe.add(mm)
                            wait(AC if n % 2 else DV, m)
                            dst = V[:, s_, 4 * half:4 * half + 4, :]
                            source4 = four(bank[:, 0:4 * H96])
                            if n % 2:
                                free[1] = [act.add(AC.activation(dst, source4, ACT.Copy))]
                            else:
                                free[0] = [dve.add(DV.tensor_copy(dst, source4))]
                            n += 1
                    bank_free = {6: free[0], 7: free[1]}
                    score_free, t_free, ot_free = ([core.last(f"{t}{n}_free") for n in range(2)] for t in ("score", "t", "ot"))
                    pt_read, done, copied = core.last("mixed"), {}, {}
                    wait(PE, *free[0], *free[1])
                    for step in range(B + 3):
                        if 2 <= step < B + 2:
                            b = step - 2
                            wait(PE, done[b])
                            E = soft.E[b % 3]
                            for s_ in range(2):
                                bank = psum[4 + s_]
                                wait(PE, *t_free[s_])
                                for h in range(4):
                                    mm = PE.transpose(bank[:, h * P:(h + 1) * P], E[:, h, s_ * P:(s_ + 1) * P], ident)
                                m = pe.add(mm)
                                soft.used[b % 3] = [m]
                                wait(DV if s_ else AC, m, *pt_read)
                                if s_:
                                    t_free[s_] = [dve.add(DV.tensor_copy(PT[:, s_, :, :], four(bank[:, :])))]
                                else:
                                    t_free[s_] = [act.add(AC.activation(PT[:, s_, :, :], four(bank[:, :]), ACT.Copy))]
                        if step < B:
                            b = step
                            banks = psum[2 * (b % 2):2 * (b % 2) + 2]
                            wait(PE, *score_free[b % 2])
                            for h in range(4):
                                mm = PE.matmul(banks[h // 2][:, h % 2 * 256:(h % 2 + 1) * 256], QT[:, h, b * P:(b + 1) * P],
                                               KT[:, b, :, :].rearrange("p s n -> p (s n)"), start=True, stop=True)
                            m = pe.add(mm)
                            core.note("scored", m)
                            tiles = [t[:, :].rearrange("p (a n) -> p a n", a=2) for t in banks]
                            done[b], freed_ = soft.run(b, m, tiles, float(H96) ** -0.5, None)
                            score_free[b % 2] = [freed_]
                        if step >= 3:
                            b = step - 3
                            if b == 0:
                                wait(PE, o.first())
                            wait(PE, copied[b], *bank_free[7])
                            for h in range(4):
                                mm = PE.matmul(psum[7][:, :], OT[b % 2][:, h, :], wo[:, h, :], start=h == 0, stop=h == 3)
                            m = last = pe.add(mm)
                            ot_free[b % 2] = [m]
                            wait(DV, m)
                            bank_free[7] = [dve.add(DV.tensor_tensor(x[:, b, :], psum[7][:, :], x[:, b, :], ALU.add))]
                        if 2 <= step < B + 2:
                            b = step - 2
                            wait(PE, *t_free[0], *t_free[1], *bank_free[6])
                            for s_ in range(2):
                                mm = PE.matmul(psum[6][0:H96, :], V[:, s_, b, :], PT[:, s_, :, :], start=s_ == 0, stop=s_ == 1)
                            m = pe.add(mm)
                            pt_read = [m]
                            core.note("mixed", m)
                            wait(DV, m, *ot_free[b % 2])
                            copied[b] = dve.add(DV.tensor_copy(OT[b % 2][:, :, :], four(psum[6][0:H96, :])))
                            bank_free[6] = [copied[b]]
                    soft.note()
                    for n in range(2):
                        for name, marks in (("score", score_free), ("t", t_free), ("ot", ot_free)):
                            core.note(f"{name}{n}_free", marks[n][0])
                        core.note(f"bank{6 + n}_free", bank_free[6 + n][0])
                with SP.Fori(0, G4 - 1) as i:
                    core.wait_at(SP, i, projected)
                    for name in ("wq", "wk", "wv"):
                        SP.dma_start(views[name], dram[f"L3_x{name}"][bass.ds(i + 1, 1)].rearrange("o p k n -> (o p) k n")).then_inc(qkv.sem, 16)
                    core.wait_at(SP, i, last)
                    SP.dma_start(wo, dram["L3_xwo"][bass.ds(i + 1, 1)].rearrange("o p k n -> (o p) k n")).then_inc(o.sem, 16)
                for eng in engines:
                    wait(eng, *core.done())
            finish_all()

        LOAD = {0: load_heads, 2: load_slots, 10: load_latent, 3: load_rotary16, 6: load_bias16, 7: load_feature, 9: load_single, 1: load_cross, 4: load_cross, 5: load_experts, 8: load_experts, 11: load_experts}
        RUN = {0: between_heads, 2: slots, 10: latent, 3: small_attention, 6: small_attention, 7: feature_attention, 9: single_head, 1: cross, 4: cross, 5: experts, 8: experts, 11: experts}
        wait_for = [x_here]
        for eng in (PE, AC, DV, PO):
            wait(eng, x_here)
        todo = list(STAGES)
        ready = LOAD[todo[0]](todo[0], [])
        rows_here = loaded_rows.add(SP.dma_start(x[:, :, :], dram["x"]))
        if todo[0] != 0:
            for eng in (PE, AC, DV, PO):
                wait(eng, rows_here)
        ended = {0: [], 1: []}
        for n, stage in enumerate(todo):
            here = ready
            if n + 1 < len(todo):
                nxt = todo[n + 1]
                ready = LOAD[nxt](nxt, ended[nxt % 2] if (nxt % 2) != (stage % 2) else [])
            RUN[stage](stage, *here)
            end = core.done()
            ended[stage % 2] = end
            for eng in (PE, AC, DV, PO):
                wait(eng, *end)
        wait(SP, *core.done())
        kept = stored.add(SP.dma_start(out, x[:, :, :]))
        wait(SP, kept)
        return core.noted


def chunks(w):
    k, n = w.shape
    return np.ascontiguousarray(w.reshape(k // P, P, n).transpose(1, 0, 2))


def rope(dim, positions):
    f = np.float32
    inv = (f(1.0) / f(10000.0) ** (np.arange(0, dim, 2, dtype=f) / f(dim))).astype(f)
    ang = np.arange(positions, dtype=f)[None, :] * inv[:, None]
    return np.cos(ang).astype(f), np.sin(ang).astype(f)


def constants():
    f = np.float32
    c = np.zeros((P, 8 * P + 32), f)
    c[:, 0:P] = np.eye(P)
    c[:, P:2 * P] = np.where(np.tril(np.ones((P, P), bool)), 0, NEG)
    c[:, 2 * P:3 * P] = np.where(np.kron(np.eye(4), np.ones((32, 32))) > 0, 0, NEG)
    cos, sin = rope(P, P)
    c[:, 3 * P:4 * P] = np.concatenate([cos, cos])
    c[:, 4 * P:5 * P] = np.concatenate([sin, -sin])
    cos, sin = rope(16, P)
    c[:, 5 * P:6 * P] = np.tile(np.concatenate([cos, cos]), (8, 1))
    c[:, 6 * P:7 * P] = np.tile(np.concatenate([-sin, sin]), (8, 1))
    partner = np.array([16 * (p // 16) + (p % 16 + 8) % 16 for p in range(P)])
    c[partner, 7 * P + np.arange(P)] = 1
    c[:, 8 * P] = (np.arange(P) // 16) % 2 == 0
    c[:, 8 * P + 1] = (np.arange(P) // 16) % 2 == 1
    c[:, 8 * P + 2:8 * P + 4] = 1
    c[:, 8 * P + 5] = EPS
    c[:, 8 * P + 6] = -0.5
    c[:, 8 * P + 16:8 * P + 24], c[:, 8 * P + 24:8 * P + 32] = EPS, -0.5
    return c


def layout(i):
    a = {"const": constants()}
    a["x"] = i["x"].transpose(1, 0, 2)
    a["xT"] = chunks(i["x"].reshape(T, D).T)
    for layer, stage in (("L1", 5), ("L2", 8), ("L3", 11)):
        f = f"{layer}_ffn_"
        a[f + "W_base"] = chunks(i[f + "W_base"].T)
        low = i[f + "A"].reshape(P, D).T
        if layer == "L1":
            parts = [low, i[f + "W_gate"].T, i[f + "W_thr"].T]
            a[f + "b_thr"] = i[f + "b_thr"]
        else:
            parts = [low, i[f + "W_router"].T]
        a[f + "route"] = chunks(np.concatenate(parts, axis=1))
        a[f + "B"] = i[f + "B"].transpose(0, 2, 1).reshape(P, D)
        a[f + "b_base"] = i[f + "b_base"]
    for layer, names, flip in (("L0", ("Wq", "Wk", "Wv", "Wd"), True), ("L1", ("wq", "wk", "wv", "wo"), False)):
        for out, name in zip(("wq", "wk", "wv"), names):
            w = i[f"{layer}_xattn_{name}"]
            w = w.T if flip else w
            a[f"{layer}_x{out}"] = w.reshape(KC, P, 8, -1).transpose(2, 1, 0, 3)
        w = i[f"{layer}_xattn_{names[3]}"]
        w = w.T if flip else w
        a[f"{layer}_xwo"] = w.reshape(8, 4, P, D).transpose(0, 2, 1, 3)
    order = np.array([(4 * j + t) * 16 + d for t in range(4) for j in range(8) for d in range(16)])
    a["L1_attn_Wq"] = chunks(i["L1_attn_Wq"][:, order])
    for n in ("Wk", "Wv"):
        a[f"L1_attn_{n}"] = chunks(i[f"L1_attn_{n}"])
    for n in ("Wq", "Wk", "Wv"):
        a[f"L2_attn_{n}"] = chunks(i[f"L2_attn_{n}"].T)
    places = [(2 * pair + par, t) for pair in range(4) for t in range(4) for par in range(2)]
    for layer, heads, w in (("L1", [4 * j + t for j, t in places], i["L1_attn_Wo"]),
                            ("L2", [8 * t + j for j, t in places], i["L2_attn_Wo"].T)):
        a[f"{layer}_attn_Wo"] = chunks(w.reshape(32, 16, D)[heads].reshape(D, D))
    a["L2_attn_bq"], a["L2_attn_bk"] = (i[f"L2_attn_{n}"].reshape(4, P).T for n in ("bq", "bk"))
    a["L2_attn_bv"], a["L2_attn_bo"] = i["L2_attn_bv"], i["L2_attn_bo"]
    a["L3_attn_Wqkv"], a["L3_attn_Wo"] = chunks(i["L3_attn_Wqkv"]), i["L3_attn_Wo"]
    a["L3_attn_bqk"] = i["L3_attn_bqkv"][0:2 * P].reshape(2, P).T
    a["L3_attn_bv"], a["L3_attn_bo"] = i["L3_attn_bqkv"][2 * P:], i["L3_attn_bo"]
    for n in "qkv":
        a[f"L0_attn_w{n}"] = chunks(i[f"L0_attn_w{n}"].T)
    a["L0_attn_bq"], a["L0_attn_bk"] = (i[f"L0_attn_{n}"].reshape(4, P).T for n in ("bq", "bk"))
    a["L0_attn_bv"] = i["L0_attn_bv"]
    same = (np.arange(64)[None, None, :] // 16 == np.arange(4)[:, None, None]) & np.ones((4, 32, 64), bool)
    a["mask_rows"] = np.stack([same, np.where(same, 0, NEG)]).astype(np.float32)
    f = "L0_ffn_"
    a[f + "Wq"], a[f + "Wr"], a[f + "WrT"] = i[f + "Wq"], i[f + "Wr"], i[f + "Wr"].T
    a[f + "aux_keysT"], a[f + "aux_valuesT"] = i[f + "aux_keys"].T, chunks(i[f + "aux_values"].T)
    a[f + "WvdT"], a[f + "WvuT"], a[f + "Wu1T"] = chunks(i[f + "Wvd"].T), i[f + "Wvu"].T, chunks(i[f + "Wu1"].T)
    for n in ("bu1", "Wu2", "bu2", "gate_w1", "gate_bias", "log_rel"):
        a[f + n] = i[f + n].reshape(-1)
    for n in ("q", "k", "v"):
        a[f"L3_xw{n}"] = i[f"L3_xattn_W{n}"].T.reshape(KC, P, 4, -1).transpose(2, 1, 0, 3)
    a["L3_xwo"] = i["L3_xattn_Wo"].T.reshape(4, 4, 96, D).transpose(0, 2, 1, 3)
    a["ctx"] = i["ctx_4096"].transpose(1, 0, 2)
    a["ctxT"] = chunks(i["ctx_4096"].reshape(T, D).T)
    a["mask"] = i["mask_BxSxS2_ff0"].transpose(1, 0, 2)
    return {k: np.ascontiguousarray(v) for k, v in a.items()}


def kernel(**inputs):
    import concourse.bacc as bacc
    from concourse.bass_utils import run_bass_kernel_spmd

    arrays = layout({k: np.asarray(v) for k, v in inputs.items()})
    known = {}
    for _ in range(2):
        nc = bacc.Bacc("TRN2", target_bir_lowering=False, num_devices=1)
        dram = {k: nc.dram_tensor(f"in_{k}", v.shape, mybir.dt.from_np(v.dtype), kind="ExternalInput").ap() for k, v in arrays.items()}
        out = nc.dram_tensor("out_x", (P, B, D), F32, kind="ExternalOutput").ap()
        known = build(nc, dram, out, known)
    result = run_bass_kernel_spmd(nc, [{f"in_{k}": v for k, v in arrays.items()}], core_ids=[0])
    return result.results[0]["out_x"].transpose(1, 0, 2)
```
